# Optimizing a Trainium2 kernel written in Bass

```python
import numpy as np
import jax
import jax.numpy as jnp

def _softmax(x, axis=-1):
    return jax.nn.softmax(x, axis=axis)

def _gelu(x):
    return jax.nn.gelu(x, approximate=True)

def _silu(x):
    return jax.nn.silu(x)

def _sigmoid(x):
    return jax.nn.sigmoid(x)

def _layernorm(x, axis=-1, eps=1e-05):
    m = jnp.mean(x, axis=axis, keepdims=True)
    v = jnp.var(x, axis=axis, keepdims=True)
    return (x - m) / jnp.sqrt(v + eps)

def _scatter_add(tgt, idx, src, axis=0):
    return tgt.at[idx].add(src)

def _segment_sum(src, seg, n):
    return jax.ops.segment_sum(src, seg, n)
kernel_name = 'mk_decoder_preln_d2_seqx_r4_43e170'

def setup_inputs(seed: int=0):
    np.random.seed(seed)
    _w = jnp.asarray

    def _rec_inputs():
        import jax
        import jax.numpy as jnp
        _rk = jax.random.key(seed)
        x = -0.0002928 + 1 * jax.random.normal(jax.random.fold_in(_rk, 1), (16, 112, 256), jnp.float32)
        _lenS = 112 - jax.random.randint(jax.random.fold_in(_rk, 7), (16,), 0, max(1, 112 // 4) + 1, jnp.int32)
        _lenS2 = 375 - jax.random.randint(jax.random.fold_in(_rk, 8), (16,), 0, max(1, 375 // 4) + 1, jnp.int32)
        _ctx_1024P = jax.random.normal(jax.random.fold_in(_rk, 11), (16, 16, 256), jnp.float32)
        _ctx_1024c = jax.random.dirichlet(jax.random.fold_in(_rk, 511), 0.3 * jnp.ones((16,), jnp.float32), (16, 375))
        _ctx_1024t = jnp.einsum('bsk,bkd->bsd', _ctx_1024c, _ctx_1024P)
        _ctx_1024t = _ctx_1024t * jax.lax.rsqrt(jnp.mean(jnp.square(_ctx_1024t)) + 1e-12) * 0.953939
        ctx_1024 = -1.39393e-06 + 0.999914 * (_ctx_1024t + 0.3 * jax.random.normal(jax.random.fold_in(_rk, 611), (16, 375, 256), jnp.float32))
        _validS = jnp.arange(112)[None, :] < _lenS[:, None]
        _validS2 = jnp.arange(375)[None, :] < _lenS2[:, None]
        _causal = jnp.tril(jnp.ones((112, 112), dtype=bool))
        mask_Bx1x1xS2_ik0 = jnp.where(jnp.broadcast_to(_validS2[:, None, None, :], (16, 1, 1, 375)), 0, 1).astype(jnp.int32)
        return (x, ctx_1024, mask_Bx1x1xS2_ik0)
    x, ctx_1024, mask_Bx1x1xS2_ik0 = _rec_inputs()

    def _L0_attn_setup():
        import jax, jax.numpy as jnp
        import numpy as np
        B, S, HID = (4, 1024, 256)
        H, D = (16, 64)
        EPS = 1e-06

        def _phi(x):
            return jax.nn.elu(x) + 1.0
        key = jax.random.key(seed)
        ks = jax.random.split(key, 9)
        sc = 1.0 / np.sqrt(HID)
        return {'x': jax.random.normal(ks[0], (B, S, HID), jnp.float32), 'Wq': jax.random.normal(ks[1], (HID, H * D), jnp.float32) * sc, 'bq': jnp.zeros((H * D,), jnp.float32), 'Wk': jax.random.normal(ks[2], (HID, H * D), jnp.float32) * sc, 'bk': jnp.zeros((H * D,), jnp.float32), 'Wv': jax.random.normal(ks[3], (HID, H * D), jnp.float32) * sc, 'bv': jnp.zeros((H * D,), jnp.float32), 'Wo': jax.random.normal(ks[4], (H * D, HID), jnp.float32) * sc, 'bo': jnp.zeros((HID,), jnp.float32)}
    _L0_attn_all = _L0_attn_setup()
    _L0_attn_in = {k: v for k, v in _L0_attn_all.items() if k in ('Wq', 'bq', 'Wk', 'bk', 'Wv', 'bv', 'Wo', 'bo')}
    del _L0_attn_all

    def _L0_xattn_setup():
        import jax, jax.numpy as jnp
        import numpy as np
        EMB = 256
        HEADS = 16
        HEAD_DIM = EMB // HEADS
        key = jax.random.key(seed)
        k1, k2, k3, k4, k5 = jax.random.split(key, 5)
        N, S = (2, 512)
        query = jax.random.normal(k1, (N, S, EMB), dtype=jnp.float32)
        key_t = jax.random.normal(k2, (N, S, EMB), dtype=jnp.float32)
        values = jax.random.normal(k3, (N, S, EMB), dtype=jnp.float32)
        mask = jax.random.randint(k4, (N, 1, 1, S), 0, 2, dtype=jnp.int32)
        W_out = jax.random.normal(k5, (EMB, EMB), dtype=jnp.float32) * (1.0 / np.sqrt(EMB))
        return {'query': query, 'key': key_t, 'values': values, 'mask': mask, 'W_out': W_out}
    _L0_xattn_all = _L0_xattn_setup()
    _L0_xattn_in = {k: v for k, v in _L0_xattn_all.items() if k in ('W_out',)}
    del _L0_xattn_all

    def _L0_ffn_setup():
        import jax, jax.numpy as jnp
        import numpy as np
        DIM = 256
        HEADS = 16
        HD = DIM // HEADS
        M = 64
        E = 4
        K = 2
        HID = 512
        MID = 512
        LB = 0.01
        EPS = 1.1920929e-07

        def _rms(x, w):
            return x * jax.lax.rsqrt(jnp.mean(x * x, axis=-1, keepdims=True) + EPS) * w

        def _gelu(x):
            return jax.nn.gelu(x, approximate=False)
        key = jax.random.key(seed)
        ks = jax.random.split(key, 20)
        d = DIM
        w = lambda k, s: jax.random.normal(k, s, jnp.float32) * 0.02
        return {'x': jax.random.normal(ks[0], (4, 256, d), jnp.float32), 'n1_w': jnp.ones((d,), jnp.float32), 'n2_w': jnp.ones((d,), jnp.float32), 'wq': w(ks[1], (d, d)), 'wk': w(ks[2], (d, d)), 'wv': w(ks[3], (d, d)), 'wo': w(ks[4], (d, d)), 'qn_w': jnp.ones((HD,), jnp.float32), 'kn_w': jnp.ones((HD,), jnp.float32), 'gate_w': w(ks[5], (E, d)), 'e0_up': w(ks[6], (HID, d)), 'e0_down': w(ks[7], (d, HID)), 'e1_w1': w(ks[8], (HID, d)), 'e1_w2': w(ks[9], (HID, d)), 'e1_down': w(ks[10], (d, HID)), 'e2_l1': w(ks[11], (MID, d)), 'e2_l2': w(ks[12], (HID, MID)), 'e2_l3': w(ks[13], (MID, HID)), 'e2_l4': w(ks[14], (d, MID)), 'e3_down': w(ks[15], (d, d)), 'e3_up': w(ks[16], (HID, d)), 'e3_out': w(ks[17], (d, HID))}
    _L0_ffn_all = _L0_ffn_setup()
    _L0_ffn_in = {k: v for k, v in _L0_ffn_all.items() if k in ('n1_w', 'n2_w', 'wq', 'wk', 'wv', 'wo', 'qn_w', 'kn_w', 'gate_w', 'e0_up', 'e0_down', 'e1_w1', 'e1_w2', 'e1_down', 'e2_l1', 'e2_l2', 'e2_l3', 'e2_l4', 'e3_down', 'e3_up', 'e3_out')}
    del _L0_ffn_all

    def _L1_attn_setup():
        import math
        import jax, jax.numpy as jnp
        import numpy as np
        D_MODEL = 256
        N_HEADS = 16
        D_K = D_MODEL // N_HEADS
        D_C = 64
        B, S = (2, 512)
        key = jax.random.key(seed)
        ks = jax.random.split(key, 7)
        sd = lambda fan_in: 1.0 / math.sqrt(fan_in)
        return {'x': jax.random.normal(ks[0], (B, S, D_MODEL), dtype=jnp.float32), 'W_dq': jax.random.uniform(ks[1], (D_MODEL, D_C), minval=-sd(D_MODEL), maxval=sd(D_MODEL), dtype=jnp.float32), 'W_uq': jax.random.uniform(ks[2], (D_C, N_HEADS * D_K), minval=-sd(D_C), maxval=sd(D_C), dtype=jnp.float32), 'W_dkv': jax.random.uniform(ks[3], (D_MODEL, D_C), minval=-sd(D_MODEL), maxval=sd(D_MODEL), dtype=jnp.float32), 'W_uk': jax.random.uniform(ks[4], (D_C, N_HEADS * D_K), minval=-sd(D_C), maxval=sd(D_C), dtype=jnp.float32), 'W_uv': jax.random.uniform(ks[5], (D_C, N_HEADS * D_K), minval=-sd(D_C), maxval=sd(D_C), dtype=jnp.float32), 'W_o': jax.random.uniform(ks[6], (N_HEADS * D_K, D_MODEL), minval=-sd(N_HEADS * D_K), maxval=sd(N_HEADS * D_K), dtype=jnp.float32)}
    _L1_attn_all = _L1_attn_setup()
    _L1_attn_in = {k: v for k, v in _L1_attn_all.items() if k in ('W_dq', 'W_uq', 'W_dkv', 'W_uk', 'W_uv', 'W_o')}
    del _L1_attn_all

    def _L1_xattn_setup():
        import jax, jax.numpy as jnp
        import numpy as np
        EMBED_DIM = 256
        NUM_HEADS = 16
        HEAD_DIM = EMBED_DIM // NUM_HEADS
        WINDOW = 64

        def apply_rope(x):
            B, H, S, d = x.shape
            half = d // 2
            pos = jnp.arange(S, dtype=x.dtype)
            freqs = 1.0 / 10000.0 ** (jnp.arange(half, dtype=x.dtype) / half)
            ang = pos[:, None] * freqs[None, :]
            cos, sin = (jnp.cos(ang), jnp.sin(ang))
            x1, x2 = (x[..., :half], x[..., half:])
            return jnp.concatenate([x1 * cos - x2 * sin, x1 * sin + x2 * cos], axis=-1)

        def _forward(query, key, value, q_w, q_b, k_w, k_b, v_w, v_b, o_w, o_b):
            B, S_q, D = query.shape
            S_k = key.shape[1]
            H, d, W = (NUM_HEADS, HEAD_DIM, WINDOW)
            q = (query @ q_w.T + q_b).reshape(B, S_q, H, d).transpose(0, 2, 1, 3)
            k = (key @ k_w.T + k_b).reshape(B, S_k, H, d).transpose(0, 2, 1, 3)
            v = (value @ v_w.T + v_b).reshape(B, S_k, H, d).transpose(0, 2, 1, 3)
            q = apply_rope(q) * d ** (-0.5)
            k = apply_rope(k)
            q_pos = jnp.arange(S_q)[:, None]
            offsets = jnp.arange(-W, 1)[None, :]
            idx = q_pos + offsets
            local_mask = (idx < 0) | (idx >= S_k)
            gidx = jnp.clip(idx, 0, S_k - 1)
            k_win = k[:, :, gidx, :]
            v_win = v[:, :, gidx, :]
            scores = jnp.einsum('bhqd,bhqwd->bhqw', q, k_win)
            mask = local_mask[None, None, :, :]
            scores = jnp.where(mask, -jnp.inf, scores)
            m = jnp.max(scores, axis=-1, keepdims=True)
            m = jnp.where(jnp.isfinite(m), m, 0.0)
            e = jnp.exp(scores - m)
            denom = jnp.sum(e, axis=-1, keepdims=True)
            probs = jnp.where(denom > 0, e / jnp.where(denom > 0, denom, 1.0), 0.0)
            ctx = jnp.einsum('bhqw,bhqwd->bhqd', probs, v_win)
            ctx = ctx.transpose(0, 2, 1, 3).reshape(B, S_q, D)
            return ctx @ o_w.T + o_b
        key = jax.random.key(seed)
        ks = jax.random.split(key, 12)
        B, S, D = (1, 512, EMBED_DIM)
        scale = 1.0 / np.sqrt(D)
        inp = {'query': jax.random.normal(ks[0], (B, S, D), jnp.float32), 'key': jax.random.normal(ks[1], (B, S, D), jnp.float32), 'value': jax.random.normal(ks[2], (B, S, D), jnp.float32), 'q_w': jax.random.normal(ks[3], (D, D), jnp.float32) * scale, 'q_b': jax.random.normal(ks[4], (D,), jnp.float32) * 0.01, 'k_w': jax.random.normal(ks[5], (D, D), jnp.float32) * scale, 'k_b': jax.random.normal(ks[6], (D,), jnp.float32) * 0.01, 'v_w': jax.random.normal(ks[7], (D, D), jnp.float32) * scale, 'v_b': jax.random.normal(ks[8], (D,), jnp.float32) * 0.01, 'o_w': jax.random.normal(ks[9], (D, D), jnp.float32) * scale, 'o_b': jax.random.normal(ks[10], (D,), jnp.float32) * 0.01}
        return inp
    _L1_xattn_all = _L1_xattn_setup()
    _L1_xattn_in = {k: v for k, v in _L1_xattn_all.items() if k in ('q_w', 'q_b', 'k_w', 'k_b', 'v_w', 'v_b', 'o_w', 'o_b')}
    del _L1_xattn_all

    def _L1_ffn_setup():
        import jax, jax.numpy as jnp
        import numpy as np
        IN_F = 256
        OUT_F = 256
        B, S = (8, 1024)

        def _pack_ternary(tern):
            enc = (tern + 1.0).astype(jnp.int32).reshape(-1)
            return (enc[0::4] | enc[1::4] << 2 | enc[2::4] << 4 | enc[3::4] << 6).astype(jnp.int32)
        key = jax.random.key(seed)
        kx, kw = jax.random.split(key)
        x = jax.random.normal(kx, (B, S, IN_F), dtype=jnp.float32)
        w = jax.random.normal(kw, (OUT_F, IN_F), dtype=jnp.float32) * 0.02
        scale = jnp.maximum(jnp.mean(jnp.abs(w)), 1e-05)
        wn = w / scale
        tern = jnp.sign(wn) * (jnp.abs(wn) > 0.5).astype(jnp.float32)
        packed = _pack_ternary(tern)
        bias = jnp.zeros((OUT_F,), dtype=jnp.float32)
        return {'x': x, 'packed_weight': packed, 'weight_scale': scale.reshape(1), 'bias': bias}
    _L1_ffn_all = _L1_ffn_setup()
    _L1_ffn_in = {k: v for k, v in _L1_ffn_all.items() if k in ('packed_weight', 'weight_scale', 'bias')}
    del _L1_ffn_all
    return {'x': x, 'ctx_1024': ctx_1024, 'mask_Bx1x1xS2_ik0': mask_Bx1x1xS2_ik0, 'L0_attn_Wq': _L0_attn_in['Wq'], 'L0_attn_bq': _L0_attn_in['bq'], 'L0_attn_Wk': _L0_attn_in['Wk'], 'L0_attn_bk': _L0_attn_in['bk'], 'L0_attn_Wv': _L0_attn_in['Wv'], 'L0_attn_bv': _L0_attn_in['bv'], 'L0_attn_Wo': _L0_attn_in['Wo'], 'L0_attn_bo': _L0_attn_in['bo'], 'L0_xattn_W_out': _L0_xattn_in['W_out'], 'L0_ffn_n1_w': _L0_ffn_in['n1_w'], 'L0_ffn_n2_w': _L0_ffn_in['n2_w'], 'L0_ffn_wq': _L0_ffn_in['wq'], 'L0_ffn_wk': _L0_ffn_in['wk'], 'L0_ffn_wv': _L0_ffn_in['wv'], 'L0_ffn_wo': _L0_ffn_in['wo'], 'L0_ffn_qn_w': _L0_ffn_in['qn_w'], 'L0_ffn_kn_w': _L0_ffn_in['kn_w'], 'L0_ffn_gate_w': _L0_ffn_in['gate_w'], 'L0_ffn_e0_up': _L0_ffn_in['e0_up'], 'L0_ffn_e0_down': _L0_ffn_in['e0_down'], 'L0_ffn_e1_w1': _L0_ffn_in['e1_w1'], 'L0_ffn_e1_w2': _L0_ffn_in['e1_w2'], 'L0_ffn_e1_down': _L0_ffn_in['e1_down'], 'L0_ffn_e2_l1': _L0_ffn_in['e2_l1'], 'L0_ffn_e2_l2': _L0_ffn_in['e2_l2'], 'L0_ffn_e2_l3': _L0_ffn_in['e2_l3'], 'L0_ffn_e2_l4': _L0_ffn_in['e2_l4'], 'L0_ffn_e3_down': _L0_ffn_in['e3_down'], 'L0_ffn_e3_up': _L0_ffn_in['e3_up'], 'L0_ffn_e3_out': _L0_ffn_in['e3_out'], 'L1_attn_W_dq': _L1_attn_in['W_dq'], 'L1_attn_W_uq': _L1_attn_in['W_uq'], 'L1_attn_W_dkv': _L1_attn_in['W_dkv'], 'L1_attn_W_uk': _L1_attn_in['W_uk'], 'L1_attn_W_uv': _L1_attn_in['W_uv'], 'L1_attn_W_o': _L1_attn_in['W_o'], 'L1_xattn_q_w': _L1_xattn_in['q_w'], 'L1_xattn_q_b': _L1_xattn_in['q_b'], 'L1_xattn_k_w': _L1_xattn_in['k_w'], 'L1_xattn_k_b': _L1_xattn_in['k_b'], 'L1_xattn_v_w': _L1_xattn_in['v_w'], 'L1_xattn_v_b': _L1_xattn_in['v_b'], 'L1_xattn_o_w': _L1_xattn_in['o_w'], 'L1_xattn_o_b': _L1_xattn_in['o_b'], 'L1_ffn_packed_weight': _L1_ffn_in['packed_weight'], 'L1_ffn_weight_scale': _L1_ffn_in['weight_scale'], 'L1_ffn_bias': _L1_ffn_in['bias']}

def reference(x, ctx_1024, mask_Bx1x1xS2_ik0, L0_attn_Wq, L0_attn_bq, L0_attn_Wk, L0_attn_bk, L0_attn_Wv, L0_attn_bv, L0_attn_Wo, L0_attn_bo, L0_xattn_W_out, L0_ffn_n1_w, L0_ffn_n2_w, L0_ffn_wq, L0_ffn_wk, L0_ffn_wv, L0_ffn_wo, L0_ffn_qn_w, L0_ffn_kn_w, L0_ffn_gate_w, L0_ffn_e0_up, L0_ffn_e0_down, L0_ffn_e1_w1, L0_ffn_e1_w2, L0_ffn_e1_down, L0_ffn_e2_l1, L0_ffn_e2_l2, L0_ffn_e2_l3, L0_ffn_e2_l4, L0_ffn_e3_down, L0_ffn_e3_up, L0_ffn_e3_out, L1_attn_W_dq, L1_attn_W_uq, L1_attn_W_dkv, L1_attn_W_uk, L1_attn_W_uv, L1_attn_W_o, L1_xattn_q_w, L1_xattn_q_b, L1_xattn_k_w, L1_xattn_k_b, L1_xattn_v_w, L1_xattn_v_b, L1_xattn_o_w, L1_xattn_o_b, L1_ffn_packed_weight, L1_ffn_weight_scale, L1_ffn_bias):
    import jax
    import jax.numpy as jnp

    def _L0_attn_ref(x, Wq, bq, Wk, bk, Wv, bv, Wo, bo):
        import jax, jax.numpy as jnp
        import numpy as np
        B, S, HID = (4, 1024, 256)
        H, D = (16, 64)
        EPS = 1e-06

        def _phi(x):
            return jax.nn.elu(x) + 1.0
        bs, n, _ = x.shape
        Q = _phi((x @ Wq + bq).reshape(bs, n, H, D)).transpose(1, 0, 2, 3)
        K = _phi((x @ Wk + bk).reshape(bs, n, H, D)).transpose(1, 0, 2, 3)
        V = (x @ Wv + bv).reshape(bs, n, H, D).transpose(1, 0, 2, 3)
        KV0 = jnp.zeros((bs, H, D, D), x.dtype)
        Ks0 = jnp.zeros((bs, H, D), x.dtype)

        def step(carry, qkv):
            KV, Ks = carry
            qi, ki, vi = qkv
            KV = KV + jnp.einsum('bhd,bhe->bhde', ki, vi)
            Ks = Ks + ki
            num = jnp.einsum('bhd,bhde->bhe', qi, KV)
            den = jnp.einsum('bhd,bhd->bh', qi, Ks)
            return ((KV, Ks), num / (den[..., None] + EPS))
        _, out = jax.lax.scan(step, (KV0, Ks0), (Q, K, V))
        out = out.transpose(1, 0, 2, 3).reshape(bs, n, H * D)
        return out @ Wo + bo

    def _L0_xattn_ref(query, key, values, mask, W_out):
        import jax, jax.numpy as jnp
        import numpy as np
        EMB = 256
        HEADS = 16
        HEAD_DIM = EMB // HEADS
        N, Q, _ = query.shape
        K = key.shape[1]
        q = query.reshape(N, Q, HEADS, HEAD_DIM)
        k = key.reshape(N, K, HEADS, HEAD_DIM)
        v = values.reshape(N, K, HEADS, HEAD_DIM)
        energy = jnp.einsum('nqhd,nkhd->nhqk', q, k)
        energy = jnp.where(mask == 0, jnp.float32(-1e+20), energy)
        attn = jax.nn.softmax(energy / jnp.sqrt(jnp.float32(EMB)), axis=-1)
        out = jnp.einsum('nhqk,nkhd->nqhd', attn, v).reshape(N, Q, EMB)
        return out @ W_out.T

    def _L0_ffn_ref(x, n1_w, n2_w, wq, wk, wv, wo, qn_w, kn_w, gate_w, e0_up, e0_down, e1_w1, e1_w2, e1_down, e2_l1, e2_l2, e2_l3, e2_l4, e3_down, e3_up, e3_out):
        import jax, jax.numpy as jnp
        import numpy as np
        DIM = 256
        HEADS = 16
        HD = DIM // HEADS
        M = 64
        E = 4
        K = 2
        HID = 512
        MID = 512
        LB = 0.01
        EPS = 1.1920929e-07

        def _rms(x, w):
            return x * jax.lax.rsqrt(jnp.mean(x * x, axis=-1, keepdims=True) + EPS) * w

        def _gelu(x):
            return jax.nn.gelu(x, approximate=False)
        B, T, C = x.shape
        h = _rms(x, n1_w)
        heads = lambda w_: (h @ w_.T).reshape(B, T, HEADS, HD).transpose(0, 2, 1, 3)
        q = _rms(heads(wq), qn_w)
        k = _rms(heads(wk), kn_w)
        v = heads(wv)
        scores = jnp.einsum('bhqd,bhkd->bhqk', q, k) * HD ** (-0.5)
        causal = jnp.tril(jnp.ones((T, T), bool))
        scores = jnp.where(causal[None, None], scores, -jnp.inf)
        attn = jax.nn.softmax(scores, axis=-1)
        ao = jnp.einsum('bhqk,bhkd->bhqd', attn, v).transpose(0, 2, 1, 3).reshape(B, T, C) @ wo.T
        ao = ao.at[:, :, :M].set(0.0)
        x = x + ao
        xf = _rms(x, n2_w).reshape(-1, C)
        N = xf.shape[0]
        logits = jnp.nan_to_num(xf @ gate_w.T)
        probs = jax.nn.softmax(logits, axis=-1)
        topv, topi = jax.lax.top_k(probs, K)
        topv = topv / (topv.sum(-1, keepdims=True) + 1e-08)
        wts = jnp.zeros((N, E), x.dtype).at[jnp.arange(N)[:, None], topi].add(topv)
        o0 = _gelu(xf @ e0_up.T) @ e0_down.T
        o1 = jax.nn.silu(xf @ e1_w1.T) * (xf @ e1_w2.T) @ e1_down.T
        o2 = _gelu(_gelu(_gelu(xf @ e2_l1.T) @ e2_l2.T) @ e2_l3.T) @ e2_l4.T
        o3 = _gelu(_gelu(xf @ e3_down.T) @ e3_up.T) @ e3_out.T
        moe = wts[:, 0:1] * o0 + wts[:, 1:2] * o1 + wts[:, 2:3] * o2 + wts[:, 3:4] * o3
        moe = moe.reshape(B, T, C).at[:, :, :M].set(0.0)
        return x + moe

    def _L1_attn_ref(x, W_dq, W_uq, W_dkv, W_uk, W_uv, W_o):
        import math
        import jax, jax.numpy as jnp
        import numpy as np
        D_MODEL = 256
        N_HEADS = 16
        D_K = D_MODEL // N_HEADS
        D_C = 64
        B, S = (2, 512)
        Bx, Sx, _ = x.shape
        c_q = x @ W_dq
        Q = (c_q @ W_uq).reshape(Bx, Sx, N_HEADS, D_K)
        c_kv = x @ W_dkv
        K = (c_kv @ W_uk).reshape(Bx, Sx, N_HEADS, D_K)
        V = (c_kv @ W_uv).reshape(Bx, Sx, N_HEADS, D_K)
        scores = jnp.einsum('bqhd,bkhd->bhqk', Q, K) / math.sqrt(D_K)
        causal = jnp.tril(jnp.ones((Sx, Sx), dtype=bool))
        scores = jnp.where(causal, scores, -jnp.inf)
        attn = jax.nn.softmax(scores, axis=-1)
        out = jnp.einsum('bhqk,bkhd->bqhd', attn, V).reshape(Bx, Sx, N_HEADS * D_K)
        return out @ W_o

    def _L1_xattn_ref(query, key, value, q_w, q_b, k_w, k_b, v_w, v_b, o_w, o_b):
        import jax, jax.numpy as jnp
        import numpy as np
        EMBED_DIM = 256
        NUM_HEADS = 16
        HEAD_DIM = EMBED_DIM // NUM_HEADS
        WINDOW = 64

        def apply_rope(x):
            B, H, S, d = x.shape
            half = d // 2
            pos = jnp.arange(S, dtype=x.dtype)
            freqs = 1.0 / 10000.0 ** (jnp.arange(half, dtype=x.dtype) / half)
            ang = pos[:, None] * freqs[None, :]
            cos, sin = (jnp.cos(ang), jnp.sin(ang))
            x1, x2 = (x[..., :half], x[..., half:])
            return jnp.concatenate([x1 * cos - x2 * sin, x1 * sin + x2 * cos], axis=-1)

        def _forward(query, key, value, q_w, q_b, k_w, k_b, v_w, v_b, o_w, o_b):
            B, S_q, D = query.shape
            S_k = key.shape[1]
            H, d, W = (NUM_HEADS, HEAD_DIM, WINDOW)
            q = (query @ q_w.T + q_b).reshape(B, S_q, H, d).transpose(0, 2, 1, 3)
            k = (key @ k_w.T + k_b).reshape(B, S_k, H, d).transpose(0, 2, 1, 3)
            v = (value @ v_w.T + v_b).reshape(B, S_k, H, d).transpose(0, 2, 1, 3)
            q = apply_rope(q) * d ** (-0.5)
            k = apply_rope(k)
            q_pos = jnp.arange(S_q)[:, None]
            offsets = jnp.arange(-W, 1)[None, :]
            idx = q_pos + offsets
            local_mask = (idx < 0) | (idx >= S_k)
            gidx = jnp.clip(idx, 0, S_k - 1)
            k_win = k[:, :, gidx, :]
            v_win = v[:, :, gidx, :]
            scores = jnp.einsum('bhqd,bhqwd->bhqw', q, k_win)
            mask = local_mask[None, None, :, :]
            scores = jnp.where(mask, -jnp.inf, scores)
            m = jnp.max(scores, axis=-1, keepdims=True)
            m = jnp.where(jnp.isfinite(m), m, 0.0)
            e = jnp.exp(scores - m)
            denom = jnp.sum(e, axis=-1, keepdims=True)
            probs = jnp.where(denom > 0, e / jnp.where(denom > 0, denom, 1.0), 0.0)
            ctx = jnp.einsum('bhqw,bhqwd->bhqd', probs, v_win)
            ctx = ctx.transpose(0, 2, 1, 3).reshape(B, S_q, D)
            return ctx @ o_w.T + o_b
        return _forward(query, key, value, q_w, q_b, k_w, k_b, v_w, v_b, o_w, o_b)

    def _L1_ffn_ref(x, packed_weight, weight_scale, bias):
        import jax, jax.numpy as jnp
        import numpy as np
        IN_F = 256
        OUT_F = 256
        B, S = (8, 1024)

        def _pack_ternary(tern):
            enc = (tern + 1.0).astype(jnp.int32).reshape(-1)
            return (enc[0::4] | enc[1::4] << 2 | enc[2::4] << 4 | enc[3::4] << 6).astype(jnp.int32)
        n = OUT_F * IN_F
        shifts = jnp.array([0, 2, 4, 6], dtype=jnp.int32)
        enc = (packed_weight[None, :] >> shifts[:, None] & 3).reshape(-1)[:n]
        w = (enc.astype(jnp.float32) - 1.0).reshape(OUT_F, IN_F) * weight_scale
        act_scale = 127.0 / jnp.maximum(jnp.max(jnp.abs(x), axis=-1, keepdims=True), 1e-05)
        x_dq = jnp.clip(jnp.round(x * act_scale), -128.0, 127.0) / act_scale
        return jnp.einsum('bsi,oi->bso', x_dq, w) + bias
    x = x + _L0_attn_ref(_layernorm(x, axis=-1), L0_attn_Wq, L0_attn_bq, L0_attn_Wk, L0_attn_bk, L0_attn_Wv, L0_attn_bv, L0_attn_Wo, L0_attn_bo)
    x = x + _L0_xattn_ref(_layernorm(x, axis=-1), ctx_1024, ctx_1024, mask_Bx1x1xS2_ik0, L0_xattn_W_out)
    x = x + _L0_ffn_ref(_layernorm(x, axis=-1), L0_ffn_n1_w, L0_ffn_n2_w, L0_ffn_wq, L0_ffn_wk, L0_ffn_wv, L0_ffn_wo, L0_ffn_qn_w, L0_ffn_kn_w, L0_ffn_gate_w, L0_ffn_e0_up, L0_ffn_e0_down, L0_ffn_e1_w1, L0_ffn_e1_w2, L0_ffn_e1_down, L0_ffn_e2_l1, L0_ffn_e2_l2, L0_ffn_e2_l3, L0_ffn_e2_l4, L0_ffn_e3_down, L0_ffn_e3_up, L0_ffn_e3_out)
    x = x + _L1_attn_ref(_layernorm(x, axis=-1), L1_attn_W_dq, L1_attn_W_uq, L1_attn_W_dkv, L1_attn_W_uk, L1_attn_W_uv, L1_attn_W_o)
    x = x + _L1_xattn_ref(_layernorm(x, axis=-1), ctx_1024, ctx_1024, L1_xattn_q_w, L1_xattn_q_b, L1_xattn_k_w, L1_xattn_k_b, L1_xattn_v_w, L1_xattn_v_b, L1_xattn_o_w, L1_xattn_o_b)
    x = x + _L1_ffn_ref(_layernorm(x, axis=-1), L1_ffn_packed_weight, L1_ffn_weight_scale, L1_ffn_bias)
    return x

_drawn_inputs = setup_inputs


def setup_inputs(seed=0):
    import zlib

    import numpy as np

    out = dict(_drawn_inputs(seed))
    spreads = {'L0_attn_bq': (0.0, 0.8),
     'L0_attn_bk': (0.0, 0.8),
     'L0_attn_bv': (0.0, 0.1),
     'L0_attn_bo': (0.0, 0.1),
     'L0_ffn_n1_w': (1.0, 0.6),
     'L0_ffn_n2_w': (1.0, 0.6),
     'L0_ffn_qn_w': (1.0, 0.6),
     'L0_ffn_kn_w': (1.0, 0.6),
     'L1_ffn_bias': (0.0, 2.0)}
    factors = {'L0_attn_Wq': 3.381,
     'L0_ffn_wq': 8.0,
     'L0_ffn_wk': 8.0,
     'L0_ffn_gate_w': 6.79,
     'L0_ffn_e0_up': 5.135,
     'L0_ffn_e0_down': 5.038,
     'L0_ffn_e1_w1': 8.0,
     'L0_ffn_e1_w2': 8.0,
     'L0_ffn_e1_down': 8.0,
     'L0_ffn_e2_l1': 8.0,
     'L0_ffn_e2_l2': 8.0,
     'L0_ffn_e2_l3': 8.0,
     'L0_ffn_e2_l4': 8.0,
     'L0_ffn_e3_down': 8.0,
     'L0_ffn_e3_up': 8.0,
     'L0_ffn_e3_out': 8.0,
     'L1_attn_W_dq': 55.572,
     'L1_attn_W_uq': 55.253,
     'L1_attn_W_uk': 55.228,
     'L1_xattn_q_b': 200.0,
     'L1_xattn_k_b': 200.0,
     'L1_xattn_v_b': 200.0,
     'L1_xattn_o_b': 200.0,
     'L1_attn_W_dkv': 6.368,
     'L1_attn_W_uv': 6.223,
     'L1_attn_W_o': 6.178,
     'L1_xattn_q_w': 17.371,
     'L1_xattn_k_w': 16.907,
     'L1_xattn_v_w': 2.703}
    for name, (base, spread) in spreads.items():
        noise = np.random.default_rng([zlib.crc32(name.encode()), seed]).standard_normal(out[name].shape)
        drawn = base * np.exp(spread * noise) if base else spread * noise
        out[name] = jnp.asarray(drawn.astype(out[name].dtype))
    for name, factor in factors.items():
        out[name] = (out[name] * factor).astype(out[name].dtype)
    return out
```

```python
from contextlib import ExitStack

import numpy as np
import concourse.bass as bass
from concourse import mybir

F32 = mybir.dt.float32
BF16 = mybir.dt.bfloat16
I32 = mybir.dt.int32
ALU = mybir.AluOpType
ACT = mybir.ActivationFunctionType
AX_X = mybir.AxisListType.X

P = 128
B, S, D = 16, 112, 256
H, HD = 16, 16
SC = 375
KC, NKC = 125, 3
LD = 64
LW = H * LD
KT = D // P
HID = 512
FT = HID // P
FREE = 64
DO = D - FREE
WINDOW = 64
QUAD = 4
QN = QUAD * S
BIG = 1e30
AREA = 13500
B_OWN = 8848
RMS_EPS = 1.1920929e-07
FLT_MAX = 3.4028234663852886e38
ROUND = 1.5 * 2.0 ** 23
UPS = 30

C_ID = 0
C_TRI = C_ID + P
C_CAUSAL = C_TRI + S
C_BAND = C_CAUSAL + S
C_BM = C_BAND + S
C_BM4 = C_BM + 8
C_COS = C_BM4 + 4
C_SIN = C_COS + HD
C_LT = C_SIN + HD
C_END = C_LT + 16


def constants():
    c = np.zeros((P, C_END), np.float32)
    c[:, C_ID:C_ID + P] = np.eye(P, dtype=np.float32)
    r = np.arange(S)
    c[:S, C_TRI:C_TRI + S] = r[:, None] <= r[None, :]
    c[:S, C_CAUSAL:C_CAUSAL + S] = np.where(r[None, :] <= r[:, None], 0, -BIG)
    c[:S, C_BAND:C_BAND + S] = np.where((r[None, :] <= r[:, None]) & (r[None, :] >= r[:, None] - WINDOW), 0, -BIG)
    p = np.arange(P)
    c[:, C_BM:C_BM + 8] = p[:, None] // HD == np.arange(8)[None, :]
    c[:, C_BM4:C_BM4 + 4] = p[:, None] // 32 == np.arange(4)[None, :]
    half = HD // 2
    freqs = (1.0 / 10000.0 ** (np.arange(half, dtype=np.float32) / half)).astype(np.float32)
    ang = r.astype(np.float32)[:, None] * freqs[None, :]
    c[:S, C_COS:C_COS + HD] = np.tile(np.cos(ang), (1, 2))
    c[:S, C_SIN:C_SIN + HD] = np.concatenate([-np.sin(ang), np.sin(ang)], 1)
    e = np.arange(4)
    c[:, C_LT:C_LT + 16] = (e[None, :] < e[:, None]).reshape(1, 16)
    return c


def on(b):
    return not isinstance(b, int) or 0 <= b < B


class Counter:

    def __init__(self, sem, base):
        self.sem, self.base = sem, base

    def at(self, value):
        return value + self.base if not isinstance(value, int) else max(value, 0) and value + self.base


def least(a, b):
    return min(a, b) if isinstance(a, int) else a


def batches(eng, body, ahead, behind=1):
    n = 6 if ahead == 1 else 5
    for b in range(-ahead, 3):
        body(b, b % 2, b // 2)
    with eng.Fori(1, n + 1) as i:
        body(2 * i + 1, 1, i)
        body(2 * i + 2, 0, i + 1)
    for b in range(2 * n + 3, B + behind):
        body(b, b % 2, b // 2)


def decoder_kernel(nc, T, out):
    ctx = ExitStack()
    with ctx:
        def sb(name, shape, dt=F32):
            return ctx.enter_context(nc.sbuf_tensor(name, shape, dt))

        def sems(prefix, names):
            return {n: Counter(ctx.enter_context(nc.semaphore(f"{prefix}_{n}")), 0) for n in names.split()}

        banks = ctx.enter_context(nc.psum_tensor("banks", [P, 8, 512], F32))
        pb = [banks[:, i, :] for i in range(8)]

        cst = sb("cst", [P, C_END])
        ident = cst[:, C_ID:C_ID + P]
        X = sb("X", [S, B * D])
        Y_room = sb("Y_room", [P, B * D])
        Y = Y_room[0:S, :]
        kcol = sb("kcol", [S, 5, 32])
        stats = sb("stats", [S, 6])
        mv = sb("mv", [S, 2])
        rstd = sb("rstd", [S, 8])
        minus_one = sb("minus_one", [P, 1])

        def xb_(b, lo=0, hi=D):
            return X[:, bass.ds(b * D + lo, hi - lo)]

        def yb_(b, lo=0, hi=D):
            return Y[:, bass.ds(b * D + lo, hi - lo)]

        room = sb("room", [P, 4 * 2048 + 1024 + D])
        wq0, wk0, wv0 = (room[:, i * 2048:(i + 1) * 2048].rearrange("p (k n) -> p k n", k=KT) for i in range(3))
        wo0 = room[:, 3 * 2048:4 * 2048].rearrange("p (k n) -> p k n", k=LW // P)
        bv0 = room[0:S, 8192:8192 + LW]
        bo0 = room[0:S, 8192 + LW:8192 + LW + D]
        bqk0 = sb("bqk0", [P, 16])
        wx0 = sb("wx0", [P, KT, D])
        wqk1, wv1, wo1 = sb("wqk1", [P, KT, 2 * D]), sb("wv1", [P, KT, D]), sb("wo1", [P, KT, DO])
        n12 = sb("n12", [P, 4])
        qkn = sb("qkn", [P, 2])
        gate = sb("gate", [P, KT, 4])
        up0, dn0 = sb("up0", [P, KT, HID]), sb("dn0", [P, FT, DO])
        g1, u1, dn1 = sb("g1", [P, KT, HID]), sb("u1", [P, KT, HID]), sb("dn1", [P, FT, DO])
        l1, l2, l3, dn2 = sb("l1", [P, KT, HID]), sb("l2", [P, FT, HID]), sb("l3", [P, FT, HID]), sb("dn2", [P, FT, DO])
        d3, up3, dn3 = sb("d3", [P, KT, D]), sb("up3", [P, KT, HID]), sb("dn3", [P, FT, DO])
        wdd = sb("wdd", [P, KT, P])
        wuqk, wuv = sb("wuqk", [P, 2, D]), sb("wuv", [P, D])
        wo4, wq5, wk5, wv5, wo5 = (Y_room[:, i * 512:(i + 1) * 512].rearrange("p (k n) -> p k n", k=KT) for i in range(5))
        b5 = Y_room[0:S, 2560:3584].rearrange("p (i n) -> p i n", i=4)
        packed = sb("packed", [P, KT, 64], I32)
        enc = sb("enc", [P, KT, 64], I32)
        tern = sb("tern", [P, KT, D], BF16)
        wscale = sb("wscale", [S, 1])
        b6 = sb("b6", [S, D])
        mask_i = sb("mask_i", [B, SC], I32)
        mask_f = sb("mask_f", [B, SC])

        area = sb("area", [P, AREA])
        top = [0]

        def take(parts, n, pattern=None, **dims):
            a = area[0:parts, top[0]:top[0] + n]
            top[0] += n
            assert top[0] <= AREA
            return a.rearrange(pattern, **dims) if pattern else a

        mask_scratch = nc.dram_tensor("mask_scratch", (B, SC), F32, kind="Internal").ap()

        ld = sems("ld", "x cst bias a0 a1 a2 a3 bo wx mask c1 c2 gate e0 e1 e2 e3 d4 e5 b5 f6 pk")
        pre = sems("pre", "bias1 pad zero scale m1 av rowbias scratch tern enc kn bx cv")

        A = sems("A", "mv pc xn xb xt xte pg pj ex ph sg sm nd chain den nm ot oe wd xu")
        Bs = sems("B", "bd sg mx nb ex tp ted tea pv den nm ot oe cp0 cp1 cv0 cv1")
        for n in "mv xn xt chain wd xu".split():
            Bs[n] = Counter(A[n].sem, B)
        Bs["pc"] = Counter(A["pc"].sem, 2 * B)
        core1 = "mv xn xt xte v ve t7 qe kb pv chain den nm ot oe wd xu"
        core4 = "sg mk mxd nb ex tp"
        Cs = sems("C", "y pc qk sq ss rc r qkn ted tea " + core1 + " " + core4)
        Ds = sems("D", "pc c ce")
        Es = sems("E", "xb z rope k0 k1")
        for s, n in ((Ds, 1), (Es, 2)):
            for names, per in ((core1, 1), (core4, 4), ("ted tea", 2)):
                for name in names.split():
                    s[name] = Counter(Cs[name].sem, n * per * B)
        for name in ("qk", "qkn"):
            Es[name] = Counter(Cs[name].sem, B)
        Es["pc"] = Counter(Ds["pc"].sem, 2 * B)
        G = sems("G", "sq pc xf xt xte lg le cp xy chain wt")
        M = sems("M", "up ev h1 t dn acc")
        Fs = sems("F", "am qz mm st")
        for n in "mv xn xt chain xu".split():
            Fs[n] = Counter(A[n].sem, 2 * B)
        for n in ("xb", "xte"):
            Fs[n] = Counter(A[n].sem, B)
        Fs["pc"] = Counter(A["pc"].sem, 4 * B)

        block = ctx.enter_context(nc.Block())

        def ln_stats(s, b, unused):
            nc.vector.wait_ge(s["xn"].sem, s["xn"].at(b))
            nc.vector.bn_stats(stats[:, :], xb_(b)).then_inc(s["chain"].sem, 1)

        def ln_rstd(s, b, n_pc):
            nc.gpsimd.wait_ge(s["mv"].sem, s["mv"].at(b + 1))
            nc.gpsimd.tensor_tensor(rstd[:, 0:1], mv[:, 1:2], kcol[:, 1, 0:1], ALU.add).then_inc(s["pc"].sem, 1)
            nc.gpsimd.wait_ge(s["pc"].sem, s["pc"].at(b * n_pc + 1))
            nc.gpsimd.tensor_tensor(rstd[:, 1:2], rstd[:, 0:1], kcol[:, 0, 0:1], ALU.pow).then_inc(s["pc"].sem, 1)

        def ln_apply(s, b, dst, n_pc, src_free):
            nc.vector.wait_ge(s["pc"].sem, s["pc"].at(b * n_pc + 2))
            if src_free is not None:
                nc.vector.wait_ge(src_free[0].sem, src_free[0].at(src_free[1]))
            return nc.vector.tensor_scalar(dst, xb_(b), mv[:, 0:1], rstd[:, 1:2], ALU.subtract, ALU.mult)

        def transposes(src, parts, n, dst):
            for k in range(n):
                last = nc.tensor.transpose(dst[:, k * parts:(k + 1) * parts], src[:, k * P:(k + 1) * P],
                                           ident[0:parts, 0:parts])
            return last

        def products(dst, lhs, rhs):
            for k, (a, w) in enumerate(zip(lhs, rhs)):
                last = nc.tensor.matmul(dst, a, w, start=(k == 0), stop=(k == len(lhs) - 1))
            return last

        top[0] = 0
        a_xn = take(S, D)
        a_xnT = take(P, KT * S, "p (k s) -> p k s", k=KT)
        a_q, a_k = take(P, 8 * S), take(P, 8 * S)
        a_z, a_e = take(P, 2 * 4 * S, "p (g n) -> p g n", g=2), take(P, 2 * 4 * S, "p (g n) -> p g n", g=2)
        a_v = take(S, H * (LD + 1), "p (h e) -> p h e", h=H)
        a_at = take(S, H * S)
        a_o = take(S, LW)
        a_oT = take(P, 8 * S)
        a_den = take(S, 32)
        assert top[0] <= B_OWN
        NUM = [(0, 6), (6, 12), (12, 16)]

        top[0] = 0
        b_xn = take(S, 4 * P, "p (h r) -> p h r", r=32)
        b_bd = [take(P, H * S) for _ in range(2)]
        b_p = take(S, 2 * 2 * SC, "p (g h s) -> p g h s", g=2, h=2)
        b_pT = take(KC, 4 * NKC * S, "p (g n) -> p g n", g=4)
        b_mx, b_nb = take(S, H), take(S, H)
        b_rc = take(S, H)
        b_o = take(S, D)
        b_oT = take(P, KT * S)
        assert top[0] <= B_OWN
        top[0] = B_OWN
        b_cp = [take(P, 4 * SC, "p (t s) -> p t s", t=4) for _ in range(2)]
        b_cv = [take(KC, NKC * H * 17, "p (c h e) -> p c h e", c=NKC, h=H) for _ in range(2)]

        top[0] = 0
        c_h = take(S, D)
        c_xnT = take(P, KT * S, "p (k s) -> p k s", k=KT)
        c_sq = take(S, 2 * D)
        c_t2, c_z = take(S, 2 * D), take(S, 2 * D)
        c_qk = take(S, 2 * D)
        c_ss, c_r = take(S, 32), take(S, 32)
        c_qT = take(P, KT * S, "p (k s) -> p k s", k=KT)
        c_kbd = take(P, KT * 8 * S, "p (k j s) -> p k j s", k=KT, j=8)
        c_v = [take(S, H * 17, "p (h e) -> p h e", h=H) for _ in range(2)]
        c_ms, c_p, c_pT = (take(S, H * S) for _ in range(3))
        c_mx, c_nb, c_rc = take(S, H), take(S, H), take(S, H)
        c_o = take(S, D)
        c_oT = take(P, KT * S, "p (k s) -> p k s", k=KT)
        c_cT = take(P, S)
        knbm = take(P, 8)
        e_ctx = [c_h_ for c_h_ in (room[:, i * KT * S:(i + 1) * KT * S].rearrange("p (k s) -> p k s", k=KT) for i in range(2))]

        top[0] = 0
        m_xfT = take(P, KT * B * S, "p (k n) -> p k n", k=KT)
        g_sq = take(S, D)
        g_xf = take(S, D)
        g_ms = take(S, 8)
        g_cols = take(P, KT * S, "p (k s) -> p k s", k=KT)
        g_lg = take(S, B * 4)
        g_a, g_b2, g_w = take(S, B * 4), take(S, B * 4), take(S, B * 4)
        g_red, g_red2 = take(S, B), take(S, B)
        g_cmp, g_cmp2 = take(S, B * 16), take(S, B * 16)
        m_g, m_s, m_u, m_t = (take(P, 2 * QN, "p (g n) -> p g n", g=2) for _ in range(4))
        m_h0, m_h1, m_ha, m_hb = (room[:, i * FT * QN:(i + 1) * FT * QN].rearrange("p (k n) -> p k n", k=FT) for i in range(4))
        m_hc = room[:, 4 * FT * QN:4 * FT * QN + KT * QN].rearrange("p (k n) -> p k n", k=KT)
        m_hd = take(P, FT * QN, "p (k n) -> p k n", k=FT)

        top[0] = 0
        f_xn = take(S, D)
        f_am, f_sc = take(S, 4), take(S, 4)
        f_q = take(S, D)
        f_xT = area[:, top[0]:top[0] + S].bitcast(BF16).rearrange("p (k s) -> p k s", k=KT)

        def wload(eng, dst, name, sem):
            src = T[name].rearrange("(k p) n -> p k n", p=P)
            eng.dma_start(dst, src).then_inc(sem.sem, 16)

        def bcast(eng, dst, name, sem, parts=S):
            eng.dma_start(dst, T[name].partition_broadcast(parts)).then_inc(sem.sem, 16)

        @block.sync
        def _(sp):
            sp.dma_start(cst[:, :], T["consts"]).then_inc(ld["cst"].sem, 16)
            sp.dma_start(X[:, :].rearrange("s (b d) -> s b d", b=B), T["x"].rearrange("b s d -> s b d")).then_inc(ld["x"].sem, 16)
            sp.dma_start(bqk0[:, 0:8], T["bq"]).then_inc(ld["bias"].sem, 16)
            sp.dma_start(bqk0[:, 8:16], T["bk"]).then_inc(ld["bias"].sem, 16)
            wload(sp, wq0, "Wq", ld["a0"])
            wload(sp, wk0, "Wk", ld["a1"])
            bcast(sp, bv0, "bv", ld["a2"])
            wload(sp, wv0, "Wv", ld["a2"])
            wload(sp, wo0, "Wo", ld["a3"])
            bcast(sp, bo0, "bo", ld["bo"])
            sp.dma_start(mask_i[:, :], T["mask"]).then_inc(ld["mask"].sem, 16)
            wload(sp, wx0[:, :, :], "W_out", ld["wx"])
            sp.wait_ge(pre["rowbias"].sem, 1)
            sp.dma_start(mask_scratch, mask_f[:, :]).then_inc(pre["scratch"].sem, 16)
            wload(sp, wqk1[:, :, 0:D], "wq", ld["c1"])
            wload(sp, wqk1[:, :, D:2 * D], "wk", ld["c1"])
            wload(sp, wv1[:, :, :], "wv", ld["c1"])
            wload(sp, wo1[:, :, :], "wo", ld["c1"])
            sp.dma_start(n12[:, :], T["n12"]).then_inc(ld["c2"].sem, 16)
            for i, n in enumerate(("qn", "kn")):
                for r in range(8):
                    sp.dma_start(qkn[HD * r:HD * r + HD, i:i + 1], T[n]).then_inc(ld["c2"].sem, 16)
            wload(sp, gate[:, :, :], "gate", ld["gate"])
            sp.wait_ge(pre["scratch"].sem, 16)

            def ctx_loads(b, u, half):
                if not on(b):
                    return
                cp, cv = Bs[f"cp{u}"], Bs[f"cv{u}"]
                sp.wait_ge(pre["pad"].sem, 1)
                sp.wait_ge(Bs["sg"].sem, Bs["sg"].at(8 * (b - 1)))
                for j in range(4):
                    src = T["ctxT"][bass.ds(b, 1)].rearrange("o (t j r) s -> (o j) r t s", j=4, r=HD)[j]
                    sp.dma_start(b_cp[u][32 * j + 1:32 * j + 1 + HD, :, :], src).then_inc(cp.sem, 16)
                    row = mask_scratch[bass.ds(b, 1)]
                    for t in range(4):
                        sp.dma_start(b_cp[u][32 * j:32 * j + 1, t, :], row).then_inc(cp.sem, 16)
                sp.wait_ge(Bs["pv"].sem, Bs["pv"].at(16 * (b - 1)))
                for c in range(NKC):
                    src = T["ctx"][bass.ds(b, 1), c * KC:(c + 1) * KC].rearrange("o p (h e) -> (o p) h e", h=H)
                    sp.dma_start(b_cv[u][:, c, :, 0:HD], src).then_inc(cv.sem, 16)

            batches(sp, ctx_loads, 1)
            for name, dst, sem in (("e0_up", up0, "e0"), ("e0_down", dn0, "e0"), ("l1", l1, "e2"),
                                   ("w1", g1, "e1"), ("w2", u1, "e1"), ("l2", l2, "e2"), ("e1_down", dn1, "e1"),
                                   ("e3_down", d3, "e3"), ("l3", l3, "e2"), ("e3_up", up3, "e3"),
                                   ("l4", dn2, "e2"), ("e3_out", dn3, "e3")):
                wload(sp, dst[:, :, :], name, ld[sem])
            sp.wait_ge(pre["pad"].sem, 2)
            wload(sp, wdd[:, :, 0:64], "W_dq", ld["d4"])
            wload(sp, wdd[:, :, 64:128], "W_dkv", ld["d4"])
            sp.dma_start(wuqk[0:64, 0, :], T["W_uq"]).then_inc(ld["d4"].sem, 16)
            sp.dma_start(wuqk[64:128, 1, :], T["W_uk"]).then_inc(ld["d4"].sem, 16)
            sp.dma_start(wuv[64:128, :], T["W_uv"]).then_inc(ld["d4"].sem, 16)
            sp.wait_ge(G["xy"].sem, G["xy"].at(B))
            wload(sp, wo4, "W_o", ld["d4"])
            for name, dst in (("q_w", wq5), ("k_w", wk5), ("v_w", wv5), ("o_w", wo5)):
                wload(sp, dst, name, ld["e5"])
            for i, name in enumerate(("q_b", "k_b", "v_b", "o_b")):
                bcast(sp, b5[:, i, :], name, ld["b5"])
            sp.dma_start(packed[:, :, :], T["packed"].rearrange("(k p) o -> p k o", p=P)).then_inc(ld["pk"].sem, 16)
            bcast(sp, wscale[:, :], "wscale", ld["f6"])
            bcast(sp, b6[:, :], "bias", ld["f6"])

            def window_loads(b, u, half):
                if not on(b):
                    return
                sp.wait_ge(M["acc"].sem, M["acc"].at(64))
                sp.wait_ge(Es["v"].sem, Es["v"].at(b - 1))
                src = T["ctxT"][bass.ds(b, 1), :, 0:S].rearrange("o (k p) s -> (o p) k s", p=P)
                sp.dma_start(e_ctx[u], src).then_inc(Es[f"k{u}"].sem, 16)

            batches(sp, window_loads, 1)

            def stores(b, u, half):
                if not on(b):
                    return
                sp.wait_ge(Fs["xu"].sem, Fs["xu"].at(b + 1))
                sp.dma_start(out[bass.ds(b, 1)].rearrange("o s d -> (o s) d"), xb_(b)).then_inc(Fs["st"].sem, 16)

            batches(sp, stores, 1)
            sp.wait_ge(Fs["st"].sem, Fs["st"].at(16 * B))

        @block.tensor
        def _(pe):
            T3 = nc.tensor

            def phase_a(b, u, half):
                if on(b):
                    pe.wait_ge(A["xte"].sem, A["xte"].at(b + 1))
                    for g in range(4):
                        pe.wait_ge(A["pj"].sem, A["pj"].at(6 * b + g - 1))
                        if isinstance(b, int) and b == 0:
                            pe.wait_ge(ld["a0" if g < 2 else "a1"].sem, 16)
                        w = wq0 if g < 2 else wk0
                        for t in range(4):
                            m = 4 * (g % 2) + t
                            last = products(pb[g % 2][:, t * S:(t + 1) * S],
                                            [w[:, k, m * P:(m + 1) * P] for k in range(KT)],
                                            [a_xnT[:, k, :] for k in range(KT)])
                        last.then_inc(A["pg"].sem, 1)
                    for g in range(2):
                        pe.wait_ge(A["pj"].sem, A["pj"].at(6 * b + 3 + g))
                        if isinstance(b, int) and b == 0:
                            pe.wait_ge(ld["a2"].sem, 32)
                        products(pb[g][0:S, :], [a_xnT[:, k, :] for k in range(KT)],
                                 [wv0[:, k, g * 512:(g + 1) * 512] for k in range(KT)]).then_inc(A["pg"].sem, 1)
                if on(b - 1):
                    pe.wait_ge(A["nm"].sem, A["nm"].at(3 * b))
                    for g in range(2):
                        transposes(a_o[:, g * 512:(g + 1) * 512], S, 4, pb[2 + g]).then_inc(A["ot"].sem, 1)
                if on(b):
                    for x in range(2):
                        pe.wait_ge(A["ph"].sem, A["ph"].at(4 * b + 3 + x))
                        pe.wait_ge(A["oe"].sem, A["oe"].at(2 * b))
                        pe.wait_ge(A["sm"].sem, A["sm"].at(4 * b + 2 * x))
                        for j in range(4):
                            m = 4 * x + j
                            for e in range(2):
                                r = LD * e
                                last = T3.matmul(pb[2 + e][0:S, j * S:(j + 1) * S], a_k[r:r + LD, m * S:(m + 1) * S],
                                                 a_q[r:r + LD, m * S:(m + 1) * S], start=True, stop=True)
                                if j == 3:
                                    last.then_inc(A["sg"].sem, 1)
                if on(b - 1):
                    pe.wait_ge(A["oe"].sem, A["oe"].at(2 * b))
                    pe.wait_ge(A["xte"].sem, A["xte"].at(least(b + 1, B)))
                    if isinstance(b, int) and b == 1:
                        pe.wait_ge(ld["a3"].sem, 16)
                    products(pb[7][0:S, 0:D], [a_oT[:, m * S:(m + 1) * S] for m in range(8)],
                             [wo0[:, m, :] for m in range(8)]).then_inc(A["wd"].sem, 1)
                if on(b + 1):
                    pe.wait_ge(A["xn"].sem, A["xn"].at(b + 2))
                    pe.wait_ge(A["xu"].sem, A["xu"].at(b))
                    transposes(a_xn, S, KT, pb[7]).then_inc(A["xt"].sem, 1)
                if on(b):
                    pe.wait_ge(A["nm"].sem, A["nm"].at(3 * b))
                    pe.wait_ge(A["pj"].sem, A["pj"].at(6 * b + 6))
                    for h in range(H):
                        if h % 8 == 0:
                            pe.wait_ge(A["sm"].sem, A["sm"].at(4 * b + h // 4 + 2))
                        n = h // 6
                        o = (h - NUM[n][0]) * (LD + 1)
                        last = T3.matmul(pb[4 + n][0:S, o:o + LD + 1], a_at[:, h * S:(h + 1) * S], a_v[:, h, :],
                                         start=True, stop=True)
                        if h + 1 == NUM[n][1]:
                            last.then_inc(A["nd"].sem, 1)

            pe.wait_ge(ld["cst"].sem, 16)
            batches(pe, phase_a, 1)

            def phase_b(b, u, half):
                for p in range(8):
                    if on(b):
                        if p == 0:
                            pe.wait_ge(Bs["bd"].sem, Bs["bd"].at(b + 1))
                            pe.wait_ge(Bs[f"cp{u}"].sem, Bs[f"cp{u}"].at(16 * 20 * (half + 1)))
                        pe.wait_ge(Bs["ex"].sem, Bs["ex"].at(16 * b + 2 * p - 2))
                        for e in range(2):
                            h = 2 * p + e
                            last = T3.matmul(pb[2 * (p % 2) + e][0:S, 0:SC], b_bd[u][:, h * S:(h + 1) * S],
                                             b_cp[u][:, h // 4, :], start=True, stop=True)
                        last.then_inc(Bs["sg"].sem, 1)
                    bt, pt = (b, p - 1) if p else (b - 1, 7)
                    if on(bt):
                        for e in range(2):
                            h = 2 * pt + e
                            pe.wait_ge(Bs["ex"].sem, Bs["ex"].at(16 * bt + h + 1))
                            pe.wait_ge(Bs["tea" if e else "ted"].sem, Bs["tea" if e else "ted"].at(8 * bt + pt))
                            for c in range(NKC):
                                last = T3.transpose(pb[4 + e][0:KC, c * S:(c + 1) * S],
                                                    b_p[:, pt % 2, e, c * KC:(c + 1) * KC], ident[0:S, 0:S])
                            last.then_inc(Bs["tp"].sem, 1)
                    bv, pv = (b, p - 2) if p > 1 else (b - 1, 6 + p)
                    if on(bv):
                        if pv == 0:
                            pe.wait_ge(Bs["nm"].sem, Bs["nm"].at(bv))
                            pe.wait_ge(Bs[f"cv{u}"].sem, Bs[f"cv{u}"].at(16 * 3 * (half + 1)))
                        uv = u if p > 1 else 1 - u
                        for e in range(2):
                            h = 2 * pv + e
                            pe.wait_ge(Bs["tea" if e else "ted"].sem, Bs["tea" if e else "ted"].at(8 * bv + pv + 1))
                            for c in range(NKC):
                                last = T3.matmul(pb[6][0:S, h * 17:(h + 1) * 17], b_pT[:, h % 4, c * S:(c + 1) * S],
                                                 b_cv[uv][:, c, h, :], start=(c == 0), stop=(c == NKC - 1))
                            last.then_inc(Bs["pv"].sem, 1)
                    if p == 2 and on(b - 1):
                        pe.wait_ge(Bs["nm"].sem, Bs["nm"].at(b))
                        pe.wait_ge(Bs["bd"].sem, Bs["bd"].at(least(b + 1, B)))
                        transposes(b_o, S, KT, pb[7]).then_inc(Bs["ot"].sem, 1)
                    if p == 3 and on(b - 1):
                        pe.wait_ge(Bs["oe"].sem, Bs["oe"].at(b))
                        if isinstance(b, int) and b == 1:
                            pe.wait_ge(ld["wx"].sem, 16)
                        products(pb[7][0:S, 0:D], [b_oT[:, k * S:(k + 1) * S] for k in range(KT)],
                                 [wx0[:, k, :] for k in range(KT)]).then_inc(Bs["wd"].sem, 1)
                    if p == 4 and on(b + 1):
                        pe.wait_ge(Bs["xn"].sem, Bs["xn"].at(b + 2))
                        pe.wait_ge(Bs["xu"].sem, Bs["xu"].at(b))
                        transposes(b_xn.rearrange("p h r -> p (h r)"), S, 4, pb[7]).then_inc(Bs["xt"].sem, 1)

            pe.wait_ge(A["xu"].sem, A["xu"].at(B))
            batches(pe, phase_b, 1)

            def attention(s, project_qk, project_v, qk_read, to_columns, w_out, dst_out):
                def body(b, u, half):
                    if on(b + 1):
                        project_qk(b + 1, u, half)
                    if on(b - 2):
                        pe.wait_ge(s["oe"].sem, s["oe"].at(b - 1))
                        pe.wait_ge(s["ve"].sem, s["ve"].at(least(b + 1, B)))
                        products(pb[1][0:S, dst_out], [c_oT[:, m, :] for m in range(KT)],
                                 [w_out[:, m, :] for m in range(KT)]).then_inc(s["wd"].sem, 1)
                    for g in range(5):
                        if g < 4 and on(b):
                            pe.wait_ge(s["kb"].sem, s["kb"].at(b + 1))
                            pe.wait_ge(s["mk"].sem, s["mk"].at(4 * b + g - 1))
                            k, j = g // 2, 4 * (g % 2)
                            T3.matmul(pb[2 + g % 2][0:S, 0:4 * S], c_qT[:, k, :],
                                      c_kbd[:, k, j:j + 4, :].rearrange("p j s -> p (j s)"),
                                      start=True, stop=True).then_inc(s["sg"].sem, 1)
                        if g < 4 and on(b - 1):
                            pe.wait_ge(s["ex"].sem, s["ex"].at(4 * b + g - 3))
                            if g % 2:
                                pe.wait_ge(s["tea"].sem, s["tea"].at(2 * b - 2 + g // 2))
                            else:
                                pe.wait_ge(s["ted"].sem, s["ted"].at(2 * b - 2 + g // 2))
                            for j in range(4):
                                h = 4 * g + j
                                last = T3.transpose(pb[4 + g % 2][0:S, j * S:(j + 1) * S],
                                                    c_p[:, h * S:(h + 1) * S], ident[0:S, 0:S])
                            last.then_inc(s["tp"].sem, 1)
                        if g > 0 and on(b - 1):
                            v = g - 1
                            if v == 0:
                                pe.wait_ge(s["oe"].sem, s["oe"].at(b - 1))
                            if v % 2:
                                pe.wait_ge(s["tea"].sem, s["tea"].at(2 * b - 1 + v // 2))
                            else:
                                pe.wait_ge(s["ted"].sem, s["ted"].at(2 * b - 1 + v // 2))
                            for j in range(4):
                                h = 4 * v + j
                                last = T3.matmul(pb[6][0:S, h * 17:(h + 1) * 17], c_pT[:, h * S:(h + 1) * S],
                                                 c_v[1 - u][:, h, :], start=True, stop=True)
                            if v == 3:
                                last.then_inc(s["pv"].sem, 1)
                    if on(b + 1):
                        project_v(b + 1, u, half)
                    if on(b + 2):
                        pe.wait_ge(s["xn"].sem, s["xn"].at(b + 3))
                        pe.wait_ge(qk_read.sem, qk_read.at(b + 2))
                        transposes(c_h, S, KT, pb[0]).then_inc(s["xt"].sem, 1)
                    if on(b + 1):
                        to_columns(b + 1)
                    if on(b - 1):
                        pe.wait_ge(s["nm"].sem, s["nm"].at(b))
                        transposes(c_o, S, KT, pb[6]).then_inc(s["ot"].sem, 1)
                batches(pe, body, 2, 2)

            def c_qk_(b, u, half):
                pe.wait_ge(Cs["xte"].sem, Cs["xte"].at(b + 1))
                products(pb[0][0:S, :], [c_xnT[:, k, :] for k in range(KT)],
                         [wqk1[:, k, :] for k in range(KT)]).then_inc(Cs["qk"].sem, 1)

            def c_v_(b, u, half):
                pe.wait_ge(Cs["ve"].sem, Cs["ve"].at(b))
                pe.wait_ge(Cs["xu"].sem, Cs["xu"].at(b - 2))
                products(pb[1][0:S, 0:D], [c_xnT[:, k, :] for k in range(KT)],
                         [wv1[:, k, :] for k in range(KT)]).then_inc(Cs["v"].sem, 1)

            def columns_of(s):
                def f(b):
                    pe.wait_ge(s["qkn"].sem, s["qkn"].at(b + 1))
                    pe.wait_ge(s["kb"].sem, s["kb"].at(b))
                    transposes(c_qk, S, 4, pb[7]).then_inc(s["t7"].sem, 1)
                return f

            pe.wait_ge(Bs["xu"].sem, Bs["xu"].at(B))
            pe.wait_ge(ld["c1"].sem, 64)
            attention(Cs, c_qk_, c_v_, Cs["qkn"], columns_of(Cs), wo1, slice(0, DO))

            def phase_g(b, u, half):
                if on(b):
                    pe.wait_ge(G["xf"].sem, G["xf"].at(b + 1))
                    pe.wait_ge(G["xte"].sem, G["xte"].at(b))
                    transposes(g_xf, S, KT, pb[0]).then_inc(G["xt"].sem, 1)
                    pe.wait_ge(G["xte"].sem, G["xte"].at(b + 1))
                    pe.wait_ge(G["le"].sem, G["le"].at(b))
                    for k in range(KT):
                        last = T3.matmul(pb[1][0:S, 0:4], g_cols[:, k, :], gate[:, k, :], start=(k == 0), stop=(k == KT - 1))
                    last.then_inc(G["lg"].sem, 1)

            pe.wait_ge(Cs["xu"].sem, Cs["xu"].at(B))
            pe.wait_ge(ld["gate"].sem, 16)
            batches(pe, phase_g, 1)

            def phase_m(i, first):
                use = [0]

                def up(w, m, src, kn, ready):
                    n = use[0]
                    use[0] += 1
                    for sem, v in ready:
                        pe.wait_ge(sem.sem, sem.at(v))
                    if not first or n >= 4:
                        pe.wait_ge(M["ev"].sem, M["ev"].at(UPS * i + (n - 3 if n >= 4 else (-1, 0, -3, -2)[n])))
                    products(pb[n % 4][:, 0:QN], [w[:, k, m * P:(m + 1) * P] for k in range(kn)],
                             [src(k) for k in range(kn)]).then_inc(M["up"].sem, 1)

                def xf(k):
                    return m_xfT[:, k, bass.ds(i * QN, QN)]

                def down(w, hsrc, e, ready):
                    for sem, v in ready:
                        pe.wait_ge(sem.sem, sem.at(v))
                    for j in range(QUAD):
                        n = e * QUAD + j
                        if not first or n >= 4:
                            pe.wait_ge(M["acc"].sem, M["acc"].at(16 * i + n - 3))
                        products(pb[4 + j][0:S, 0:DO], [hsrc[:, k, j * S:(j + 1) * S] for k in range(FT)],
                                 [w[:, k, :] for k in range(FT)]).then_inc(M["dn"].sem, 1)

                for m in range(FT):
                    up(up0, m, xf, KT, [])
                for m in range(FT):
                    up(l1, m, xf, KT, [])
                for m in range(FT):
                    up(g1, m, xf, KT, [])
                    up(u1, m, xf, KT, [])
                for m in range(FT):
                    up(l2, m, lambda k: m_ha[:, k, :], FT, [(M["ev"], UPS * i + 8)])
                down(dn0, m_h0, 0, [(M["ev"], UPS * i + 4)])
                for m in range(KT):
                    up(d3, m, xf, KT, [])
                for m in range(FT):
                    up(l3, m, lambda k: m_hb[:, k, :], FT, [(M["ev"], UPS * i + 20)])
                for m in range(FT):
                    up(up3, m, lambda k: m_hc[:, k, :], KT, [(M["ev"], UPS * i + 22)])
                down(dn1, m_h1, 1, [(M["h1"], 4 * i + 4)])
                down(dn2, m_ha, 2, [(M["ev"], UPS * i + 26)])
                down(dn3, m_hd, 3, [(M["ev"], UPS * i + 30)])

            for sem, n in (("e0", 2), ("e1", 3), ("e2", 4), ("e3", 3)):
                pe.wait_ge(ld[sem].sem, ld[sem].at(16 * n))
            pe.wait_ge(G["le"].sem, G["le"].at(B))
            pe.wait_ge(G["cp"].sem, G["cp"].at(B))
            phase_m(0, True)
            with pe.Fori(1, B // QUAD) as i:
                phase_m(i, False)

            def d_qk_(b, u, half):
                pe.wait_ge(Ds["xte"].sem, Ds["xte"].at(b + 1))
                products(pb[0][:, 0:S], [wdd[:, k, :] for k in range(KT)],
                         [c_xnT[:, k, :] for k in range(KT)]).then_inc(Ds["c"].sem, 1)

            def d_v_(b, u, half):
                pe.wait_ge(Ds["ce"].sem, Ds["ce"].at(b + 1))
                pe.wait_ge(Ds["ve"].sem, Ds["ve"].at(b))
                pe.wait_ge(Ds["xu"].sem, Ds["xu"].at(b - 2))
                products(pb[1][0:S, 0:D], [c_cT], [wuv[:, :]]).then_inc(Ds["v"].sem, 1)

            def d_columns(b):
                pe.wait_ge(Ds["kb"].sem, Ds["kb"].at(b))
                for n in range(4):
                    last = T3.matmul(pb[7][:, n * S:(n + 1) * S], wuqk[:, n // 2, (n % 2) * P:(n % 2 + 1) * P], c_cT,
                                     start=True, stop=True)
                last.then_inc(Ds["t7"].sem, 1)

            pe.wait_ge(M["acc"].sem, M["acc"].at(64))
            pe.wait_ge(ld["d4"].sem, 96)
            attention(Ds, d_qk_, d_v_, Ds["ce"], d_columns, wo4, slice(0, D))

            def e_qk_(b, u, half):
                v = 1 - u
                pe.wait_ge(Es["xte"].sem, Es["xte"].at(b + 1))
                pe.wait_ge(Es[f"k{v}"].sem, Es[f"k{v}"].at(16 * (half + 1) if v else 16 * (half + 2)))
                products(pb[0][0:S, 0:D], [c_xnT[:, k, :] for k in range(KT)], [wq5[:, k, :] for k in range(KT)])
                products(pb[0][0:S, D:2 * D], [e_ctx[v][:, k, :] for k in range(KT)],
                         [wk5[:, k, :] for k in range(KT)]).then_inc(Es["qk"].sem, 1)

            def e_v_(b, u, half):
                pe.wait_ge(Es["ve"].sem, Es["ve"].at(b))
                pe.wait_ge(Es["xu"].sem, Es["xu"].at(b - 2))
                products(pb[1][0:S, 0:D], [e_ctx[1 - u][:, k, :] for k in range(KT)],
                         [wv5[:, k, :] for k in range(KT)]).then_inc(Es["v"].sem, 1)

            pe.wait_ge(Ds["xu"].sem, Ds["xu"].at(B))
            pe.wait_ge(ld["e5"].sem, 64)
            attention(Es, e_qk_, e_v_, Es["z"], columns_of(Es), wo5, slice(0, D))

            def phase_f(b, u, half):
                if on(b):
                    pe.wait_ge(Fs["qz"].sem, Fs["qz"].at(b + 1))
                    pe.wait_ge(Fs["xte"].sem, Fs["xte"].at(b))
                    transposes(f_q, S, KT, pb[u]).then_inc(Fs["xt"].sem, 1)
                    pe.wait_ge(Fs["xte"].sem, Fs["xte"].at(b + 1))
                    pe.wait_ge(Fs["xu"].sem, Fs["xu"].at(b - 1))
                    products(pb[2 + u][0:S, 0:D], [f_xT[:, k, :] for k in range(KT)],
                             [tern[:, k, :] for k in range(KT)]).then_inc(Fs["mm"].sem, 1)

            pe.wait_ge(Es["xu"].sem, Es["xu"].at(B))
            pe.wait_ge(pre["tern"].sem, 4)
            batches(pe, phase_f, 1)

        @block.gpsimd
        def _(pool):
            g_ = nc.gpsimd
            for i, v in enumerate((-0.5, 1e-5, RMS_EPS, 1.0 / HD, 1.0 / D)):
                g_.memset(kcol[:, i, :], v).then_inc(pre["scale"].sem, 1)
            for u in range(2):
                g_.memset(b_cp[u], 0.0).then_inc(pre["zero"].sem, 1)
            for u in range(2):
                last = g_.memset(b_cv[u][:, :, :, HD:HD + 1], 1.0)
            last.then_inc(pre["pad"].sem, 1)
            pool.wait_ge(pre["scale"].sem, 5)
            pool.wait_ge(pre["zero"].sem, 2)
            g_.memset(wuqk[:, :, :], 0.0).then_inc(pre["pad"].sem, 1)
            pool.wait_ge(pre["pad"].sem, 2)
            g_.memset(wuv[:, :], 0.0).then_inc(pre["pad"].sem, 1)

            def phase_a(b, u, half):
                if on(b + 1):
                    ln_rstd(A, b + 1, 2)
                    pool.wait_ge(A["xn"].sem, A["xn"].at(b + 2))
                    pool.wait_ge(ld["bo"].sem, 16)
                    g_.tensor_tensor(xb_(b + 1), xb_(b + 1), bo0, ALU.add).then_inc(A["xb"].sem, 1)

            batches(pool, phase_a, 1)

            def phase_b(b, u, half):
                if on(b + 1):
                    ln_rstd(Bs, b + 1, 2)

            pool.wait_ge(A["xu"].sem, A["xu"].at(B))
            g_.memset(b_xn, 0.0).then_inc(pre["bx"].sem, 1)
            pool.wait_ge(pre["bx"].sem, 1)
            g_.memset(b_xn[:, :, 0:1], 1.0).then_inc(pre["bx"].sem, 1)
            batches(pool, phase_b, 1)

            def phase_c(b, u, half):
                if on(b + 1):
                    n = b + 1
                    pool.wait_ge(Cs["ss"].sem, Cs["ss"].at(n + 1))
                    pool.wait_ge(Cs["qkn"].sem, Cs["qkn"].at(n))
                    g_.tensor_tensor(c_r, c_ss, kcol[:, 3, :], ALU.mult).then_inc(Cs["rc"].sem, 1)
                    pool.wait_ge(Cs["rc"].sem, Cs["rc"].at(2 * n + 1))
                    g_.tensor_tensor(c_r, c_r, kcol[:, 2, :], ALU.add).then_inc(Cs["rc"].sem, 1)
                    pool.wait_ge(Cs["rc"].sem, Cs["rc"].at(2 * n + 2))
                    g_.tensor_tensor(c_r, c_r, kcol[:, 0, :], ALU.pow).then_inc(Cs["r"].sem, 1)
                if on(b + 2):
                    n = b + 2
                    ln_rstd(Cs, n, 6)
                    pool.wait_ge(Cs["pc"].sem, Cs["pc"].at(6 * n + 2))
                    g_.tensor_tensor(rstd[:, 2:3], rstd[:, 1:2], rstd[:, 1:2], ALU.mult).then_inc(Cs["pc"].sem, 1)
                    pool.wait_ge(Cs["pc"].sem, Cs["pc"].at(6 * n + 3))
                    g_.tensor_tensor(rstd[:, 3:4], rstd[:, 2:3], mv[:, 1:2], ALU.mult).then_inc(Cs["pc"].sem, 1)
                    pool.wait_ge(Cs["pc"].sem, Cs["pc"].at(6 * n + 4))
                    g_.tensor_tensor(rstd[:, 4:5], rstd[:, 3:4], kcol[:, 2, 0:1], ALU.add).then_inc(Cs["pc"].sem, 1)
                    pool.wait_ge(Cs["pc"].sem, Cs["pc"].at(6 * n + 5))
                    g_.tensor_tensor(rstd[:, 5:6], rstd[:, 4:5], kcol[:, 0, 0:1], ALU.pow).then_inc(Cs["pc"].sem, 1)

            pool.wait_ge(Bs["xu"].sem, Bs["xu"].at(B))
            g_.memset(c_v[0][:, :, HD:HD + 1], 1.0)
            g_.memset(c_v[1][:, :, HD:HD + 1], 1.0).then_inc(pre["cv"].sem, 1)
            pool.wait_ge(pre["cv"].sem, 1)
            batches(pool, phase_c, 2)

            def phase_g(b, u, half):
                if on(b):
                    pool.wait_ge(G["sq"].sem, G["sq"].at(b + 1))
                    g_.tensor_tensor(g_ms[:, 1:2], g_ms[:, 0:1], kcol[:, 4, 0:1], ALU.mult).then_inc(G["pc"].sem, 1)
                    pool.wait_ge(G["pc"].sem, G["pc"].at(3 * b + 1))
                    g_.tensor_tensor(g_ms[:, 2:3], g_ms[:, 1:2], kcol[:, 2, 0:1], ALU.add).then_inc(G["pc"].sem, 1)
                    pool.wait_ge(G["pc"].sem, G["pc"].at(3 * b + 2))
                    g_.tensor_tensor(g_ms[:, 3:4], g_ms[:, 2:3], kcol[:, 0, 0:1], ALU.pow).then_inc(G["pc"].sem, 1)
                    g_.tensor_tensor(xb_(b), xb_(b), yb_(b), ALU.add).then_inc(G["xy"].sem, 1)
                if on(b - 1):
                    pool.wait_ge(G["xte"].sem, G["xte"].at(b))
                    pool.wait_ge(ld["gate"].sem, 16)
                    g_.tensor_copy(m_xfT[:, :, bass.ds((b - 1) * S, S)], g_cols).then_inc(G["cp"].sem, 1)

            pool.wait_ge(Cs["xu"].sem, Cs["xu"].at(B))
            batches(pool, phase_g, 1)

            def normalise(s, bias):
                def body(b, u, half):
                    if bias is not None and on(b + 1):
                        n = b + 1
                        pool.wait_ge(s["rope"].sem, s["rope"].at(n + 1))
                        pool.wait_ge(s["t7"].sem, s["t7"].at(n))
                        g_.tensor_tensor(c_qk, c_sq, c_t2, ALU.add).then_inc(s["qkn"].sem, 1)
                    if on(b + 2):
                        n = b + 2
                        ln_rstd(s, n, 2)
                        if bias is not None:
                            pool.wait_ge(s["xn"].sem, s["xn"].at(n + 1))
                            pool.wait_ge(ld["b5"].sem, 64)
                            g_.tensor_tensor(xb_(n), xb_(n), bias, ALU.add).then_inc(s["xb"].sem, 1)
                return body

            pool.wait_ge(M["acc"].sem, M["acc"].at(64))
            g_.memset(c_v[0][:, :, HD:HD + 1], 1.0)
            g_.memset(c_v[1][:, :, HD:HD + 1], 1.0).then_inc(pre["cv"].sem, 1)
            pool.wait_ge(pre["cv"].sem, 2)
            batches(pool, normalise(Ds, None), 2)
            pool.wait_ge(Ds["xu"].sem, Ds["xu"].at(B))
            pool.wait_ge(ld["b5"].sem, 64)
            batches(pool, normalise(Es, b5[:, 3, :]), 2)

            def phase_f(b, u, half):
                if on(b + 1):
                    ln_rstd(Fs, b + 1, 2)
                    pool.wait_ge(Fs["xn"].sem, Fs["xn"].at(b + 2))
                    pool.wait_ge(ld["f6"].sem, 32)
                    g_.tensor_tensor(xb_(b + 1), xb_(b + 1), b6[:, :], ALU.add).then_inc(Fs["xb"].sem, 1)

            pool.wait_ge(Es["xu"].sem, Es["xu"].at(B))
            pool.wait_ge(ld["f6"].sem, 32)
            batches(pool, phase_f, 1)

        @block.scalar
        def _(act):
            a_ = nc.scalar

            def phase_a(b, u, half):
                if on(b):
                    for g in range(4):
                        act.wait_ge(A["pj"].sem, A["pj"].at(6 * b + g + 1))
                        act.wait_ge(A["ph"].sem, A["ph"].at(4 * b + g - 1))
                        a_.activation(a_e[:, g % 2, :], a_z[:, g % 2, :], ACT.Exp, bias=minus_one[:, :]).then_inc(A["ex"].sem, 1)
                if on(b - 1):
                    for g in range(2):
                        act.wait_ge(A["ot"].sem, A["ot"].at(2 * (b - 1) + g + 1))
                        a_.activation(a_oT[:, g * 4 * S:(g + 1) * 4 * S], pb[2 + g][:, 0:4 * S], ACT.Copy).then_inc(A["oe"].sem, 1)
                if on(b + 1):
                    act.wait_ge(A["xt"].sem, A["xt"].at(b + 2))
                    a_.activation(a_xnT.rearrange("p k s -> p (k s)"), pb[7][:, 0:KT * S], ACT.Copy).then_inc(A["xte"].sem, 1)

            act.wait_ge(pre["m1"].sem, 1)
            batches(act, phase_a, 1)

            def phase_b(b, u, half):
                for p in range(8):
                    if on(b):
                        for e in range(2):
                            h = 2 * p + e
                            act.wait_ge(Bs["nb"].sem, Bs["nb"].at(8 * b + p + 1))
                            act.wait_ge(Bs["tp"].sem, Bs["tp"].at(16 * b + 2 * p - 2))
                            a_.activation(b_p[:, p % 2, e, :], pb[2 * (p % 2) + e][0:S, 0:SC], ACT.Exp,
                                          bias=b_nb[:, h:h + 1], scale=1.0 / 16).then_inc(Bs["ex"].sem, 1)
                    bt, pt = (b, p - 1) if p else (b - 1, 7)
                    if on(bt):
                        h = 2 * pt + 1
                        act.wait_ge(Bs["tp"].sem, Bs["tp"].at(16 * bt + h + 1))
                        a_.activation(b_pT[:, h % 4, :], pb[5][0:KC, 0:NKC * S], ACT.Copy).then_inc(Bs["tea"].sem, 1)
                    if p == 2 and on(b - 1):
                        act.wait_ge(Bs["ot"].sem, Bs["ot"].at(b))
                        a_.activation(b_oT, pb[7][:, 0:KT * S], ACT.Copy).then_inc(Bs["oe"].sem, 1)

            act.wait_ge(A["xu"].sem, A["xu"].at(B))
            batches(act, phase_b, 1)

            def attention(s, scale, head, columns, xt_scale):
                def body(b, u, half):
                    if on(b + 1) and head is not None:
                        head(b + 1)
                    for g in range(4):
                        if g % 2 and on(b - 1):
                            act.wait_ge(s["tp"].sem, s["tp"].at(4 * b + g - 3))
                            a_.activation(c_pT[:, g * 4 * S:(g + 1) * 4 * S], pb[5][0:S, 0:4 * S],
                                          ACT.Copy).then_inc(s["tea"].sem, 1)
                        if on(b):
                            act.wait_ge(s["nb"].sem, s["nb"].at(4 * b + g + 1))
                            act.wait_ge(s["tp"].sem, s["tp"].at(4 * b + g - 3))
                            for j in range(4):
                                h = 4 * g + j
                                last = a_.activation(c_p[:, h * S:(h + 1) * S], c_ms[:, h * S:(h + 1) * S], ACT.Exp,
                                                     bias=c_nb[:, h:h + 1], scale=scale)
                            last.then_inc(s["ex"].sem, 1)
                    if on(b + 2):
                        act.wait_ge(s["xt"].sem, s["xt"].at(b + 3))
                        for k in range(KT):
                            f = xt_scale[:, k:k + 1] if xt_scale is not None else 1.0
                            last = a_.activation(c_xnT[:, k, :], pb[0][:, k * S:(k + 1) * S], ACT.Copy, scale=f)
                        last.then_inc(s["xte"].sem, 1)
                    if on(b + 1):
                        act.wait_ge(s["t7"].sem, s["t7"].at(b + 2))
                        a_.activation(c_qT.rearrange("p k s -> p (k s)"), pb[7][:, 0:KT * S], ACT.Copy,
                                      scale=columns).then_inc(s["qe"].sem, 1)
                    if on(b - 1):
                        act.wait_ge(s["ot"].sem, s["ot"].at(b))
                        a_.activation(c_oT.rearrange("p k s -> p (k s)"), pb[6][:, 0:KT * S],
                                      ACT.Copy).then_inc(s["oe"].sem, 1)
                batches(act, body, 2, 2)

            def c_square(b):
                act.wait_ge(Cs["qk"].sem, Cs["qk"].at(b + 1))
                act.wait_ge(Cs["ss"].sem, Cs["ss"].at(b))
                a_.activation(c_sq, pb[0][0:S, :], ACT.Square).then_inc(Cs["sq"].sem, 1)

            act.wait_ge(Bs["xu"].sem, Bs["xu"].at(B))
            act.wait_ge(ld["c2"].sem, ld["c2"].at(16 * 17))
            attention(Cs, 0.25, c_square, qkn[:, 0:1], n12[:, 0:2])

            def phase_g(b, u, half):
                if on(b):
                    act.wait_ge(G["pc"].sem, G["pc"].at(3 * b))
                    a_.activation(g_sq, yb_(b), ACT.Square, accum_out=g_ms[:, 0:1]).then_inc(G["sq"].sem, 1)
                if on(b):
                    act.wait_ge(G["xt"].sem, G["xt"].at(b + 1))
                    act.wait_ge(G["lg"].sem, G["lg"].at(b))
                    act.wait_ge(G["cp"].sem, G["cp"].at(b))
                    for k in range(KT):
                        last = a_.activation(g_cols[:, k, :], pb[0][:, k * S:(k + 1) * S], ACT.Copy, scale=n12[:, 2 + k:3 + k])
                    last.then_inc(G["xte"].sem, 1)
                    act.wait_ge(G["lg"].sem, G["lg"].at(b + 1))
                    a_.activation(g_lg[:, bass.ds(b * 4, 4)], pb[1][0:S, 0:4], ACT.Copy).then_inc(G["le"].sem, 1)

            act.wait_ge(Cs["xu"].sem, Cs["xu"].at(B))
            batches(act, phase_g, 1)
            act.wait_ge(G["wt"].sem, G["wt"].at(1))
            a_.activation(g_b2, g_a, ACT.Exp).then_inc(G["wt"].sem, 1)

            def phase_m(i):
                plan = ([("gelu", m_h0, m) for m in range(4)] + [("gelu", m_ha, m) for m in range(4)]
                        + [x for m in range(4) for x in (("gate", None, m), ("up", None, m))]
                        + [("gelu", m_hb, m) for m in range(4)] + [("gelu", m_hc, m) for m in range(2)]
                        + [("gelu", m_ha, m) for m in range(4)] + [("gelu", m_hd, m) for m in range(4)])
                for n, (what, dst, m) in enumerate(plan):
                    src = pb[n % 4][:, 0:QN]
                    act.wait_ge(M["up"].sem, M["up"].at(UPS * i + n + 1))
                    if what == "gelu":
                        a_.activation(dst[:, m, :], src, ACT.Gelu).then_inc(M["ev"].sem, 1)
                    elif what == "gate":
                        act.wait_ge(M["h1"].sem, M["h1"].at(4 * i + m - 1))
                        a_.activation(m_s[:, m % 2, :], src, ACT.Tanh, scale=0.5)
                        a_.activation(m_g[:, m % 2, :], src, ACT.Copy).then_inc(M["ev"].sem, 1)
                    else:
                        a_.activation(m_u[:, m % 2, :], src, ACT.Copy).then_inc(M["ev"].sem, 1)

            phase_m(0)
            with act.Fori(1, B // QUAD) as i:
                phase_m(i)

            def d_latent(b):
                act.wait_ge(Ds["c"].sem, Ds["c"].at(b + 1))
                a_.activation(c_cT, pb[0][:, 0:S], ACT.Copy).then_inc(Ds["ce"].sem, 1)

            act.wait_ge(M["acc"].sem, M["acc"].at(64))
            attention(Ds, 0.25, d_latent, 1.0, None)
            act.wait_ge(Ds["xu"].sem, Ds["xu"].at(B))
            attention(Es, 0.25, None, 1.0, None)

            def phase_f(b, u, half):
                if on(b):
                    act.wait_ge(Fs["xt"].sem, Fs["xt"].at(b + 1))
                    act.wait_ge(Fs["mm"].sem, Fs["mm"].at(b))
                    a_.activation(f_xT.rearrange("p k s -> p (k s)"), pb[u][:, 0:KT * S], ACT.Copy).then_inc(Fs["xte"].sem, 1)

            act.wait_ge(Es["xu"].sem, Es["xu"].at(B))
            batches(act, phase_f, 1)

        @block.vector
        def _(dve):
            v_ = nc.vector

            def chain(s):
                return s["chain"]

            v_.memset(minus_one[:, :], -1.0).then_inc(pre["m1"].sem, 1)
            v_.memset(a_v[:, :, LD:LD + 1], 1.0).then_inc(pre["av"].sem, 1)
            dve.wait_ge(ld["bias"].sem, 32)
            v_.tensor_scalar(bqk0[:, :], bqk0[:, :], 1.0, None, ALU.add).then_inc(pre["bias1"].sem, 1)
            dve.wait_ge(ld["x"].sem, 16)
            dve.wait_ge(pre["bias1"].sem, 1)
            dve.wait_ge(ld["cst"].sem, 16)

            def stats_of(s, b, per, at):
                ln_stats(s, b, None)
                dve.wait_ge(s["chain"].sem, s["chain"].at(per * b + at + 1))
                v_.memset(rstd[:, 7:8], 0.0)
                v_.bn_aggr(mv[:, :], stats[:, :]).then_inc(s["mv"].sem, 1)

            def phase_a(b, u, half):
                if on(b + 1):
                    stats_of(A, b + 1, 1, 0)
                if isinstance(b, int) and b == -1:
                    ln_apply(A, 0, a_xn, 2, None).then_inc(A["xn"].sem, 1)
                if on(b):
                    def z_of(g):
                        dve.wait_ge(A["pg"].sem, A["pg"].at(6 * b + g + 1))
                        dve.wait_ge(A["ph"].sem, A["ph"].at(4 * b + g - 1))
                        bias = bqk0[:, 4 * g:4 * g + 4].unsqueeze(2).to_broadcast([P, 4, S])
                        v_.tensor_tensor(a_z[:, g % 2, :].rearrange("p (m s) -> p m s", m=4),
                                         pb[g % 2][:, 0:4 * S].rearrange("p (m s) -> p m s", m=4), bias,
                                         ALU.add).then_inc(A["pj"].sem, 1)

                    def phi_of(g):
                        dve.wait_ge(A["ex"].sem, A["ex"].at(4 * b + g + 1))
                        dst = (a_q if g < 2 else a_k)[:, (g % 2) * 4 * S:(g % 2 + 1) * 4 * S]
                        v_.scalar_tensor_tensor(dst, a_e[:, g % 2, :], 1.0, a_z[:, g % 2, :], ALU.min,
                                                ALU.max).then_inc(A["ph"].sem, 1)

                    def v_of(g):
                        dve.wait_ge(A["pg"].sem, A["pg"].at(6 * b + 5 + g))
                        v_.tensor_tensor(a_v[:, 8 * g:8 * g + 8, 0:LD],
                                         pb[g][0:S, :].rearrange("s (h e) -> s h e", h=8),
                                         bv0[:, g * 512:(g + 1) * 512].rearrange("s (h e) -> s h e", h=8),
                                         ALU.add).then_inc(A["pj"].sem, 1)

                    for g in range(4):
                        z_of(g)
                        if g:
                            phi_of(g - 1)
                    v_of(0)
                    phi_of(3)
                    v_of(1)
                    if on(b + 1):
                        ln_apply(A, b + 1, a_xn, 2, (A["xt"], b + 1)).then_inc(A["xn"].sem, 1)
                    tri = cst[0:S, C_TRI:C_TRI + S].unsqueeze(1).to_broadcast([S, 4, S])
                    for g in range(4):
                        dve.wait_ge(A["sg"].sem, A["sg"].at(4 * b + g + 1))
                        v_.tensor_tensor(a_at.rearrange("k (x j e s) -> k x e j s", x=2, j=4, e=2)[:, g // 2, g % 2],
                                         pb[2 + g % 2][0:S, 0:4 * S].rearrange("p (j s) -> p j s", j=4), tri,
                                         ALU.mult).then_inc(A["sm"].sem, 1)
                if on(b - 1):
                    dve.wait_ge(A["wd"].sem, A["wd"].at(b))
                    dve.wait_ge(A["xb"].sem, A["xb"].at(b))
                    v_.tensor_tensor(xb_(b - 1), xb_(b - 1), pb[7][0:S, 0:D], ALU.add).then_inc(A["xu"].sem, 1)
                if on(b):
                    dve.wait_ge(A["nd"].sem, A["nd"].at(3 * b + 3))
                    for n, (lo, hi) in enumerate(NUM):
                        num = pb[4 + n][0:S, 0:(hi - lo) * (LD + 1)].rearrange("s (h e) -> s h e", e=LD + 1)
                        last = v_.tensor_scalar(a_den[:, lo:hi].unsqueeze(2), num[:, :, LD:LD + 1], 1e-6, None, ALU.add)
                    last.then_inc(A["den"].sem, 1)
                    dve.wait_ge(A["den"].sem, A["den"].at(2 * b + 1))
                    v_.reciprocal(a_den[:, 16:32], a_den[:, 0:16]).then_inc(A["den"].sem, 1)
                    dve.wait_ge(A["den"].sem, A["den"].at(2 * b + 2))
                    for n, (lo, hi) in enumerate(NUM):
                        num = pb[4 + n][0:S, 0:(hi - lo) * (LD + 1)].rearrange("s (h e) -> s h e", e=LD + 1)
                        v_.tensor_tensor(a_o[:, lo * LD:hi * LD].rearrange("s (h e) -> s h e", e=LD), num[:, :, 0:LD],
                                         a_den[:, 16 + lo:16 + hi].unsqueeze(2).to_broadcast([S, hi - lo, LD]),
                                         ALU.mult).then_inc(A["nm"].sem, 1)

            dve.wait_ge(pre["av"].sem, 1)
            dve.wait_ge(ld["a2"].sem, 32)
            batches(dve, phase_a, 1)

            def phase_b(b, u, half):
                for p in range(8):
                    if p == 0 and on(b + 1):
                        stats_of(Bs, b + 1, 1, 0)
                    if on(b):
                        dve.wait_ge(Bs["sg"].sem, Bs["sg"].at(8 * b + p + 1))
                        pair = banks[0:S, 2 * (p % 2):2 * (p % 2) + 2, 0:SC]
                        v_.tensor_reduce(b_mx[:, 2 * p:2 * p + 2], pair, AX_X, ALU.max).then_inc(Bs["mx"].sem, 1)
                        dve.wait_ge(Bs["mx"].sem, Bs["mx"].at(8 * b + p + 1))
                        v_.tensor_scalar(b_nb[:, 2 * p:2 * p + 2], b_mx[:, 2 * p:2 * p + 2], -1.0 / 16, None,
                                         ALU.mult).then_inc(Bs["nb"].sem, 1)
                    bt, pt = (b, p - 1) if p else (b - 1, 7)
                    if on(bt):
                        h = 2 * pt
                        dve.wait_ge(Bs["tp"].sem, Bs["tp"].at(16 * bt + h + 1))
                        v_.tensor_copy(b_pT[:, h % 4, :], pb[4][0:KC, 0:NKC * S]).then_inc(Bs["ted"].sem, 1)
                    if p == 1 and on(b - 1):
                        normalise(Bs, b - 1, 16 * b, b_rc, b_o)
                    if on(b + 1) and p == 2:
                        dve.wait_ge(pre["bx"].sem, 2)
                        ln_heads(b + 1)
                    if p == 3 and on(b - 1):
                        dve.wait_ge(Bs["wd"].sem, Bs["wd"].at(b))
                        v_.tensor_tensor(xb_(b - 1), xb_(b - 1), pb[7][0:S, 0:D], ALU.add).then_inc(Bs["xu"].sem, 1)
                    if p == 5 and on(b + 1):
                        dve.wait_ge(Bs["xt"].sem, Bs["xt"].at(b + 2))
                        bm4 = cst[:, C_BM4:C_BM4 + 4].unsqueeze(2).to_broadcast([P, 4, S])
                        for t in range(4):
                            last = v_.tensor_tensor(b_bd[1 - u][:, t * 4 * S:(t + 1) * 4 * S].rearrange("p (j s) -> p j s", j=4),
                                                    pb[7][:, t * S:(t + 1) * S].unsqueeze(1).to_broadcast([P, 4, S]), bm4, ALU.mult)
                        last.then_inc(Bs["bd"].sem, 1)

            def ln_heads(b):
                dve.wait_ge(Bs["pc"].sem, Bs["pc"].at(b * 2 + 2))
                dve.wait_ge(Bs["xt"].sem, Bs["xt"].at(b))
                v_.tensor_scalar(b_xn[:, :, 1:1 + HD], xb_(b).rearrange("s (h e) -> s h e", h=H), mv[:, 0:1],
                                 rstd[:, 1:2], ALU.subtract, ALU.mult).then_inc(Bs["xn"].sem, 1)

            def normalise(s, b, pv, rc, o):
                dve.wait_ge(s["pv"].sem, s["pv"].at(pv))
                acc = pb[6][0:S, 0:H * 17].rearrange("s (h e) -> s h e", e=17)
                v_.reciprocal(rc.unsqueeze(2), acc[:, :, HD:HD + 1]).then_inc(s["den"].sem, 1)
                dve.wait_ge(s["den"].sem, s["den"].at(b + 1))
                v_.tensor_tensor(o.rearrange("s (h e) -> s h e", e=HD), acc[:, :, 0:HD],
                                 rc.unsqueeze(2).to_broadcast([S, H, HD]), ALU.mult).then_inc(s["nm"].sem, 1)

            dve.wait_ge(ld["mask"].sem, 16)
            v_.tensor_scalar(mask_f[:, :], mask_i[:, :], 0, -1e20, ALU.is_equal, ALU.mult).then_inc(pre["rowbias"].sem, 1)
            dve.wait_ge(A["xu"].sem, A["xu"].at(B))
            batches(dve, phase_b, 1)

            def c_ln(b):
                ln_apply(Cs, b, yb_(b), 6, None).then_inc(Cs["y"].sem, 1)
                dve.wait_ge(Cs["y"].sem, Cs["y"].at(b + 1))
                dve.wait_ge(Cs["pc"].sem, Cs["pc"].at(6 * b + 6))
                dve.wait_ge(Cs["xt"].sem, Cs["xt"].at(b))
                v_.tensor_scalar(c_h, yb_(b), rstd[:, 5:6], None, ALU.mult).then_inc(Cs["xn"].sem, 1)

            def x_ln(s):
                def f(b):
                    ln_apply(s, b, c_h, 2, (s["xt"], b)).then_inc(s["xn"].sem, 1)
                return f

            def attention(s, mask_col, ln_of, v_in, before, between, kbm, residual):
                mask = cst[0:S, mask_col:mask_col + S].unsqueeze(1).to_broadcast([S, 4, S])

                def body(b, u, half):
                    if on(b + 1):
                        before(b + 1)
                    for g in range(4):
                        if on(b):
                            dve.wait_ge(s["sg"].sem, s["sg"].at(4 * b + g + 1))
                            dve.wait_ge(s["ex"].sem, s["ex"].at(4 * b + g - 3))
                            ms = c_ms[:, g * 4 * S:(g + 1) * 4 * S].rearrange("q (j s) -> q j s", j=4)
                            v_.tensor_tensor(ms, pb[2 + g % 2][0:S, 0:4 * S].rearrange("q (j s) -> q j s", j=4),
                                             mask, ALU.add).then_inc(s["mk"].sem, 1)
                            dve.wait_ge(s["mk"].sem, s["mk"].at(4 * b + g + 1))
                            v_.tensor_reduce(c_mx[:, 4 * g:4 * g + 4], ms, AX_X, ALU.max).then_inc(s["mxd"].sem, 1)
                            dve.wait_ge(s["mxd"].sem, s["mxd"].at(4 * b + g + 1))
                            v_.tensor_scalar(c_nb[:, 4 * g:4 * g + 4], c_mx[:, 4 * g:4 * g + 4], -0.25, None,
                                             ALU.mult).then_inc(s["nb"].sem, 1)
                        if g % 2 == 0 and on(b - 1):
                            dve.wait_ge(s["tp"].sem, s["tp"].at(4 * b + g - 3))
                            v_.tensor_copy(c_pT[:, g * 4 * S:(g + 1) * 4 * S], pb[4][0:S, 0:4 * S]).then_inc(s["ted"].sem, 1)
                        if g == 0 and on(b - 2):
                            dve.wait_ge(s["wd"].sem, s["wd"].at(b - 1))
                            residual(b - 2)
                        if g == 1 and on(b + 1):
                            between(b + 1)
                        if g == 1 and on(b + 2):
                            stats_of(s, b + 2, 1, 0)
                        if g == 3 and on(b + 2):
                            ln_of(b + 2)
                    if on(b - 1):
                        normalise(s, b - 1, b, c_rc, c_o)
                    if on(b + 1):
                        v_in(b + 1, 1 - u)
                        dve.wait_ge(s["qe"].sem, s["qe"].at(b + 2))
                        for k in range(KT):
                            last = v_.tensor_tensor(c_kbd[:, k, :, :],
                                                    pb[7][:, (KT + k) * S:(KT + k + 1) * S].unsqueeze(1).to_broadcast([P, 8, S]),
                                                    kbm.unsqueeze(2).to_broadcast([P, 8, S]), ALU.mult)
                        last.then_inc(s["kb"].sem, 1)
                batches(dve, body, 2, 2)

            def plain_v(s):
                def f(b, u):
                    dve.wait_ge(s["v"].sem, s["v"].at(b + 1))
                    v_.tensor_copy(c_v[u][:, :, 0:HD], pb[1][0:S, 0:D].rearrange("s (h e) -> s h e", h=H)).then_inc(s["ve"].sem, 1)
                return f

            def nothing(b):
                pass

            def c_sums(b):
                dve.wait_ge(Cs["sq"].sem, Cs["sq"].at(b + 1))
                dve.wait_ge(Cs["r"].sem, Cs["r"].at(b))
                v_.tensor_reduce(c_ss, c_sq.rearrange("s (h e) -> s h e", e=HD), AX_X, ALU.add).then_inc(Cs["ss"].sem, 1)

            def c_scaled(b):
                dve.wait_ge(Cs["r"].sem, Cs["r"].at(b + 1))
                v_.tensor_tensor(c_qk.rearrange("s (h e) -> s h e", e=HD), pb[0][0:S, :].rearrange("s (h e) -> s h e", e=HD),
                                 c_r.unsqueeze(2).to_broadcast([S, 32, HD]), ALU.mult).then_inc(Cs["qkn"].sem, 1)

            def c_residual(b):
                v_.tensor_tensor(yb_(b, FREE), yb_(b, FREE), pb[1][0:S, 0:DO], ALU.add).then_inc(Cs["xu"].sem, 1)

            def x_residual(s):
                def f(b):
                    v_.tensor_tensor(xb_(b), xb_(b), pb[1][0:S, 0:D], ALU.add).then_inc(s["xu"].sem, 1)
                return f

            dve.wait_ge(Bs["xu"].sem, Bs["xu"].at(B))
            dve.wait_ge(ld["c2"].sem, ld["c2"].at(16 * 17))
            v_.tensor_scalar(knbm, cst[:, C_BM:C_BM + 8], qkn[:, 1:2], None, ALU.mult).then_inc(pre["kn"].sem, 1)
            dve.wait_ge(pre["kn"].sem, 1)
            attention(Cs, C_CAUSAL, c_ln, plain_v(Cs), c_sums, c_scaled, knbm, c_residual)

            def phase_g(b, u, half):
                if on(b):
                    dve.wait_ge(G["pc"].sem, G["pc"].at(3 * b + 3))
                    dve.wait_ge(G["xt"].sem, G["xt"].at(b))
                    v_.tensor_scalar(g_xf, yb_(b), g_ms[:, 3:4], None, ALU.mult).then_inc(G["xf"].sem, 1)

            batches(dve, phase_g, 1)
            dve.wait_ge(G["le"].sem, G["le"].at(B))
            steps = [0]

            def step(ins):
                steps[0] += 1
                ins.then_inc(G["chain"].sem, 1)
                dve.wait_ge(G["chain"].sem, G["chain"].at(steps[0]))

            lg3, a3, p3, w3 = (t.rearrange("s (b e) -> s b e", e=4) for t in (g_lg, g_a, g_b2, g_w))
            step(v_.tensor_scalar(g_lg, g_lg, -FLT_MAX, FLT_MAX, ALU.max, ALU.min))
            step(v_.tensor_reduce(g_red, lg3, AX_X, ALU.max))
            v_.tensor_tensor(a3, lg3, g_red.unsqueeze(2).to_broadcast([S, B, 4]), ALU.subtract).then_inc(G["wt"].sem, 1)
            dve.wait_ge(G["wt"].sem, G["wt"].at(2))
            step(v_.tensor_reduce(g_red, p3, AX_X, ALU.add))
            step(v_.reciprocal(g_red2, g_red))
            step(v_.tensor_tensor(a3, p3, g_red2.unsqueeze(2).to_broadcast([S, B, 4]), ALU.mult))
            c4, d4 = (t.rearrange("s (b e f) -> s b e f", e=4, f=4) for t in (g_cmp, g_cmp2))
            other = a3.unsqueeze(2).to_broadcast([S, B, 4, 4])
            own = a3.unsqueeze(3).to_broadcast([S, B, 4, 4])
            lt = cst[0:S, C_LT:C_LT + 16].rearrange("s (e f) -> s e f", e=4).unsqueeze(1).to_broadcast([S, B, 4, 4])
            step(v_.tensor_tensor(c4, other, own, ALU.is_equal))
            step(v_.tensor_tensor(c4, c4, lt, ALU.mult))
            step(v_.tensor_tensor(d4, other, own, ALU.is_gt))
            step(v_.tensor_tensor(g_cmp, g_cmp, g_cmp2, ALU.add))
            step(v_.tensor_reduce(g_b2, g_cmp.rearrange("s (n f) -> s n f", f=4), AX_X, ALU.add))
            step(v_.tensor_scalar(g_b2, g_b2, 2.0, None, ALU.is_lt))
            step(v_.tensor_tensor(g_w, g_b2, g_a, ALU.mult))
            step(v_.tensor_reduce(g_red, w3, AX_X, ALU.add))
            step(v_.tensor_scalar(g_red, g_red, 1e-8, None, ALU.add))
            step(v_.reciprocal(g_red2, g_red))
            step(v_.tensor_tensor(w3, w3, g_red2.unsqueeze(2).to_broadcast([S, B, 4]), ALU.mult))
            dve.wait_ge(G["xy"].sem, G["xy"].at(B))

            def phase_m(i, first):
                for m in range(FT):
                    dve.wait_ge(M["ev"].sem, M["ev"].at(UPS * i + 10 + 2 * m))
                    v_.scalar_tensor_tensor(m_t[:, m % 2, :], m_s[:, m % 2, :], 1.0, m_g[:, m % 2, :], ALU.add,
                                            ALU.mult).then_inc(M["t"].sem, 1)
                    dve.wait_ge(M["t"].sem, M["t"].at(4 * i + m + 1))
                    v_.scalar_tensor_tensor(m_h1[:, m, :], m_t[:, m % 2, :], 0.5, m_u[:, m % 2, :], ALU.mult,
                                            ALU.mult).then_inc(M["h1"].sem, 1)
                for e in range(4):
                    for j in range(QUAD):
                        n = e * QUAD + j
                        b = i * QUAD + j
                        dve.wait_ge(M["dn"].sem, M["dn"].at(16 * i + n + 1))
                        if n >= QUAD:
                            dve.wait_ge(M["acc"].sem, M["acc"].at(16 * i + n - 3))
                        v_.scalar_tensor_tensor(xb_(b, FREE), pb[4 + j][0:S, 0:DO], g_w[:, bass.ds(b * 4 + e, 1)],
                                                xb_(b, FREE), ALU.mult, ALU.add).then_inc(M["acc"].sem, 1)

            phase_m(0, True)
            with dve.Fori(1, B // QUAD) as i:
                phase_m(i, False)

            dve.wait_ge(M["acc"].sem, M["acc"].at(64))
            attention(Ds, C_CAUSAL, x_ln(Ds), plain_v(Ds), nothing, nothing, cst[:, C_BM:C_BM + 8], x_residual(Ds))

            def e_v(b, u):
                dve.wait_ge(Es["v"].sem, Es["v"].at(b + 1))
                v_.tensor_tensor(c_v[u][:, :, 0:HD], pb[1][0:S, 0:D].rearrange("s (h e) -> s h e", h=H),
                                 b5[:, 2, :].rearrange("s (h e) -> s h e", h=H), ALU.add).then_inc(Es["ve"].sem, 1)

            def e_rotary(b):
                dve.wait_ge(Es["qk"].sem, Es["qk"].at(b + 1))
                dve.wait_ge(Es["rope"].sem, Es["rope"].at(b))
                z = c_z
                v_.tensor_tensor(z, pb[0][0:S, :], b5[:, 0:2, :].rearrange("s i n -> s (i n)"), ALU.add).then_inc(Es["z"].sem, 1)
                dve.wait_ge(Es["z"].sem, Es["z"].at(b + 1))
                dve.wait_ge(Es["qkn"].sem, Es["qkn"].at(b))
                z3, c3, t3 = (t.rearrange("s (h e) -> s h e", e=HD) for t in (z, c_sq, c_t2))
                cos = cst[0:S, C_COS:C_COS + HD].unsqueeze(1).to_broadcast([S, 32, HD])
                v_.tensor_tensor(c3, z3, cos, ALU.mult)
                for lo, hi in ((0, 8), (8, 0)):
                    sin = cst[0:S, C_SIN + lo:C_SIN + lo + 8].unsqueeze(1).to_broadcast([S, 32, 8])
                    last = v_.tensor_tensor(t3[:, :, lo:lo + 8], z3[:, :, hi:hi + 8], sin, ALU.mult)
                last.then_inc(Es["rope"].sem, 1)

            dve.wait_ge(Ds["xu"].sem, Ds["xu"].at(B))
            dve.wait_ge(ld["b5"].sem, 64)

            def e_res(b):
                dve.wait_ge(Es["xb"].sem, Es["xb"].at(b + 1))
                x_residual(Es)(b)

            attention(Es, C_BAND, x_ln(Es), e_v, e_rotary, nothing, cst[:, C_BM:C_BM + 8], e_res)

            dve.wait_ge(ld["pk"].sem, 16)
            dve.wait_ge(ld["f6"].sem, 32)
            for q in range(4):
                dve.wait_ge(pre["tern"].sem, pre["tern"].at(q))
                v_.tensor_scalar(enc[:, :, :], packed[:, :, :], 2 * q, 3, ALU.logical_shift_right,
                                 ALU.bitwise_and).then_inc(pre["enc"].sem, 1)
                dve.wait_ge(pre["enc"].sem, pre["enc"].at(q + 1))
                v_.tensor_scalar(tern[:, :, 64 * q:64 * q + 64], enc[:, :, :], -1.0, None, ALU.add).then_inc(pre["tern"].sem, 1)

            def phase_f(b, u, half):
                if on(b + 1):
                    stats_of(Fs, b + 1, 1, 0)
                if on(b):
                    dve.wait_ge(Fs["xn"].sem, Fs["xn"].at(b + 1))
                    v_.tensor_reduce(f_am[:, 0:1], f_xn, AX_X, ALU.max, apply_absolute_value=True).then_inc(Fs["am"].sem, 1)
                    dve.wait_ge(Fs["am"].sem, Fs["am"].at(6 * b + 1))
                    v_.tensor_scalar(f_am[:, 1:2], f_am[:, 0:1], 1e-5, None, ALU.max).then_inc(Fs["am"].sem, 1)
                    dve.wait_ge(Fs["am"].sem, Fs["am"].at(6 * b + 2))
                    v_.reciprocal(f_am[:, 2:3], f_am[:, 1:2]).then_inc(Fs["am"].sem, 1)
                    v_.tensor_scalar(f_sc[:, u:u + 1], f_am[:, 1:2], wscale[:, 0:1], 1.0 / 127, ALU.mult, ALU.mult)
                    dve.wait_ge(Fs["am"].sem, Fs["am"].at(6 * b + 3))
                    v_.tensor_scalar(f_am[:, 3:4], f_am[:, 2:3], 127.0, None, ALU.mult).then_inc(Fs["am"].sem, 1)
                    dve.wait_ge(Fs["am"].sem, Fs["am"].at(6 * b + 4))
                    dve.wait_ge(Fs["xt"].sem, Fs["xt"].at(b))
                    v_.tensor_scalar(f_q, f_xn, f_am[:, 3:4], ROUND, ALU.mult, ALU.add).then_inc(Fs["am"].sem, 1)
                    dve.wait_ge(Fs["am"].sem, Fs["am"].at(6 * b + 5))
                    v_.tensor_scalar(f_q, f_q, -ROUND, 127.0, ALU.add, ALU.min).then_inc(Fs["am"].sem, 1)
                    dve.wait_ge(Fs["am"].sem, Fs["am"].at(6 * b + 6))
                    v_.tensor_scalar(f_q, f_q, -128.0, None, ALU.max).then_inc(Fs["qz"].sem, 1)
                if on(b + 1):
                    ln_apply(Fs, b + 1, f_xn, 2, (Fs["qz"], b + 1)).then_inc(Fs["xn"].sem, 1)
                if on(b - 1):
                    dve.wait_ge(Fs["mm"].sem, Fs["mm"].at(b))
                    dve.wait_ge(Fs["xb"].sem, Fs["xb"].at(b))
                    v_.scalar_tensor_tensor(xb_(b - 1), pb[2 + (1 - u)][0:S, 0:D], f_sc[:, 1 - u:2 - u], xb_(b - 1), ALU.mult,
                                            ALU.add).then_inc(Fs["xu"].sem, 1)

            dve.wait_ge(Es["xu"].sem, Es["xu"].at(B))
            batches(dve, phase_f, 1)


def kernel(**inputs):
    import numpy as _np
    import concourse.bacc as _bacc
    from concourse import mybir as _mybir
    from concourse.bass_utils import run_bass_kernel_spmd as _run

    def a(name):
        return _np.asarray(inputs[name])

    def cols(v):
        return v.reshape(-1, P).T

    def row(v):
        return v.reshape(-1)

    f = "L0_ffn_"
    arrays = {
        "x": a("x"), "ctx": a("ctx_1024"), "ctxT": a("ctx_1024").transpose(0, 2, 1),
        "mask": a("mask_Bx1x1xS2_ik0").reshape(B, SC), "consts": constants(),
        "Wq": a("L0_attn_Wq"), "Wk": a("L0_attn_Wk"), "Wv": a("L0_attn_Wv"), "Wo": a("L0_attn_Wo"),
        "bq": cols(a("L0_attn_bq")), "bk": cols(a("L0_attn_bk")), "bv": row(a("L0_attn_bv")), "bo": row(a("L0_attn_bo")),
        "W_out": a("L0_xattn_W_out").T,
        "n12": _np.concatenate([cols(a(f + "n1_w")), cols(a(f + "n2_w"))], 1),
        "qn": a(f + "qn_w").reshape(HD, 1), "kn": a(f + "kn_w").reshape(HD, 1),
        "wq": a(f + "wq").T, "wk": a(f + "wk").T, "wv": a(f + "wv").T, "wo": a(f + "wo").T[:, FREE:],
        "gate": a(f + "gate_w").T,
        "e0_up": a(f + "e0_up").T, "e0_down": a(f + "e0_down").T[:, FREE:],
        "w1": a(f + "e1_w1").T, "w2": a(f + "e1_w2").T, "e1_down": a(f + "e1_down").T[:, FREE:],
        "l1": a(f + "e2_l1").T, "l2": a(f + "e2_l2").T, "l3": a(f + "e2_l3").T, "l4": a(f + "e2_l4").T[:, FREE:],
        "e3_down": a(f + "e3_down").T, "e3_up": a(f + "e3_up").T, "e3_out": a(f + "e3_out").T[:, FREE:],
        "W_dq": a("L1_attn_W_dq"), "W_uq": a("L1_attn_W_uq"), "W_dkv": a("L1_attn_W_dkv"),
        "W_uk": a("L1_attn_W_uk"), "W_uv": a("L1_attn_W_uv"), "W_o": a("L1_attn_W_o"),
        "packed": a("L1_ffn_packed_weight").reshape(64, D).T, "wscale": row(a("L1_ffn_weight_scale")),
        "bias": row(a("L1_ffn_bias")),
    }
    for n in "qkvo":
        arrays[f"{n}_w"] = a(f"L1_xattn_{n}_w").T
        arrays[f"{n}_b"] = row(a(f"L1_xattn_{n}_b"))
    arrays = {n: _np.ascontiguousarray(v) for n, v in arrays.items()}
    nc = _bacc.Bacc("TRN2", target_bir_lowering=False, num_devices=1)
    tensors = {n: nc.dram_tensor(f"in_{n}", v.shape, _mybir.dt.from_np(v.dtype), kind="ExternalInput").ap()
               for n, v in arrays.items()}
    out = nc.dram_tensor("out_0", (B, S, D), _mybir.dt.float32, kind="ExternalOutput").ap()
    decoder_kernel(nc, tensors, out)
    r = _run(nc, [{f"in_{n}": v for n, v in arrays.items()}], core_ids=[0])
    return r.results[0]["out_0"]
```

```python
from contextlib import ExitStack

import numpy as np
import concourse.bass as bass
from concourse import mybir

F32 = mybir.dt.float32
BF16 = mybir.dt.bfloat16
I32 = mybir.dt.int32
F32R = mybir.dt.float32r
ALU = mybir.AluOpType
ACT = mybir.ActivationFunctionType
AX_X = mybir.AxisListType.X

P = 128
B, S, D = 16, 112, 256
H, HD = 16, 16
SC = 375
SCP = SC + SC % 2
KC, NKC = 125, 3
LD = 64
LW = H * LD
KT = D // P
HID = 512
FT = HID // P
FREE = 64
DO = D - FREE
WINDOW = 64
QUAD = 4
QN = QUAD * S
BIG = 1e30
HIGH = -4096
B_WORK = 3600
STACK = 4 * HD + 1
AREA = 15696
B_OWN = 8864
RMS_EPS = 1.1920929e-07
FLT_MAX = 3.4028234663852886e38
ROUND = 1.5 * 2.0 ** 23
UPS = 30

C_ID = 0
C_TRI = C_ID + P
C_CAUSAL = C_TRI + S
C_BAND = C_CAUSAL + S
C_BM = C_BAND + S
C_COS = C_BM + 8
C_SIN = C_COS + HD
C_LT = C_SIN + HD
C_END = C_LT + 16


def constants():
    c = np.zeros((P, C_END), np.float32)
    c[:, C_ID:C_ID + P] = np.eye(P, dtype=np.float32)
    r = np.arange(S)
    c[:S, C_TRI:C_TRI + S] = r[:, None] <= r[None, :]
    c[:S, C_CAUSAL:C_CAUSAL + S] = np.where(r[None, :] <= r[:, None], 0, -BIG)
    c[:S, C_BAND:C_BAND + S] = np.where((r[None, :] <= r[:, None]) & (r[None, :] >= r[:, None] - WINDOW), 0, -BIG)
    p = np.arange(P)
    c[:, C_BM:C_BM + 8] = p[:, None] // HD == np.arange(8)[None, :]
    half = HD // 2
    freqs = (1.0 / 10000.0 ** (np.arange(half, dtype=np.float32) / half)).astype(np.float32)
    ang = r.astype(np.float32)[:, None] * freqs[None, :]
    c[:S, C_COS:C_COS + HD] = np.tile(np.cos(ang), (1, 2))
    c[:S, C_SIN:C_SIN + HD] = np.concatenate([-np.sin(ang), np.sin(ang)], 1)
    e = np.arange(4)
    c[:, C_LT:C_LT + 16] = (e[None, :] < e[:, None]).reshape(1, 16)
    return c


def on(b):
    return not isinstance(b, int) or 0 <= b < B


class Counter:

    def __init__(self, sem, base):
        self.sem, self.base = sem, base

    def at(self, value):
        return value + self.base if not isinstance(value, int) else max(value, 0) and value + self.base


def least(a, b):
    return min(a, b) if isinstance(a, int) else a


def batches(eng, body, ahead, behind=1):
    n = 6 if ahead == 1 else 5
    for b in range(-ahead, 3):
        body(b, b % 2, b // 2)
    with eng.Fori(1, n + 1) as i:
        body(2 * i + 1, 1, i)
        body(2 * i + 2, 0, i + 1)
    for b in range(2 * n + 3, B + behind):
        body(b, b % 2, b // 2)


def decoder_kernel(nc, T, out):
    ctx = ExitStack()
    with ctx:
        def sb(name, shape, dt=F32):
            return ctx.enter_context(nc.sbuf_tensor(name, shape, dt))

        def sems(prefix, names):
            return {n: Counter(ctx.enter_context(nc.semaphore(f"{prefix}_{n}")), 0) for n in names.split()}

        banks = ctx.enter_context(nc.psum_tensor("banks", [P, 8, 512], F32))
        pb = [banks[:, i, :] for i in range(8)]

        cst = sb("cst", [P, C_END])
        ident = cst[:, C_ID:C_ID + P]
        X = sb("X", [S, B * D])
        Y_room = sb("Y_room", [P, B * D])
        Y = Y_room[0:S, :]
        kcol = sb("kcol", [S, 5, 32])
        stats = sb("stats", [S, 6])
        mv = sb("mv", [S, 2])
        rstd = sb("rstd", [S, 8])
        minus_one = sb("minus_one", [P, 1])
        ident_b = sb("ident_b", [S, S], BF16)
        masks_b = sb("masks_b", [S, 2, 4 * S], BF16)

        def xb_(b, lo=0, hi=D):
            return X[:, bass.ds(b * D + lo, hi - lo)]

        def yb_(b, lo=0, hi=D):
            return Y[:, bass.ds(b * D + lo, hi - lo)]

        def overlay(*parts):
            with ExitStack() as lent:
                return [lent.enter_context(nc.sbuf_tensor(*p)) for p in parts]

        _, b_cp1 = overlay(("room_fp32", [P, 8 * SC], F32), ("b_cp1", [STACK, H * SCP], F32R))
        room = sb("room", [P, 4 * 2048 + 1024 + D])
        wq0, wk0, wv0 = (room[:, i * 2048:(i + 1) * 2048].rearrange("p (k n) -> p k n", k=KT) for i in range(3))
        wo0 = room[:, 3 * 2048:4 * 2048].rearrange("p (k n) -> p k n", k=LW // P)
        bv0 = room[0:S, 8192:8192 + LW]
        bo0 = room[0:S, 8192 + LW:8192 + LW + D]
        bqk0 = sb("bqk0", [P, 16])
        wx0 = sb("wx0", [P, KT, D])
        wqk1, wv1, wo1 = sb("wqk1", [P, KT, 2 * D]), sb("wv1", [P, KT, D]), sb("wo1", [P, KT, DO])
        n12 = sb("n12", [P, 4])
        qkn = sb("qkn", [P, 2])
        gate = sb("gate", [P, KT, 4])
        up0, dn0 = sb("up0", [P, KT, HID]), sb("dn0", [P, FT, DO])
        g1, u1, dn1 = sb("g1", [P, KT, HID]), sb("u1", [P, KT, HID]), sb("dn1", [P, FT, DO])
        l1, l2, l3, dn2 = sb("l1", [P, KT, HID]), sb("l2", [P, FT, HID]), sb("l3", [P, FT, HID]), sb("dn2", [P, FT, DO])
        d3, up3, dn3 = sb("d3", [P, KT, D]), sb("up3", [P, KT, HID]), sb("dn3", [P, FT, DO])
        wdd = sb("wdd", [P, KT, P])
        wuqk, wuv = sb("wuqk", [P, 2, D]), sb("wuv", [P, D])
        wo4, wq5, wk5, wv5, wo5 = (Y_room[:, i * 512:(i + 1) * 512].rearrange("p (k n) -> p k n", k=KT) for i in range(5))
        b5 = Y_room[0:S, 2560:3584].rearrange("p (i n) -> p i n", i=4)
        packed = sb("packed", [P, KT, 64], I32)
        enc = sb("enc", [P, KT, 64], I32)
        tern = sb("tern", [P, KT, D], BF16)
        wscale = sb("wscale", [S, 1])
        b6 = sb("b6", [S, D])
        mask_i = sb("mask_i", [B, SC], I32)
        mask_f = sb("mask_f", [B, SC])

        _, b_qs0, b_qs1, _, b_cp0 = overlay(("area_fp32", [P, B_WORK], F32), ("b_qs0", [STACK, H * S], F32R),
                                            ("b_qs1", [STACK, H * S], F32R),
                                            ("area_gap", [P, B_OWN - B_WORK - 2 * H * S], F32),
                                            ("b_cp0", [STACK, H * SCP], F32R))
        area = sb("area", [P, AREA])
        top = [0]

        def take(parts, n, pattern=None, **dims):
            a = area[0:parts, top[0]:top[0] + n]
            top[0] += n
            assert top[0] <= AREA
            return a.rearrange(pattern, **dims) if pattern else a

        parts_scratch = nc.dram_tensor("parts_scratch", (2, B, D, SC), F32, kind="Internal").ap()
        mask_scratch = nc.dram_tensor("mask_scratch", (B, SC), F32, kind="Internal").ap()

        ld = sems("ld", "x cst bias a0 a1 a2 a3 bo wx mask c1 c2 gate e0 e1 e2 e3 d4 e5 b5 f6 pk")
        pre = sems("pre", "masks bias1 pad zero scale m1 av rowbias scratch tern enc kn bx b6 cv raw0 raw1 hi lo parts")

        A = sems("A", "mv pc xn xb xt xte pg pj ex ph sg sm nd chain den nm ot oe wd xu")
        Bs = sems("B", "qh ql xq qs ue ut sg nb ex tp ted tea pv den nm ot oe cp0 cp1 cv0 cv1")
        for n in "mv xn chain wd xu".split():
            Bs[n] = Counter(A[n].sem, B)
        Bs["pc"] = Counter(A["pc"].sem, 2 * B)
        core1 = "mv xn xt xte v ve t7 qe kb pv chain den nm ot oe wd xu"
        core4 = "sg nb ex tp"
        Cs = sems("C", "y pc qk sq ss rc r qkn ted tea " + core1 + " " + core4)
        Ds = sems("D", "pc c ce")
        Es = sems("E", "xb z rope k0 k1")
        for s, n in ((Ds, 1), (Es, 2)):
            for names, per in ((core1, 1), (core4, 4), ("ted tea", 2)):
                for name in names.split():
                    s[name] = Counter(Cs[name].sem, n * per * B)
        for name in ("qk", "qkn"):
            Es[name] = Counter(Cs[name].sem, B)
        Es["pc"] = Counter(Ds["pc"].sem, 2 * B)
        G = sems("G", "sq pc xf xt xte lg le cp xy chain wt")
        M = sems("M", "up ev h1 t dn acc")
        Fs = sems("F", "am qz mm st")
        for n in "mv xn chain xu".split():
            Fs[n] = Counter(A[n].sem, 2 * B)
        for n in ("xb", "xt", "xte"):
            Fs[n] = Counter(A[n].sem, B)
        Fs["pc"] = Counter(A["pc"].sem, 4 * B)

        block = ctx.enter_context(nc.Block())

        def ln_stats(s, b, unused):
            nc.vector.wait_ge(s["xn"].sem, s["xn"].at(b))
            nc.vector.bn_stats(stats[:, :], xb_(b)).then_inc(s["chain"].sem, 1)

        def ln_rstd(s, b, n_pc):
            nc.gpsimd.wait_ge(s["mv"].sem, s["mv"].at(b + 1))
            nc.gpsimd.tensor_tensor(rstd[:, 0:1], mv[:, 1:2], kcol[:, 1, 0:1], ALU.add).then_inc(s["pc"].sem, 1)
            nc.gpsimd.wait_ge(s["pc"].sem, s["pc"].at(b * n_pc + 1))
            nc.gpsimd.tensor_tensor(rstd[:, 1:2], rstd[:, 0:1], kcol[:, 0, 0:1], ALU.pow).then_inc(s["pc"].sem, 1)

        def ln_apply(s, b, dst, n_pc, src_free):
            nc.vector.wait_ge(s["pc"].sem, s["pc"].at(b * n_pc + 2))
            if src_free is not None:
                nc.vector.wait_ge(src_free[0].sem, src_free[0].at(src_free[1]))
            return nc.vector.tensor_scalar(dst, xb_(b), mv[:, 0:1], rstd[:, 1:2], ALU.subtract, ALU.mult)

        def twice(a):
            return a.rearrange("s (h e) -> s h e", h=H).unsqueeze(2).to_broadcast([S, H, 2, HD])

        def parts_of(a, c):
            return a[:, :, c * HD:(c + 2) * HD].rearrange("s h (c e) -> s h c e", c=2)

        def transposes(src, parts, n, dst):
            for k in range(n):
                last = nc.tensor.transpose(dst[:, k * parts:(k + 1) * parts], src[:, k * P:(k + 1) * P],
                                           ident[0:parts, 0:parts])
            return last

        def products(dst, lhs, rhs):
            for k, (a, w) in enumerate(zip(lhs, rhs)):
                last = nc.tensor.matmul(dst, a, w, start=(k == 0), stop=(k == len(lhs) - 1))
            return last

        top[0] = 0
        a_xn = take(S, D)
        a_xnT = take(P, KT * S, "p (k s) -> p k s", k=KT)
        a_q, a_k = take(P, 8 * S), take(P, 8 * S)
        a_z, a_e = take(P, 2 * 4 * S, "p (g n) -> p g n", g=2), take(P, 2 * 4 * S, "p (g n) -> p g n", g=2)
        a_v = take(S, H * (LD + 1), "p (h e) -> p h e", h=H)
        a_at = take(S, H * S)
        a_o = take(S, LW)
        a_oT = take(P, 8 * S)
        a_den = take(S, 32)
        assert top[0] <= B_OWN
        NUM = [(0, 6), (6, 12), (12, 16)]

        top[0] = 0
        b_x = take(S, D)
        b_xs = take(S, H * STACK, "p (h c) -> p h c", h=H)
        b_qs = [b_qs0[:, :], b_qs1[:, :]]
        b_pT = take(KC, 4 * NKC * S, "p (g n) -> p g n", g=4)
        b_nb = take(S, H)
        b_rc = take(S, H)
        b_u = take(P, 4 * S)
        b_o = take(S, D)
        b_oT = take(P, KT * S)
        assert top[0] <= B_WORK
        top[0] = B_OWN + H * SCP
        b_cp = [t[:, :].rearrange("p (h s) -> p h s", h=H) for t in (b_cp0, b_cp1)]
        b_p = room[0:S, 0:4 * 2 * SC].rearrange("p (g h s) -> p g h s", g=4, h=2)
        b_cv = [take(KC, NKC * H * 17, "p (c h e) -> p c h e", c=NKC, h=H),
                Y_room[0:KC, 4 * 2 * SC:4 * 2 * SC + NKC * H * 17].rearrange("p (c h e) -> p c h e", c=NKC, h=H)]
        s_raw = [Y_room[:, i * 2 * SC:(i + 1) * 2 * SC].rearrange("p (k s) -> p k s", k=KT) for i in range(2)]
        s_high, s_low = (Y_room[:, i * 2 * SC:(i + 1) * 2 * SC].rearrange("p (k s) -> p k s", k=KT) for i in (2, 3))

        top[0] = 0
        c_h = take(S, D)
        c_xnT = [take(P, KT * S, "p (k s) -> p k s", k=KT) for _ in range(2)]
        c_sq = take(S, 2 * D)
        c_t2, c_z = take(S, 2 * D), take(S, 2 * D)
        c_qk = take(S, 2 * D)
        c_ss, c_r = take(S, 32), take(S, 32)
        c_qT = [take(P, KT * S, "p (k s) -> p k s", k=KT) for _ in range(2)]
        c_kT = take(P, KT * S, "p (k s) -> p k s", k=KT)
        c_kbd = [take(P, KT * 8 * S, "p (k j s) -> p k j s", k=KT, j=8) for _ in range(2)]
        c_v = [take(S, H * 17, "p (h e) -> p h e", h=H) for _ in range(2)]
        c_p, c_pT = (take(S, H * S) for _ in range(2))
        c_nb, c_rc = take(S, H), take(S, H)
        c_o = take(S, D)
        c_oT = take(P, KT * S, "p (k s) -> p k s", k=KT)
        c_cT = [take(P, S) for _ in range(2)]
        knbm, qn4 = take(P, 8), take(P, 1)
        e_ctx = [c_h_ for c_h_ in (room[:, i * KT * S:(i + 1) * KT * S].rearrange("p (k s) -> p k s", k=KT) for i in range(2))]

        top[0] = 0
        m_xfT = take(P, KT * B * S, "p (k n) -> p k n", k=KT)
        g_sq = take(S, D)
        g_xf = take(S, D)
        g_ms = take(S, 8)
        g_cols = take(P, KT * S, "p (k s) -> p k s", k=KT)
        g_lg = take(S, B * 4)
        g_a, g_b2, g_w = take(S, B * 4), take(S, B * 4), take(S, B * 4)
        g_red, g_red2 = take(S, B), take(S, B)
        g_cmp, g_cmp2 = take(S, B * 16), take(S, B * 16)
        m_g, m_s, m_u, m_t = (take(P, 2 * QN, "p (g n) -> p g n", g=2) for _ in range(4))
        m_h0, m_h1, m_ha, m_hb = (room[:, i * FT * QN:(i + 1) * FT * QN].rearrange("p (k n) -> p k n", k=FT) for i in range(4))
        m_hc = room[:, 4 * FT * QN:4 * FT * QN + KT * QN].rearrange("p (k n) -> p k n", k=KT)
        m_hd = take(P, FT * QN, "p (k n) -> p k n", k=FT)

        top[0] = 0
        f_xn = take(S, D)
        f_am, f_sc = take(S, 4), take(S, 4)
        f_q = take(S, D)
        f_xT = area[:, top[0]:top[0] + S].bitcast(BF16).rearrange("p (k s) -> p k s", k=KT)

        def wload(eng, dst, name, sem):
            src = T[name].rearrange("(k p) n -> p k n", p=P)
            eng.dma_start(dst, src).then_inc(sem.sem, 16)

        def bcast(eng, dst, name, sem, parts=S):
            eng.dma_start(dst, T[name].partition_broadcast(parts)).then_inc(sem.sem, 16)

        @block.sync
        def _(sp):
            sp.dma_start(cst[:, :], T["consts"]).then_inc(ld["cst"].sem, 16)
            sp.dma_start(X[:, :].rearrange("s (b d) -> s b d", b=B), T["x"].rearrange("b s d -> s b d")).then_inc(ld["x"].sem, 16)
            sp.dma_start(bqk0[:, 0:8], T["bq"]).then_inc(ld["bias"].sem, 16)
            sp.dma_start(bqk0[:, 8:16], T["bk"]).then_inc(ld["bias"].sem, 16)
            wload(sp, wq0, "Wq", ld["a0"])
            wload(sp, wk0, "Wk", ld["a1"])
            bcast(sp, bv0, "bv", ld["a2"])
            wload(sp, wv0, "Wv", ld["a2"])
            wload(sp, wo0, "Wo", ld["a3"])
            bcast(sp, bo0, "bo", ld["bo"])
            sp.dma_start(mask_i[:, :], T["mask"]).then_inc(ld["mask"].sem, 16)
            wload(sp, wx0[:, :, :], "W_out", ld["wx"])
            sp.dma_start(s_raw[0], T["ctxT"][0].rearrange("(k p) s -> p k s", p=P)).then_inc(pre["raw0"].sem, 16)
            sp.wait_ge(pre["rowbias"].sem, 1)
            sp.dma_start(mask_scratch, mask_f[:, :]).then_inc(pre["scratch"].sem, 16)
            wload(sp, wqk1[:, :, 0:D], "wq", ld["c1"])
            wload(sp, wqk1[:, :, D:2 * D], "wk", ld["c1"])
            wload(sp, wv1[:, :, :], "wv", ld["c1"])
            wload(sp, wo1[:, :, :], "wo", ld["c1"])
            sp.dma_start(n12[:, :], T["n12"]).then_inc(ld["c2"].sem, 16)
            for i, n in enumerate(("qn", "kn")):
                for r in range(8):
                    sp.dma_start(qkn[HD * r:HD * r + HD, i:i + 1], T[n]).then_inc(ld["c2"].sem, 16)
            wload(sp, gate[:, :, :], "gate", ld["gate"])
            sp.wait_ge(pre["scratch"].sem, 16)

            def part_stores(b, u, half):
                if on(b + 1) and not (isinstance(b, int) and b < 0):
                    n = b + 1
                    sp.wait_ge(pre["lo"].sem, b)
                    src = T["ctxT"][bass.ds(n, 1)].rearrange("o (k p) s -> (o p) k s", p=P)
                    sp.dma_start(s_raw[1 - u], src).then_inc(pre[f"raw{1 - u}"].sem, 16)
                if on(b):
                    sp.wait_ge(pre["lo"].sem, b + 1)
                    for i, src in enumerate((s_high, s_low)):
                        dst = parts_scratch[i, bass.ds(b, 1)].rearrange("o (k p) s -> (o p) k s", p=P)
                        sp.dma_start(dst, src).then_inc(pre["parts"].sem, 16)

            batches(sp, part_stores, 1)
            sp.wait_ge(pre["parts"].sem, 32 * B)

            def ctx_loads(b, u, half):
                if not on(b):
                    return
                cv = Bs[f"cv{u}"]
                sp.wait_ge(pre["pad"].sem, 2)
                sp.wait_ge(Bs["pv"].sem, Bs["pv"].at(8 * (b - 1)))
                for c in range(NKC):
                    src = T["ctx"][bass.ds(b, 1), c * KC:(c + 1) * KC].rearrange("o p (h e) -> (o p) h e", h=H)
                    sp.dma_start(b_cv[u][:, c, :, 0:HD], src).then_inc(cv.sem, 16)

            batches(sp, ctx_loads, 1)
            for name, dst, sem in (("e0_up", up0, "e0"), ("e0_down", dn0, "e0"), ("l1", l1, "e2"),
                                   ("w1", g1, "e1"), ("w2", u1, "e1"), ("l2", l2, "e2"), ("e1_down", dn1, "e1"),
                                   ("e3_down", d3, "e3"), ("l3", l3, "e2"), ("e3_up", up3, "e3"),
                                   ("l4", dn2, "e2"), ("e3_out", dn3, "e3")):
                wload(sp, dst[:, :, :], name, ld[sem])
            sp.wait_ge(pre["pad"].sem, 3)
            wload(sp, wdd[:, :, 0:64], "W_dq", ld["d4"])
            wload(sp, wdd[:, :, 64:128], "W_dkv", ld["d4"])
            sp.dma_start(wuqk[0:64, 0, :], T["W_uq"]).then_inc(ld["d4"].sem, 16)
            sp.dma_start(wuqk[64:128, 1, :], T["W_uk"]).then_inc(ld["d4"].sem, 16)
            sp.dma_start(wuv[64:128, :], T["W_uv"]).then_inc(ld["d4"].sem, 16)
            sp.wait_ge(G["xy"].sem, G["xy"].at(B))
            wload(sp, wo4, "W_o", ld["d4"])
            for name, dst in (("q_w", wq5), ("k_w", wk5), ("v_w", wv5), ("o_w", wo5)):
                wload(sp, dst, name, ld["e5"])
            for i, name in enumerate(("q_b", "k_b", "v_b", "o_b")):
                bcast(sp, b5[:, i, :], name, ld["b5"])
            sp.dma_start(packed[:, :, :], T["packed"].rearrange("(k p) o -> p k o", p=P)).then_inc(ld["pk"].sem, 16)
            bcast(sp, wscale[:, :], "wscale", ld["f6"])
            bcast(sp, b6[:, :], "bias", ld["f6"])

            def window_loads(b, u, half):
                if not on(b):
                    return
                sp.wait_ge(M["acc"].sem, M["acc"].at(64))
                sp.wait_ge(Es["v"].sem, Es["v"].at(b - 1))
                src = T["ctxT"][bass.ds(b, 1), :, 0:S].rearrange("o (k p) s -> (o p) k s", p=P)
                sp.dma_start(e_ctx[u], src).then_inc(Es[f"k{u}"].sem, 16)

            batches(sp, window_loads, 1)

            def stores(b, u, half):
                if not on(b):
                    return
                sp.wait_ge(Fs["xu"].sem, Fs["xu"].at(b + 1))
                sp.dma_start(out[bass.ds(b, 1)].rearrange("o s d -> (o s) d"), xb_(b)).then_inc(Fs["st"].sem, 16)

            batches(sp, stores, 1)
            sp.wait_ge(Fs["st"].sem, Fs["st"].at(16 * B))

        @block.tensor
        def _(pe):
            T3 = nc.tensor

            def phase_a(b, u, half):
                if on(b):
                    pe.wait_ge(A["xte"].sem, A["xte"].at(b + 1))
                    for g in range(4):
                        pe.wait_ge(A["pj"].sem, A["pj"].at(6 * b + g - 1))
                        if isinstance(b, int) and b == 0:
                            pe.wait_ge(ld["a0" if g < 2 else "a1"].sem, 16)
                        w = wq0 if g < 2 else wk0
                        for t in range(4):
                            m = 4 * (g % 2) + t
                            last = products(pb[g % 2][:, t * S:(t + 1) * S],
                                            [w[:, k, m * P:(m + 1) * P] for k in range(KT)],
                                            [a_xnT[:, k, :] for k in range(KT)])
                        last.then_inc(A["pg"].sem, 1)
                    for g in range(2):
                        pe.wait_ge(A["pj"].sem, A["pj"].at(6 * b + 3 + g))
                        if isinstance(b, int) and b == 0:
                            pe.wait_ge(ld["a2"].sem, 32)
                        products(pb[g][0:S, :], [a_xnT[:, k, :] for k in range(KT)],
                                 [wv0[:, k, g * 512:(g + 1) * 512] for k in range(KT)]).then_inc(A["pg"].sem, 1)
                if on(b - 1):
                    pe.wait_ge(A["nm"].sem, A["nm"].at(3 * b))
                    for g in range(2):
                        transposes(a_o[:, g * 512:(g + 1) * 512], S, 4, pb[2 + g]).then_inc(A["ot"].sem, 1)
                if on(b):
                    for x in range(2):
                        pe.wait_ge(A["ph"].sem, A["ph"].at(4 * b + 3 + x))
                        pe.wait_ge(A["oe"].sem, A["oe"].at(2 * b))
                        pe.wait_ge(A["sm"].sem, A["sm"].at(4 * b + 2 * x))
                        for j in range(4):
                            m = 4 * x + j
                            for e in range(2):
                                r = LD * e
                                last = T3.matmul(pb[2 + e][0:S, j * S:(j + 1) * S], a_k[r:r + LD, m * S:(m + 1) * S],
                                                 a_q[r:r + LD, m * S:(m + 1) * S], start=True, stop=True)
                                if j == 3:
                                    last.then_inc(A["sg"].sem, 1)
                if on(b - 1):
                    pe.wait_ge(A["oe"].sem, A["oe"].at(2 * b))
                    pe.wait_ge(A["xte"].sem, A["xte"].at(least(b + 1, B)))
                    if isinstance(b, int) and b == 1:
                        pe.wait_ge(ld["a3"].sem, 16)
                    products(pb[7][0:S, 0:D], [a_oT[:, m * S:(m + 1) * S] for m in range(8)],
                             [wo0[:, m, :] for m in range(8)]).then_inc(A["wd"].sem, 1)
                if on(b + 1):
                    pe.wait_ge(A["xn"].sem, A["xn"].at(b + 2))
                    pe.wait_ge(A["xu"].sem, A["xu"].at(b))
                    transposes(a_xn, S, KT, pb[7]).then_inc(A["xt"].sem, 1)
                if on(b):
                    pe.wait_ge(A["nm"].sem, A["nm"].at(3 * b))
                    pe.wait_ge(A["pj"].sem, A["pj"].at(6 * b + 6))
                    for h in range(H):
                        if h % 8 == 0:
                            pe.wait_ge(A["sm"].sem, A["sm"].at(4 * b + h // 4 + 2))
                        n = h // 6
                        o = (h - NUM[n][0]) * (LD + 1)
                        last = T3.matmul(pb[4 + n][0:S, o:o + LD + 1], a_at[:, h * S:(h + 1) * S], a_v[:, h, :],
                                         start=True, stop=True)
                        if h + 1 == NUM[n][1]:
                            last.then_inc(A["nd"].sem, 1)

            pe.wait_ge(ld["cst"].sem, 16)
            batches(pe, phase_a, 1)

            def phase_b(b, u, half):
                for p in range(8):
                    if on(b):
                        if p == 0:
                            pe.wait_ge(Bs[f"cp{u}"].sem, Bs[f"cp{u}"].at(16 * 5 * (half + 1)))
                        if p % 2 == 0:
                            pe.wait_ge(Bs["qs"].sem, Bs["qs"].at(4 * b + p // 2 + 1))
                        pe.wait_ge(Bs["ex"].sem, Bs["ex"].at(16 * b + 2 * p - 2))
                        for e in range(2):
                            h = 2 * p + e
                            last = T3.matmul(pb[2 * (p % 2) + e][0:S, 0:SCP],
                                             b_qs[u][:, h * S:(h + 1) * S], b_cp[u][:, h, :], start=True, stop=True)
                        last.then_inc(Bs["sg"].sem, 1)
                    bt, pt = (b, p - 2) if p > 1 else (b - 1, 6 + p)
                    if on(bt):
                        for e in range(2):
                            h = 2 * pt + e
                            pe.wait_ge(Bs["ex"].sem, Bs["ex"].at(16 * bt + h + 1))
                            pe.wait_ge(Bs["tea" if e else "ted"].sem, Bs["tea" if e else "ted"].at(8 * bt + pt))
                            for c in range(NKC):
                                last = T3.transpose(pb[4 + e][0:KC, c * S:(c + 1) * S],
                                                    b_p[:, pt % 4, e, c * KC:(c + 1) * KC], ident[0:S, 0:S])
                            last.then_inc(Bs["tp"].sem, 1)
                    bv, pv = (b, p - 3) if p > 2 else (b - 1, 5 + p)
                    if on(bv):
                        if pv == 0:
                            pe.wait_ge(Bs["ue"].sem, Bs["ue"].at(bv))
                            pe.wait_ge(Bs[f"cv{u}"].sem, Bs[f"cv{u}"].at(16 * 3 * (half + 1)))
                            if isinstance(b, int) and b == 0:
                                pe.wait_ge(pre["b6"].sem, 1)
                        uv = u if p > 2 else 1 - u
                        pe.wait_ge(Bs["ted"].sem, Bs["ted"].at(8 * bv + pv + 1))
                        pe.wait_ge(Bs["tea"].sem, Bs["tea"].at(8 * bv + pv + 1))
                        for c in range(NKC):
                            for e in range(2):
                                h = 2 * pv + e
                                r = 32 * (h % 4)
                                last = T3.matmul(pb[6][r:r + 17, (h // 4) * S:(h // 4 + 1) * S], b_cv[uv][:, c, h, :],
                                                 b_pT[:, h % 4, c * S:(c + 1) * S], start=(c == 0), stop=(c == NKC - 1),
                                                 tile_position=(0, r))
                        last.then_inc(Bs["pv"].sem, 1)
                    if p == 3 and on(b - 1):
                        pe.wait_ge(Bs["ue"].sem, Bs["ue"].at(b))
                        pe.wait_ge(Bs["qs"].sem, Bs["qs"].at(4 * least(b + 1, B)))
                        for t in range(4):
                            last = T3.transpose(pb[7][0:S, t * P:(t + 1) * P], b_u[:, t * S:(t + 1) * S], ident)
                        last.then_inc(Bs["ut"].sem, 1)
                    if p == 4 and on(b - 1):
                        pe.wait_ge(Bs["nm"].sem, Bs["nm"].at(b))
                        transposes(b_o, S, KT, pb[7]).then_inc(Bs["ot"].sem, 1)
                    if p == 5 and on(b - 1):
                        pe.wait_ge(Bs["oe"].sem, Bs["oe"].at(b))
                        if isinstance(b, int) and b == 1:
                            pe.wait_ge(ld["wx"].sem, 16)
                        products(pb[7][0:S, 0:D], [b_oT[:, k * S:(k + 1) * S] for k in range(KT)],
                                 [wx0[:, k, :] for k in range(KT)]).then_inc(Bs["wd"].sem, 1)
                    if p < 2 and on(b):
                        stack(b, p + 2)
                    if p > 5 and on(b + 1):
                        if p == 6:
                            pe.wait_ge(Bs["ql"].sem, Bs["ql"].at(b + 2))
                            pe.wait_ge(Bs["xu"].sem, Bs["xu"].at(b))
                        stack(b + 1, p - 6)

            def stack(b, g):
                pe.wait_ge(Bs["qs"].sem, Bs["qs"].at(4 * b + g))
                for j in range(4):
                    last = T3.transpose(pb[7][0:STACK, j * S:(j + 1) * S], b_xs[:, 4 * g + j, :], ident[0:S, 0:S])
                last.then_inc(Bs["xq"].sem, 1)

            pe.wait_ge(A["xu"].sem, A["xu"].at(B))
            batches(pe, phase_b, 1)

            def attention(s, mask, project_qk, project_v, qk_read, to_columns, w_out, dst_out):
                def body(b, u, half):
                    if on(b - 2):
                        pe.wait_ge(s["oe"].sem, s["oe"].at(b - 1))
                        pe.wait_ge(s["ve"].sem, s["ve"].at(least(b + 1, B)))
                        products(pb[1][0:S, dst_out], [c_oT[:, m, :] for m in range(KT)],
                                 [w_out[:, m, :] for m in range(KT)]).then_inc(s["wd"].sem, 1)
                    for g in range(5):
                        if g < 4 and on(b):
                            if g == 0:
                                pe.wait_ge(s["kb"].sem, s["kb"].at(b + 1))
                            pe.wait_ge(s["ex"].sem, s["ex"].at(4 * b + g - 1))
                            k, j = g // 2, 4 * (g % 2)
                            T3.matmul(pb[2 + g % 2][0:S, 0:4 * S], c_qT[u][:, k, :],
                                      c_kbd[u][:, k, j:j + 4, :].rearrange("p j s -> p (j s)"),
                                      start=True, stop=False)
                            T3.matmul(pb[2 + g % 2][0:S, 0:4 * S], ident_b[:, :], mask,
                                      start=False, stop=True).then_inc(s["sg"].sem, 1)
                        if g < 4 and on(b - 1):
                            pe.wait_ge(s["ex"].sem, s["ex"].at(4 * b + g - 3))
                            if g % 2:
                                pe.wait_ge(s["tea"].sem, s["tea"].at(2 * b - 2 + g // 2))
                            else:
                                pe.wait_ge(s["ted"].sem, s["ted"].at(2 * b - 2 + g // 2))
                            for j in range(4):
                                h = 4 * g + j
                                last = T3.transpose(pb[4 + g % 2][0:S, j * S:(j + 1) * S],
                                                    c_p[:, h * S:(h + 1) * S], ident[0:S, 0:S])
                            last.then_inc(s["tp"].sem, 1)
                        if g > 0 and on(b - 1):
                            v = g - 1
                            if v == 0:
                                pe.wait_ge(s["oe"].sem, s["oe"].at(b - 1))
                            if v % 2:
                                pe.wait_ge(s["tea"].sem, s["tea"].at(2 * b - 1 + v // 2))
                            else:
                                pe.wait_ge(s["ted"].sem, s["ted"].at(2 * b - 1 + v // 2))
                            for j in range(4):
                                h = 4 * v + j
                                last = T3.matmul(pb[6][0:S, h * 17:(h + 1) * 17], c_pT[:, h * S:(h + 1) * S],
                                                 c_v[1 - u][:, h, :], start=True, stop=True)
                            if v == 3:
                                last.then_inc(s["pv"].sem, 1)
                        if g == 1 and on(b + 2):
                            pe.wait_ge(s["xn"].sem, s["xn"].at(b + 3))
                            pe.wait_ge(s["ve"].sem, s["ve"].at(b + 1))
                            pe.wait_ge(s["xu"].sem, s["xu"].at(b - 1))
                            transposes(c_h, S, KT, pb[1]).then_inc(s["xt"].sem, 1)
                        if g == 2 and on(b + 1):
                            to_columns(b + 1, 1 - u)
                        if g == 3 and on(b + 2):
                            pe.wait_ge(qk_read.sem, qk_read.at(b + 2))
                            pe.wait_ge(s["xte"].sem, s["xte"].at(b + 3))
                            project_qk(b + 2, u, half + 1)
                    if on(b + 1):
                        pe.wait_ge(s["ve"].sem, s["ve"].at(b + 1))
                        pe.wait_ge(s["xu"].sem, s["xu"].at(b - 1))
                        pe.wait_ge(s["xte"].sem, s["xte"].at(least(b + 3, B)))
                        project_v(b + 1, 1 - u)
                    if on(b - 1):
                        pe.wait_ge(s["nm"].sem, s["nm"].at(b))
                        transposes(c_o, S, KT, pb[6]).then_inc(s["ot"].sem, 1)
                batches(pe, body, 3, 2)

            def c_qk_(b, u, half):
                products(pb[0][0:S, :], [c_xnT[u][:, k, :] for k in range(KT)],
                         [wqk1[:, k, :] for k in range(KT)]).then_inc(Cs["qk"].sem, 1)

            def c_v_(b, u):
                products(pb[1][0:S, 0:D], [c_xnT[u][:, k, :] for k in range(KT)],
                         [wv1[:, k, :] for k in range(KT)]).then_inc(Cs["v"].sem, 1)

            def columns_of(s):
                def f(b, u):
                    pe.wait_ge(s["qkn"].sem, s["qkn"].at(b + 1))
                    pe.wait_ge(s["qe"].sem, s["qe"].at(b))
                    transposes(c_qk, S, 4, pb[7]).then_inc(s["t7"].sem, 1)
                return f

            pe.wait_ge(Bs["xu"].sem, Bs["xu"].at(B))
            pe.wait_ge(ld["c1"].sem, 64)
            pe.wait_ge(pre["masks"].sem, 1)
            attention(Cs, masks_b[:, 0, :], c_qk_, c_v_, Cs["qkn"], columns_of(Cs), wo1, slice(0, DO))

            def phase_g(b, u, half):
                if on(b):
                    pe.wait_ge(G["xf"].sem, G["xf"].at(b + 1))
                    pe.wait_ge(G["xte"].sem, G["xte"].at(b))
                    transposes(g_xf, S, KT, pb[0]).then_inc(G["xt"].sem, 1)
                    pe.wait_ge(G["xte"].sem, G["xte"].at(b + 1))
                    pe.wait_ge(G["le"].sem, G["le"].at(b))
                    for k in range(KT):
                        last = T3.matmul(pb[1][0:S, 0:4], g_cols[:, k, :], gate[:, k, :], start=(k == 0), stop=(k == KT - 1))
                    last.then_inc(G["lg"].sem, 1)

            pe.wait_ge(Cs["xu"].sem, Cs["xu"].at(B))
            pe.wait_ge(ld["gate"].sem, 16)
            batches(pe, phase_g, 1)

            def phase_m(i, first):
                use = [0]

                def up(w, m, src, kn, ready):
                    n = use[0]
                    use[0] += 1
                    for sem, v in ready:
                        pe.wait_ge(sem.sem, sem.at(v))
                    if not first or n >= 4:
                        pe.wait_ge(M["ev"].sem, M["ev"].at(UPS * i + (n - 3 if n >= 4 else (-1, 0, -3, -2)[n])))
                    products(pb[n % 4][:, 0:QN], [w[:, k, m * P:(m + 1) * P] for k in range(kn)],
                             [src(k) for k in range(kn)]).then_inc(M["up"].sem, 1)

                def xf(k):
                    return m_xfT[:, k, bass.ds(i * QN, QN)]

                def down(w, hsrc, e, ready):
                    for sem, v in ready:
                        pe.wait_ge(sem.sem, sem.at(v))
                    for j in range(QUAD):
                        n = e * QUAD + j
                        if not first or n >= 4:
                            pe.wait_ge(M["acc"].sem, M["acc"].at(16 * i + n - 3))
                        products(pb[4 + j][0:S, 0:DO], [hsrc[:, k, j * S:(j + 1) * S] for k in range(FT)],
                                 [w[:, k, :] for k in range(FT)]).then_inc(M["dn"].sem, 1)

                for m in range(FT):
                    up(up0, m, xf, KT, [])
                for m in range(FT):
                    up(l1, m, xf, KT, [])
                for m in range(FT):
                    up(g1, m, xf, KT, [])
                    up(u1, m, xf, KT, [])
                for m in range(FT):
                    up(l2, m, lambda k: m_ha[:, k, :], FT, [(M["ev"], UPS * i + 8)])
                down(dn0, m_h0, 0, [(M["ev"], UPS * i + 4)])
                for m in range(KT):
                    up(d3, m, xf, KT, [])
                for m in range(FT):
                    up(l3, m, lambda k: m_hb[:, k, :], FT, [(M["ev"], UPS * i + 20)])
                for m in range(FT):
                    up(up3, m, lambda k: m_hc[:, k, :], KT, [(M["ev"], UPS * i + 22)])
                down(dn1, m_h1, 1, [(M["h1"], 4 * i + 4)])
                down(dn2, m_ha, 2, [(M["ev"], UPS * i + 26)])
                down(dn3, m_hd, 3, [(M["ev"], UPS * i + 30)])

            for sem, n in (("e0", 2), ("e1", 3), ("e2", 4), ("e3", 3)):
                pe.wait_ge(ld[sem].sem, ld[sem].at(16 * n))
            pe.wait_ge(G["le"].sem, G["le"].at(B))
            pe.wait_ge(G["cp"].sem, G["cp"].at(B))
            phase_m(0, True)
            with pe.Fori(1, B // QUAD) as i:
                phase_m(i, False)

            def d_qk_(b, u, half):
                products(pb[0][:, 0:S], [wdd[:, k, :] for k in range(KT)],
                         [c_xnT[u][:, k, :] for k in range(KT)]).then_inc(Ds["c"].sem, 1)

            def d_v_(b, u):
                products(pb[1][0:S, 0:D], [c_cT[u]], [wuv[:, :]]).then_inc(Ds["v"].sem, 1)

            def d_columns(b, u):
                pe.wait_ge(Ds["ce"].sem, Ds["ce"].at(b + 1))
                pe.wait_ge(Ds["qe"].sem, Ds["qe"].at(b))
                for n in range(4):
                    last = T3.matmul(pb[7][:, n * S:(n + 1) * S], wuqk[:, n // 2, (n % 2) * P:(n % 2 + 1) * P],
                                     c_cT[u],
                                     start=True, stop=True)
                last.then_inc(Ds["t7"].sem, 1)

            pe.wait_ge(M["acc"].sem, M["acc"].at(64))
            pe.wait_ge(ld["d4"].sem, 96)
            attention(Ds, masks_b[:, 0, :], d_qk_, d_v_, Ds["ce"], d_columns, wo4, slice(0, D))

            def e_qk_(b, u, half):
                pe.wait_ge(Es[f"k{u}"].sem, Es[f"k{u}"].at(16 * (half + 1)))
                products(pb[0][0:S, 0:D], [c_xnT[u][:, k, :] for k in range(KT)], [wq5[:, k, :] for k in range(KT)])
                products(pb[0][0:S, D:2 * D], [e_ctx[u][:, k, :] for k in range(KT)],
                         [wk5[:, k, :] for k in range(KT)]).then_inc(Es["qk"].sem, 1)

            def e_v_(b, u):
                products(pb[1][0:S, 0:D], [e_ctx[u][:, k, :] for k in range(KT)],
                         [wv5[:, k, :] for k in range(KT)]).then_inc(Es["v"].sem, 1)

            pe.wait_ge(Ds["xu"].sem, Ds["xu"].at(B))
            pe.wait_ge(ld["e5"].sem, 64)
            attention(Es, masks_b[:, 1, :], e_qk_, e_v_, Es["z"], columns_of(Es), wo5, slice(0, D))

            def phase_f(b, u, half):
                if on(b):
                    pe.wait_ge(Fs["qz"].sem, Fs["qz"].at(b + 1))
                    pe.wait_ge(Fs["xte"].sem, Fs["xte"].at(b))
                    transposes(f_q, S, KT, pb[u]).then_inc(Fs["xt"].sem, 1)
                    pe.wait_ge(Fs["xte"].sem, Fs["xte"].at(b + 1))
                    pe.wait_ge(Fs["xu"].sem, Fs["xu"].at(b - 1))
                    products(pb[2 + u][0:S, 0:D], [f_xT[:, k, :] for k in range(KT)],
                             [tern[:, k, :] for k in range(KT)]).then_inc(Fs["mm"].sem, 1)

            pe.wait_ge(Es["xu"].sem, Es["xu"].at(B))
            pe.wait_ge(pre["tern"].sem, 4)
            batches(pe, phase_f, 1)

        @block.gpsimd
        def _(pool):
            g_ = nc.gpsimd
            for i, v in enumerate((-0.5, 1e-5, RMS_EPS, 1.0 / HD, 1.0 / D)):
                g_.memset(kcol[:, i, :], v).then_inc(pre["scale"].sem, 1)
            for u in range(2):
                last = g_.memset(b_cv[u][:, :, :, HD:HD + 1], 1.0)
            last.then_inc(pre["pad"].sem, 1)
            pool.wait_ge(pre["scale"].sem, 5)

            def even_out(u):
                return g_.tensor_copy(b_cp[u][:, :, SC:SCP], kcol[0:STACK, 0, 0:H].unsqueeze(2))

            even_out(0).then_inc(pre["pad"].sem, 1)
            g_.memset(wuqk[:, :, :], 0.0).then_inc(pre["pad"].sem, 1)
            pool.wait_ge(pre["pad"].sem, 3)
            g_.memset(wuv[:, :], 0.0).then_inc(pre["pad"].sem, 1)

            def stacked_context(b, u):
                for c in range(4):
                    src = parts_scratch[c % 2, bass.ds(b, 1)].rearrange("o (h r) s -> (o r) h s", r=HD)
                    g_.dma_start(b_cp[u][HD * c:HD * c + HD, :, 0:SC], src).then_inc(Bs[f"cp{u}"].sem, 16)
                src = mask_scratch[bass.ds(b, 1)].unsqueeze(1).to_broadcast([1, H, SC])
                g_.dma_start(b_cp[u][4 * HD:STACK, :, 0:SC], src).then_inc(Bs[f"cp{u}"].sem, 16)

            def phase_a(b, u, half):
                if on(b + 1):
                    ln_rstd(A, b + 1, 2)
                    pool.wait_ge(A["xn"].sem, A["xn"].at(b + 2))
                    pool.wait_ge(ld["bo"].sem, 16)
                    g_.tensor_tensor(xb_(b + 1), xb_(b + 1), bo0, ALU.add).then_inc(A["xb"].sem, 1)
                if isinstance(b, int) and b == 2:
                    pool.wait_ge(pre["parts"].sem, 32)
                    stacked_context(0, 0)
                if on(b - 1):
                    pool.wait_ge(pre["hi"].sem, b)
                    g_.tensor_tensor(s_low, s_raw[1 - u], s_high, ALU.subtract).then_inc(pre["lo"].sem, 1)

            batches(pool, phase_a, 1)

            def phase_b(b, u, half):
                if on(b + 1) and not (isinstance(b, int) and b < 0):
                    pool.wait_ge(Bs["sg"].sem, Bs["sg"].at(8 * b))
                    stacked_context(b + 1, 1 - u)
                if on(b + 1):
                    ln_rstd(Bs, b + 1, 2)
                    pool.wait_ge(Bs["qh"].sem, Bs["qh"].at(b + 2))
                    g_.tensor_tensor(parts_of(b_xs, 2), twice(b_x), parts_of(b_xs, 0), ALU.subtract).then_inc(Bs["ql"].sem, 1)

            pool.wait_ge(A["xu"].sem, A["xu"].at(B))
            pool.wait_ge(pre["parts"].sem, 32 * B)
            even_out(1).then_inc(pre["bx"].sem, 1)
            g_.memset(b_xs[:, :, 4 * HD:STACK], 1.0).then_inc(pre["bx"].sem, 1)
            batches(pool, phase_b, 1)

            def keys(s, b, v, kbm):
                pool.wait_ge(s["qe"].sem, s["qe"].at(b + 1))
                for k in range(KT):
                    last = g_.tensor_tensor(c_kbd[v][:, k, :, :], c_kT[:, k, :].unsqueeze(1).to_broadcast([P, 8, S]),
                                            kbm.unsqueeze(2).to_broadcast([P, 8, S]), ALU.mult)
                last.then_inc(s["kb"].sem, 1)

            def phase_c(b, u, half):
                if on(b + 3):
                    n = b + 3
                    ln_rstd(Cs, n, 6)
                    pool.wait_ge(Cs["pc"].sem, Cs["pc"].at(6 * n + 2))
                    g_.tensor_tensor(rstd[:, 2:3], rstd[:, 1:2], rstd[:, 1:2], ALU.mult).then_inc(Cs["pc"].sem, 1)
                    pool.wait_ge(Cs["pc"].sem, Cs["pc"].at(6 * n + 3))
                    g_.tensor_tensor(rstd[:, 3:4], rstd[:, 2:3], mv[:, 1:2], ALU.mult).then_inc(Cs["pc"].sem, 1)
                    pool.wait_ge(Cs["pc"].sem, Cs["pc"].at(6 * n + 4))
                    g_.tensor_tensor(rstd[:, 4:5], rstd[:, 3:4], kcol[:, 2, 0:1], ALU.add).then_inc(Cs["pc"].sem, 1)
                    pool.wait_ge(Cs["pc"].sem, Cs["pc"].at(6 * n + 5))
                    g_.tensor_tensor(rstd[:, 5:6], rstd[:, 4:5], kcol[:, 0, 0:1], ALU.pow).then_inc(Cs["pc"].sem, 1)
                if on(b + 1):
                    keys(Cs, b + 1, 1 - u, knbm)
                if on(b + 2):
                    n = b + 2
                    pool.wait_ge(Cs["ss"].sem, Cs["ss"].at(n + 1))
                    pool.wait_ge(Cs["qkn"].sem, Cs["qkn"].at(n))
                    g_.tensor_tensor(c_r, c_ss, kcol[:, 2, :], ALU.add).then_inc(Cs["rc"].sem, 1)
                    pool.wait_ge(Cs["rc"].sem, Cs["rc"].at(n + 1))
                    g_.tensor_tensor(c_r, c_r, kcol[:, 0, :], ALU.pow).then_inc(Cs["r"].sem, 1)

            pool.wait_ge(Bs["xu"].sem, Bs["xu"].at(B))
            g_.memset(c_v[0][:, :, HD:HD + 1], 1.0)
            g_.memset(c_v[1][:, :, HD:HD + 1], 1.0).then_inc(pre["cv"].sem, 1)
            pool.wait_ge(pre["cv"].sem, 1)
            pool.wait_ge(pre["kn"].sem, 1)
            batches(pool, phase_c, 3)

            def phase_g(b, u, half):
                if on(b):
                    pool.wait_ge(G["sq"].sem, G["sq"].at(b + 1))
                    g_.tensor_tensor(g_ms[:, 1:2], g_ms[:, 0:1], kcol[:, 4, 0:1], ALU.mult).then_inc(G["pc"].sem, 1)
                    pool.wait_ge(G["pc"].sem, G["pc"].at(3 * b + 1))
                    g_.tensor_tensor(g_ms[:, 2:3], g_ms[:, 1:2], kcol[:, 2, 0:1], ALU.add).then_inc(G["pc"].sem, 1)
                    pool.wait_ge(G["pc"].sem, G["pc"].at(3 * b + 2))
                    g_.tensor_tensor(g_ms[:, 3:4], g_ms[:, 2:3], kcol[:, 0, 0:1], ALU.pow).then_inc(G["pc"].sem, 1)
                    g_.tensor_tensor(xb_(b), xb_(b), yb_(b), ALU.add).then_inc(G["xy"].sem, 1)
                if on(b - 1):
                    pool.wait_ge(G["xte"].sem, G["xte"].at(b))
                    pool.wait_ge(ld["gate"].sem, 16)
                    g_.tensor_copy(m_xfT[:, :, bass.ds((b - 1) * S, S)], g_cols).then_inc(G["cp"].sem, 1)

            pool.wait_ge(Cs["xu"].sem, Cs["xu"].at(B))
            batches(pool, phase_g, 1)

            def normalise(s, bias):
                def body(b, u, half):
                    if on(b + 3):
                        n = b + 3
                        ln_rstd(s, n, 2)
                        if bias is not None:
                            pool.wait_ge(s["xn"].sem, s["xn"].at(n + 1))
                            pool.wait_ge(ld["b5"].sem, 64)
                            g_.tensor_tensor(xb_(n), xb_(n), bias, ALU.add).then_inc(s["xb"].sem, 1)
                    if on(b + 1):
                        keys(s, b + 1, 1 - u, cst[:, C_BM:C_BM + 8])
                    if bias is not None and on(b + 2):
                        n = b + 2
                        pool.wait_ge(s["rope"].sem, s["rope"].at(n + 1))
                        pool.wait_ge(s["t7"].sem, s["t7"].at(n))
                        g_.tensor_tensor(c_qk, c_sq, c_t2, ALU.add).then_inc(s["qkn"].sem, 1)
                return body

            pool.wait_ge(M["acc"].sem, M["acc"].at(64))
            g_.memset(c_v[0][:, :, HD:HD + 1], 1.0)
            g_.memset(c_v[1][:, :, HD:HD + 1], 1.0).then_inc(pre["cv"].sem, 1)
            pool.wait_ge(pre["cv"].sem, 2)
            batches(pool, normalise(Ds, None), 3)
            pool.wait_ge(Ds["xu"].sem, Ds["xu"].at(B))
            pool.wait_ge(ld["b5"].sem, 64)
            batches(pool, normalise(Es, b5[:, 3, :]), 3)

            def phase_f(b, u, half):
                if on(b + 1):
                    ln_rstd(Fs, b + 1, 2)
                    pool.wait_ge(Fs["xn"].sem, Fs["xn"].at(b + 2))
                    pool.wait_ge(ld["f6"].sem, 32)
                    g_.tensor_tensor(xb_(b + 1), xb_(b + 1), b6[:, :], ALU.add).then_inc(Fs["xb"].sem, 1)

            pool.wait_ge(Es["xu"].sem, Es["xu"].at(B))
            pool.wait_ge(ld["f6"].sem, 32)
            batches(pool, phase_f, 1)

        @block.scalar
        def _(act):
            a_ = nc.scalar

            def phase_a(b, u, half):
                if on(b):
                    for g in range(4):
                        act.wait_ge(A["pj"].sem, A["pj"].at(6 * b + g + 1))
                        act.wait_ge(A["ph"].sem, A["ph"].at(4 * b + g - 1))
                        a_.activation(a_e[:, g % 2, :], a_z[:, g % 2, :], ACT.Exp, bias=minus_one[:, :]).then_inc(A["ex"].sem, 1)
                if on(b - 1):
                    for g in range(2):
                        act.wait_ge(A["ot"].sem, A["ot"].at(2 * (b - 1) + g + 1))
                        a_.activation(a_oT[:, g * 4 * S:(g + 1) * 4 * S], pb[2 + g][:, 0:4 * S], ACT.Copy).then_inc(A["oe"].sem, 1)
                if on(b + 1):
                    act.wait_ge(A["xt"].sem, A["xt"].at(b + 2))
                    a_.activation(a_xnT.rearrange("p k s -> p (k s)"), pb[7][:, 0:KT * S], ACT.Copy).then_inc(A["xte"].sem, 1)

            act.wait_ge(pre["m1"].sem, 1)
            batches(act, phase_a, 1)

            def phase_b(b, u, half):
                for p in range(8):
                    if on(b):
                        for e in range(2):
                            h = 2 * p + e
                            act.wait_ge(Bs["nb"].sem, Bs["nb"].at(8 * b + p + 1))
                            act.wait_ge(Bs["tp"].sem, Bs["tp"].at(16 * b + 2 * p - 6))
                            a_.activation(b_p[:, p % 4, e, :], pb[2 * (p % 2) + e][0:S, 0:SC], ACT.Exp,
                                          bias=b_nb[:, h:h + 1]).then_inc(Bs["ex"].sem, 1)
                    bt, pt = (b, p - 2) if p > 1 else (b - 1, 6 + p)
                    if on(bt):
                        h = 2 * pt + 1
                        act.wait_ge(Bs["tp"].sem, Bs["tp"].at(16 * bt + h + 1))
                        a_.activation(b_pT[:, h % 4, :], pb[5][0:KC, 0:NKC * S], ACT.Copy).then_inc(Bs["tea"].sem, 1)
                    if p < 2 and on(b):
                        stack(b, p + 2, u)
                    if p > 5 and on(b + 1):
                        stack(b + 1, p - 6, 1 - u)
                    if p == 2 and on(b - 1):
                        act.wait_ge(Bs["pv"].sem, Bs["pv"].at(8 * b))
                        a_.activation(b_u, pb[6][:, 0:4 * S], ACT.Copy).then_inc(Bs["ue"].sem, 1)
                    if p == 4 and on(b - 1):
                        act.wait_ge(Bs["ot"].sem, Bs["ot"].at(b))
                        a_.activation(b_oT, pb[7][:, 0:KT * S], ACT.Copy).then_inc(Bs["oe"].sem, 1)

            def stack(b, g, u):
                act.wait_ge(Bs["xq"].sem, Bs["xq"].at(4 * b + g + 1))
                a_.activation(b_qs[u][:, g * 4 * S:(g + 1) * 4 * S], pb[7][0:STACK, 0:4 * S], ACT.Copy,
                              scale=D ** -0.5).then_inc(Bs["qs"].sem, 1)

            act.wait_ge(A["xu"].sem, A["xu"].at(B))
            batches(act, phase_b, 1)

            def attention(s, head, columns, xt_scale):
                def body(b, u, half):
                    for g in range(4):
                        if g % 2 and on(b - 1):
                            act.wait_ge(s["tp"].sem, s["tp"].at(4 * b + g - 3))
                            a_.activation(c_pT[:, g * 4 * S:(g + 1) * 4 * S], pb[5][0:S, 0:4 * S],
                                          ACT.Copy).then_inc(s["tea"].sem, 1)
                        if on(b):
                            act.wait_ge(s["nb"].sem, s["nb"].at(4 * b + g + 1))
                            act.wait_ge(s["tp"].sem, s["tp"].at(4 * b + g - 3))
                            for j in range(4):
                                h = 4 * g + j
                                last = a_.activation(c_p[:, h * S:(h + 1) * S], pb[2 + g % 2][0:S, j * S:(j + 1) * S], ACT.Exp,
                                                     bias=c_nb[:, h:h + 1])
                            last.then_inc(s["ex"].sem, 1)
                        if g == 1 and on(b + 2):
                            act.wait_ge(s["xt"].sem, s["xt"].at(b + 3))
                            act.wait_ge(s["v"].sem, s["v"].at(b + 1))
                            for k in range(KT):
                                f = xt_scale[:, k:k + 1] if xt_scale is not None else 1.0
                                last = a_.activation(c_xnT[u][:, k, :], pb[1][:, k * S:(k + 1) * S], ACT.Copy, scale=f)
                            last.then_inc(s["xte"].sem, 1)
                        if g == 2 and on(b + 1):
                            act.wait_ge(s["t7"].sem, s["t7"].at(b + 2))
                            act.wait_ge(s["kb"].sem, s["kb"].at(b + 1))
                            a_.activation(c_qT[1 - u].rearrange("p k s -> p (k s)"), pb[7][:, 0:KT * S], ACT.Copy,
                                          scale=columns)
                            a_.activation(c_kT.rearrange("p k s -> p (k s)"), pb[7][:, KT * S:2 * KT * S],
                                          ACT.Copy).then_inc(s["qe"].sem, 1)
                    if on(b + 2) and head is not None:
                        head(b + 2, u)
                    if on(b - 1):
                        act.wait_ge(s["ot"].sem, s["ot"].at(b))
                        a_.activation(c_oT.rearrange("p k s -> p (k s)"), pb[6][:, 0:KT * S],
                                      ACT.Copy).then_inc(s["oe"].sem, 1)
                batches(act, body, 3, 2)

            def c_square(b, u):
                act.wait_ge(Cs["qk"].sem, Cs["qk"].at(b + 1))
                act.wait_ge(Cs["ss"].sem, Cs["ss"].at(b))
                a_.activation(c_sq, pb[0][0:S, :], ACT.Square, scale=HD ** -0.5).then_inc(Cs["sq"].sem, 1)

            act.wait_ge(Bs["xu"].sem, Bs["xu"].at(B))
            act.wait_ge(ld["c2"].sem, ld["c2"].at(16 * 17))
            act.wait_ge(pre["kn"].sem, 1)
            attention(Cs, c_square, qn4, n12[:, 0:2])

            def phase_g(b, u, half):
                if on(b):
                    act.wait_ge(G["pc"].sem, G["pc"].at(3 * b))
                    a_.activation(g_sq, yb_(b), ACT.Square, accum_out=g_ms[:, 0:1]).then_inc(G["sq"].sem, 1)
                if on(b):
                    act.wait_ge(G["xt"].sem, G["xt"].at(b + 1))
                    act.wait_ge(G["lg"].sem, G["lg"].at(b))
                    act.wait_ge(G["cp"].sem, G["cp"].at(b))
                    for k in range(KT):
                        last = a_.activation(g_cols[:, k, :], pb[0][:, k * S:(k + 1) * S], ACT.Copy, scale=n12[:, 2 + k:3 + k])
                    last.then_inc(G["xte"].sem, 1)
                    act.wait_ge(G["lg"].sem, G["lg"].at(b + 1))
                    a_.activation(g_lg[:, bass.ds(b * 4, 4)], pb[1][0:S, 0:4], ACT.Copy).then_inc(G["le"].sem, 1)

            act.wait_ge(Cs["xu"].sem, Cs["xu"].at(B))
            batches(act, phase_g, 1)
            act.wait_ge(G["wt"].sem, G["wt"].at(1))
            a_.activation(g_b2, g_a, ACT.Exp).then_inc(G["wt"].sem, 1)

            def phase_m(i):
                plan = ([("gelu", m_h0, m) for m in range(4)] + [("gelu", m_ha, m) for m in range(4)]
                        + [x for m in range(4) for x in (("gate", None, m), ("up", None, m))]
                        + [("gelu", m_hb, m) for m in range(4)] + [("gelu", m_hc, m) for m in range(2)]
                        + [("gelu", m_ha, m) for m in range(4)] + [("gelu", m_hd, m) for m in range(4)])
                for n, (what, dst, m) in enumerate(plan):
                    src = pb[n % 4][:, 0:QN]
                    act.wait_ge(M["up"].sem, M["up"].at(UPS * i + n + 1))
                    if what == "gelu":
                        a_.activation(dst[:, m, :], src, ACT.Gelu).then_inc(M["ev"].sem, 1)
                    elif what == "gate":
                        act.wait_ge(M["h1"].sem, M["h1"].at(4 * i + m - 1))
                        a_.activation(m_s[:, m % 2, :], src, ACT.Tanh, scale=0.5)
                        a_.activation(m_g[:, m % 2, :], src, ACT.Copy).then_inc(M["ev"].sem, 1)
                    else:
                        a_.activation(m_u[:, m % 2, :], src, ACT.Copy).then_inc(M["ev"].sem, 1)

            phase_m(0)
            with act.Fori(1, B // QUAD) as i:
                phase_m(i)

            def d_latent(b, u):
                act.wait_ge(Ds["c"].sem, Ds["c"].at(b + 1))
                act.wait_ge(Ds["v"].sem, Ds["v"].at(b - 1))
                a_.activation(c_cT[u], pb[0][:, 0:S], ACT.Copy).then_inc(Ds["ce"].sem, 1)

            act.wait_ge(M["acc"].sem, M["acc"].at(64))
            attention(Ds, d_latent, HD ** -0.5, None)
            act.wait_ge(Ds["xu"].sem, Ds["xu"].at(B))
            attention(Es, None, HD ** -0.5, None)

            def phase_f(b, u, half):
                if on(b):
                    act.wait_ge(Fs["xt"].sem, Fs["xt"].at(b + 1))
                    act.wait_ge(Fs["mm"].sem, Fs["mm"].at(b))
                    a_.activation(f_xT.rearrange("p k s -> p (k s)"), pb[u][:, 0:KT * S], ACT.Copy).then_inc(Fs["xte"].sem, 1)

            act.wait_ge(Es["xu"].sem, Es["xu"].at(B))
            batches(act, phase_f, 1)

        @block.vector
        def _(dve):
            v_ = nc.vector

            def chain(s):
                return s["chain"]

            v_.memset(minus_one[:, :], -1.0).then_inc(pre["m1"].sem, 1)
            v_.memset(a_v[:, :, LD:LD + 1], 1.0).then_inc(pre["av"].sem, 1)
            dve.wait_ge(ld["bias"].sem, 32)
            dve.wait_ge(ld["cst"].sem, 16)
            v_.tensor_copy(ident_b[:, :], cst[0:S, C_ID:C_ID + S])
            for i, c in enumerate((C_CAUSAL, C_BAND)):
                last = v_.tensor_copy(masks_b[:, i, :].rearrange("q (j s) -> q j s", j=4),
                                      cst[0:S, c:c + S].unsqueeze(1).to_broadcast([S, 4, S]))
            last.then_inc(pre["masks"].sem, 1)
            v_.tensor_scalar(bqk0[:, :], bqk0[:, :], 1.0, None, ALU.add).then_inc(pre["bias1"].sem, 1)
            dve.wait_ge(ld["x"].sem, 16)
            dve.wait_ge(pre["bias1"].sem, 1)
            dve.wait_ge(ld["cst"].sem, 16)

            def stats_of(s, b, per, at):
                ln_stats(s, b, None)
                dve.wait_ge(s["chain"].sem, s["chain"].at(per * b + at + 1))
                v_.memset(rstd[:, 7:8], 0.0)
                v_.bn_aggr(mv[:, :], stats[:, :]).then_inc(s["mv"].sem, 1)

            def phase_a(b, u, half):
                if on(b + 1):
                    stats_of(A, b + 1, 1, 0)
                if isinstance(b, int) and b == -1:
                    ln_apply(A, 0, a_xn, 2, None).then_inc(A["xn"].sem, 1)
                if on(b):
                    def z_of(g):
                        dve.wait_ge(A["pg"].sem, A["pg"].at(6 * b + g + 1))
                        dve.wait_ge(A["ph"].sem, A["ph"].at(4 * b + g - 1))
                        bias = bqk0[:, 4 * g:4 * g + 4].unsqueeze(2).to_broadcast([P, 4, S])
                        v_.tensor_tensor(a_z[:, g % 2, :].rearrange("p (m s) -> p m s", m=4),
                                         pb[g % 2][:, 0:4 * S].rearrange("p (m s) -> p m s", m=4), bias,
                                         ALU.add).then_inc(A["pj"].sem, 1)

                    def phi_of(g):
                        dve.wait_ge(A["ex"].sem, A["ex"].at(4 * b + g + 1))
                        dst = (a_q if g < 2 else a_k)[:, (g % 2) * 4 * S:(g % 2 + 1) * 4 * S]
                        v_.scalar_tensor_tensor(dst, a_e[:, g % 2, :], 1.0, a_z[:, g % 2, :], ALU.min,
                                                ALU.max).then_inc(A["ph"].sem, 1)

                    def v_of(g):
                        dve.wait_ge(A["pg"].sem, A["pg"].at(6 * b + 5 + g))
                        v_.tensor_tensor(a_v[:, 8 * g:8 * g + 8, 0:LD],
                                         pb[g][0:S, :].rearrange("s (h e) -> s h e", h=8),
                                         bv0[:, g * 512:(g + 1) * 512].rearrange("s (h e) -> s h e", h=8),
                                         ALU.add).then_inc(A["pj"].sem, 1)

                    for g in range(4):
                        z_of(g)
                        if g:
                            phi_of(g - 1)
                    v_of(0)
                    phi_of(3)
                    v_of(1)
                    if on(b + 1):
                        ln_apply(A, b + 1, a_xn, 2, (A["xt"], b + 1)).then_inc(A["xn"].sem, 1)
                    tri = cst[0:S, C_TRI:C_TRI + S].unsqueeze(1).to_broadcast([S, 4, S])
                    for g in range(4):
                        dve.wait_ge(A["sg"].sem, A["sg"].at(4 * b + g + 1))
                        v_.tensor_tensor(a_at.rearrange("k (x j e s) -> k x e j s", x=2, j=4, e=2)[:, g // 2, g % 2],
                                         pb[2 + g % 2][0:S, 0:4 * S].rearrange("p (j s) -> p j s", j=4), tri,
                                         ALU.mult).then_inc(A["sm"].sem, 1)
                if isinstance(b, int) and b == 0:
                    dve.wait_ge(ld["mask"].sem, 16)
                    v_.tensor_scalar(mask_f[:, :], mask_i[:, :], 0, -1e20, ALU.is_equal, ALU.mult).then_inc(pre["rowbias"].sem, 1)
                if on(b - 1):
                    v = 1 - u
                    dve.wait_ge(pre[f"raw{v}"].sem, 16 * half if v else 16 * (half + 1))
                    dve.wait_ge(pre["parts"].sem, max(32 * (b - 1), 0) if isinstance(b, int) else 32 * (b - 1))
                    v_.tensor_scalar(s_high.bitcast(I32), s_raw[v].bitcast(I32), HIGH, None,
                                     ALU.bitwise_and).then_inc(pre["hi"].sem, 1)
                    dve.wait_ge(A["wd"].sem, A["wd"].at(b))
                    dve.wait_ge(A["xb"].sem, A["xb"].at(b))
                    v_.tensor_tensor(xb_(b - 1), xb_(b - 1), pb[7][0:S, 0:D], ALU.add).then_inc(A["xu"].sem, 1)
                if on(b):
                    dve.wait_ge(A["nd"].sem, A["nd"].at(3 * b + 3))
                    for n, (lo, hi) in enumerate(NUM):
                        num = pb[4 + n][0:S, 0:(hi - lo) * (LD + 1)].rearrange("s (h e) -> s h e", e=LD + 1)
                        last = v_.tensor_scalar(a_den[:, lo:hi].unsqueeze(2), num[:, :, LD:LD + 1], 1e-6, None, ALU.add)
                    last.then_inc(A["den"].sem, 1)
                    dve.wait_ge(A["den"].sem, A["den"].at(2 * b + 1))
                    v_.reciprocal(a_den[:, 16:32], a_den[:, 0:16]).then_inc(A["den"].sem, 1)
                    dve.wait_ge(A["den"].sem, A["den"].at(2 * b + 2))
                    for n, (lo, hi) in enumerate(NUM):
                        num = pb[4 + n][0:S, 0:(hi - lo) * (LD + 1)].rearrange("s (h e) -> s h e", e=LD + 1)
                        v_.tensor_tensor(a_o[:, lo * LD:hi * LD].rearrange("s (h e) -> s h e", e=LD), num[:, :, 0:LD],
                                         a_den[:, 16 + lo:16 + hi].unsqueeze(2).to_broadcast([S, hi - lo, LD]),
                                         ALU.mult).then_inc(A["nm"].sem, 1)

            dve.wait_ge(pre["av"].sem, 1)
            dve.wait_ge(ld["a2"].sem, 32)
            batches(dve, phase_a, 1)

            def phase_b(b, u, half):
                for p in range(8):
                    if p == 0 and on(b + 1):
                        stats_of(Bs, b + 1, 1, 0)
                    if on(b):
                        dve.wait_ge(Bs["sg"].sem, Bs["sg"].at(8 * b + p + 1))
                        pair = banks[0:S, 2 * (p % 2):2 * (p % 2) + 2, 0:SC]
                        v_.tensor_reduce(b_nb[:, 2 * p:2 * p + 2], pair, AX_X, ALU.max, negate=True).then_inc(Bs["nb"].sem, 1)
                    bt, pt = (b, p - 2) if p > 1 else (b - 1, 6 + p)
                    if on(bt):
                        h = 2 * pt
                        dve.wait_ge(Bs["tp"].sem, Bs["tp"].at(16 * bt + h + 1))
                        v_.tensor_copy(b_pT[:, h % 4, :], pb[4][0:KC, 0:NKC * S]).then_inc(Bs["ted"].sem, 1)
                    if p == 3 and on(b - 1):
                        dve.wait_ge(Bs["ut"].sem, Bs["ut"].at(b))
                        normalise(Bs, b - 1, pb[7][0:S, :].rearrange("s (h e) -> s h e", e=32), b_rc, b_o)
                    if on(b + 1) and p == 2:
                        dve.wait_ge(pre["bx"].sem, 2)
                        ln_heads(b + 1)
                    if p == 5 and on(b - 1):
                        dve.wait_ge(Bs["wd"].sem, Bs["wd"].at(b))
                        v_.tensor_tensor(xb_(b - 1), xb_(b - 1), pb[7][0:S, 0:D], ALU.add).then_inc(Bs["xu"].sem, 1)

            def ln_heads(b):
                dve.wait_ge(Bs["pc"].sem, Bs["pc"].at(b * 2 + 2))
                dve.wait_ge(Bs["ql"].sem, Bs["ql"].at(b))
                v_.tensor_scalar(b_x, xb_(b), mv[:, 0:1], rstd[:, 1:2], ALU.subtract, ALU.mult).then_inc(Bs["xn"].sem, 1)
                dve.wait_ge(Bs["xn"].sem, Bs["xn"].at(b + 1))
                dve.wait_ge(Bs["xq"].sem, Bs["xq"].at(4 * b))
                v_.tensor_scalar(parts_of(b_xs.bitcast(I32), 0), twice(b_x.bitcast(I32)), HIGH, None,
                                 ALU.bitwise_and).then_inc(Bs["qh"].sem, 1)

            def normalise(s, b, acc, rc, o):
                v_.reciprocal(rc.unsqueeze(2), acc[:, :, HD:HD + 1]).then_inc(s["den"].sem, 1)
                dve.wait_ge(s["den"].sem, s["den"].at(b + 1))
                v_.tensor_tensor(o.rearrange("s (h e) -> s h e", e=HD), acc[:, :, 0:HD],
                                 rc.unsqueeze(2).to_broadcast([S, H, HD]), ALU.mult).then_inc(s["nm"].sem, 1)

            dve.wait_ge(A["xu"].sem, A["xu"].at(B))
            v_.memset(pb[6][:, 0:4 * S], 0.0).then_inc(pre["b6"].sem, 1)
            batches(dve, phase_b, 1)

            def c_ln(b):
                ln_apply(Cs, b, yb_(b), 6, None).then_inc(Cs["y"].sem, 1)
                dve.wait_ge(Cs["y"].sem, Cs["y"].at(b + 1))
                dve.wait_ge(Cs["pc"].sem, Cs["pc"].at(6 * b + 6))
                dve.wait_ge(Cs["xt"].sem, Cs["xt"].at(b))
                v_.tensor_scalar(c_h, yb_(b), rstd[:, 5:6], None, ALU.mult).then_inc(Cs["xn"].sem, 1)

            def x_ln(s):
                def f(b):
                    ln_apply(s, b, c_h, 2, (s["xt"], b)).then_inc(s["xn"].sem, 1)
                return f

            def attention(s, ln_of, v_in, before, between, residual):
                def body(b, u, half):
                    for g in range(4):
                        if on(b):
                            dve.wait_ge(s["sg"].sem, s["sg"].at(4 * b + g + 1))
                            v_.tensor_reduce(c_nb[:, 4 * g:4 * g + 4],
                                             pb[2 + g % 2][0:S, 0:4 * S].rearrange("q (j s) -> q j s", j=4),
                                             AX_X, ALU.max, negate=True).then_inc(s["nb"].sem, 1)
                        if g == 2 and on(b + 1):
                            between(b + 1)
                        if g % 2 == 0 and on(b - 1):
                            dve.wait_ge(s["tp"].sem, s["tp"].at(4 * b + g - 3))
                            v_.tensor_copy(c_pT[:, g * 4 * S:(g + 1) * 4 * S], pb[4][0:S, 0:4 * S]).then_inc(s["ted"].sem, 1)
                        if g == 0 and on(b - 2):
                            dve.wait_ge(s["wd"].sem, s["wd"].at(b - 1))
                            residual(b - 2)
                        if g == 1 and on(b + 3):
                            stats_of(s, b + 3, 1, 0)
                        if g == 3 and on(b + 3):
                            ln_of(b + 3)
                    if on(b - 1):
                        dve.wait_ge(s["pv"].sem, s["pv"].at(b))
                        normalise(s, b - 1, pb[6][0:S, 0:H * 17].rearrange("s (h e) -> s h e", e=17), c_rc, c_o)
                    if on(b + 1):
                        v_in(b + 1, 1 - u)
                    if on(b + 2):
                        before(b + 2)
                batches(dve, body, 3, 2)

            def plain_v(s):
                def f(b, u):
                    dve.wait_ge(s["v"].sem, s["v"].at(b + 1))
                    v_.tensor_copy(c_v[u][:, :, 0:HD], pb[1][0:S, 0:D].rearrange("s (h e) -> s h e", h=H)).then_inc(s["ve"].sem, 1)
                return f

            def nothing(b):
                pass

            def c_sums(b):
                dve.wait_ge(Cs["sq"].sem, Cs["sq"].at(b + 1))
                dve.wait_ge(Cs["r"].sem, Cs["r"].at(b))
                v_.tensor_reduce(c_ss, c_sq.rearrange("s (h e) -> s h e", e=HD), AX_X, ALU.add).then_inc(Cs["ss"].sem, 1)

            def c_scaled(b):
                dve.wait_ge(Cs["r"].sem, Cs["r"].at(b + 1))
                v_.tensor_tensor(c_qk.rearrange("s (h e) -> s h e", e=HD), pb[0][0:S, :].rearrange("s (h e) -> s h e", e=HD),
                                 c_r.unsqueeze(2).to_broadcast([S, 32, HD]), ALU.mult).then_inc(Cs["qkn"].sem, 1)

            def c_residual(b):
                v_.tensor_tensor(yb_(b, FREE), yb_(b, FREE), pb[1][0:S, 0:DO], ALU.add).then_inc(Cs["xu"].sem, 1)

            def x_residual(s):
                def f(b):
                    v_.tensor_tensor(xb_(b), xb_(b), pb[1][0:S, 0:D], ALU.add).then_inc(s["xu"].sem, 1)
                return f

            dve.wait_ge(Bs["xu"].sem, Bs["xu"].at(B))
            dve.wait_ge(ld["c2"].sem, ld["c2"].at(16 * 17))
            v_.tensor_scalar(qn4, qkn[:, 0:1], HD ** -0.5, None, ALU.mult)
            v_.tensor_scalar(knbm, cst[:, C_BM:C_BM + 8], qkn[:, 1:2], None, ALU.mult).then_inc(pre["kn"].sem, 1)
            attention(Cs, c_ln, plain_v(Cs), c_sums, c_scaled, c_residual)

            def phase_g(b, u, half):
                if on(b):
                    dve.wait_ge(G["pc"].sem, G["pc"].at(3 * b + 3))
                    dve.wait_ge(G["xt"].sem, G["xt"].at(b))
                    v_.tensor_scalar(g_xf, yb_(b), g_ms[:, 3:4], None, ALU.mult).then_inc(G["xf"].sem, 1)

            batches(dve, phase_g, 1)
            dve.wait_ge(G["le"].sem, G["le"].at(B))
            steps = [0]

            def step(ins):
                steps[0] += 1
                ins.then_inc(G["chain"].sem, 1)
                dve.wait_ge(G["chain"].sem, G["chain"].at(steps[0]))

            lg3, a3, p3, w3 = (t.rearrange("s (b e) -> s b e", e=4) for t in (g_lg, g_a, g_b2, g_w))
            step(v_.tensor_scalar(g_lg, g_lg, -FLT_MAX, FLT_MAX, ALU.max, ALU.min))
            step(v_.tensor_reduce(g_red, lg3, AX_X, ALU.max))
            v_.tensor_tensor(a3, lg3, g_red.unsqueeze(2).to_broadcast([S, B, 4]), ALU.subtract).then_inc(G["wt"].sem, 1)
            dve.wait_ge(G["wt"].sem, G["wt"].at(2))
            step(v_.tensor_reduce(g_red, p3, AX_X, ALU.add))
            step(v_.reciprocal(g_red2, g_red))
            step(v_.tensor_tensor(a3, p3, g_red2.unsqueeze(2).to_broadcast([S, B, 4]), ALU.mult))
            c4, d4 = (t.rearrange("s (b e f) -> s b e f", e=4, f=4) for t in (g_cmp, g_cmp2))
            other = a3.unsqueeze(2).to_broadcast([S, B, 4, 4])
            own = a3.unsqueeze(3).to_broadcast([S, B, 4, 4])
            lt = cst[0:S, C_LT:C_LT + 16].rearrange("s (e f) -> s e f", e=4).unsqueeze(1).to_broadcast([S, B, 4, 4])
            step(v_.tensor_tensor(c4, other, own, ALU.is_equal))
            step(v_.tensor_tensor(c4, c4, lt, ALU.mult))
            step(v_.tensor_tensor(d4, other, own, ALU.is_gt))
            step(v_.tensor_tensor(g_cmp, g_cmp, g_cmp2, ALU.add))
            step(v_.tensor_reduce(g_b2, g_cmp.rearrange("s (n f) -> s n f", f=4), AX_X, ALU.add))
            step(v_.tensor_scalar(g_b2, g_b2, 2.0, None, ALU.is_lt))
            step(v_.tensor_tensor(g_w, g_b2, g_a, ALU.mult))
            step(v_.tensor_reduce(g_red, w3, AX_X, ALU.add))
            step(v_.tensor_scalar(g_red, g_red, 1e-8, None, ALU.add))
            step(v_.reciprocal(g_red2, g_red))
            step(v_.tensor_tensor(w3, w3, g_red2.unsqueeze(2).to_broadcast([S, B, 4]), ALU.mult))
            dve.wait_ge(G["xy"].sem, G["xy"].at(B))

            def phase_m(i, first):
                for m in range(FT):
                    dve.wait_ge(M["ev"].sem, M["ev"].at(UPS * i + 10 + 2 * m))
                    v_.scalar_tensor_tensor(m_t[:, m % 2, :], m_s[:, m % 2, :], 1.0, m_g[:, m % 2, :], ALU.add,
                                            ALU.mult).then_inc(M["t"].sem, 1)
                    dve.wait_ge(M["t"].sem, M["t"].at(4 * i + m + 1))
                    v_.scalar_tensor_tensor(m_h1[:, m, :], m_t[:, m % 2, :], 0.5, m_u[:, m % 2, :], ALU.mult,
                                            ALU.mult).then_inc(M["h1"].sem, 1)
                for e in range(4):
                    for j in range(QUAD):
                        n = e * QUAD + j
                        b = i * QUAD + j
                        dve.wait_ge(M["dn"].sem, M["dn"].at(16 * i + n + 1))
                        if n >= QUAD:
                            dve.wait_ge(M["acc"].sem, M["acc"].at(16 * i + n - 3))
                        v_.scalar_tensor_tensor(xb_(b, FREE), pb[4 + j][0:S, 0:DO], g_w[:, bass.ds(b * 4 + e, 1)],
                                                xb_(b, FREE), ALU.mult, ALU.add).then_inc(M["acc"].sem, 1)

            phase_m(0, True)
            with dve.Fori(1, B // QUAD) as i:
                phase_m(i, False)

            dve.wait_ge(M["acc"].sem, M["acc"].at(64))
            attention(Ds, x_ln(Ds), plain_v(Ds), nothing, nothing, x_residual(Ds))

            def e_v(b, u):
                dve.wait_ge(Es["v"].sem, Es["v"].at(b + 1))
                v_.tensor_tensor(c_v[u][:, :, 0:HD], pb[1][0:S, 0:D].rearrange("s (h e) -> s h e", h=H),
                                 b5[:, 2, :].rearrange("s (h e) -> s h e", h=H), ALU.add).then_inc(Es["ve"].sem, 1)

            def e_rotary(b):
                dve.wait_ge(Es["qk"].sem, Es["qk"].at(b + 1))
                dve.wait_ge(Es["rope"].sem, Es["rope"].at(b))
                z = c_z
                v_.tensor_tensor(z, pb[0][0:S, :], b5[:, 0:2, :].rearrange("s i n -> s (i n)"), ALU.add).then_inc(Es["z"].sem, 1)
                dve.wait_ge(Es["z"].sem, Es["z"].at(b + 1))
                dve.wait_ge(Es["qkn"].sem, Es["qkn"].at(b))
                z3, c3, t3 = (t.rearrange("s (h e) -> s h e", e=HD) for t in (z, c_sq, c_t2))
                cos = cst[0:S, C_COS:C_COS + HD].unsqueeze(1).to_broadcast([S, 32, HD])
                v_.tensor_tensor(c3, z3, cos, ALU.mult)
                for lo, hi in ((0, 8), (8, 0)):
                    sin = cst[0:S, C_SIN + lo:C_SIN + lo + 8].unsqueeze(1).to_broadcast([S, 32, 8])
                    last = v_.tensor_tensor(t3[:, :, lo:lo + 8], z3[:, :, hi:hi + 8], sin, ALU.mult)
                last.then_inc(Es["rope"].sem, 1)

            dve.wait_ge(Ds["xu"].sem, Ds["xu"].at(B))
            dve.wait_ge(ld["b5"].sem, 64)

            def e_res(b):
                dve.wait_ge(Es["xb"].sem, Es["xb"].at(b + 1))
                x_residual(Es)(b)

            attention(Es, x_ln(Es), e_v, e_rotary, nothing, e_res)

            dve.wait_ge(ld["pk"].sem, 16)
            dve.wait_ge(ld["f6"].sem, 32)
            for q in range(4):
                dve.wait_ge(pre["tern"].sem, pre["tern"].at(q))
                v_.tensor_scalar(enc[:, :, :], packed[:, :, :], 2 * q, 3, ALU.logical_shift_right,
                                 ALU.bitwise_and).then_inc(pre["enc"].sem, 1)
                dve.wait_ge(pre["enc"].sem, pre["enc"].at(q + 1))
                v_.tensor_scalar(tern[:, :, 64 * q:64 * q + 64], enc[:, :, :], -1.0, None, ALU.add).then_inc(pre["tern"].sem, 1)

            def phase_f(b, u, half):
                if on(b + 1):
                    stats_of(Fs, b + 1, 1, 0)
                if on(b):
                    dve.wait_ge(Fs["xn"].sem, Fs["xn"].at(b + 1))
                    v_.tensor_reduce(f_am[:, 0:1], f_xn, AX_X, ALU.max, apply_absolute_value=True).then_inc(Fs["am"].sem, 1)
                    dve.wait_ge(Fs["am"].sem, Fs["am"].at(6 * b + 1))
                    v_.tensor_scalar(f_am[:, 1:2], f_am[:, 0:1], 1e-5, None, ALU.max).then_inc(Fs["am"].sem, 1)
                    dve.wait_ge(Fs["am"].sem, Fs["am"].at(6 * b + 2))
                    v_.reciprocal(f_am[:, 2:3], f_am[:, 1:2]).then_inc(Fs["am"].sem, 1)
                    v_.tensor_scalar(f_sc[:, u:u + 1], f_am[:, 1:2], wscale[:, 0:1], 1.0 / 127, ALU.mult, ALU.mult)
                    dve.wait_ge(Fs["am"].sem, Fs["am"].at(6 * b + 3))
                    v_.tensor_scalar(f_am[:, 3:4], f_am[:, 2:3], 127.0, None, ALU.mult).then_inc(Fs["am"].sem, 1)
                    dve.wait_ge(Fs["am"].sem, Fs["am"].at(6 * b + 4))
                    dve.wait_ge(Fs["xt"].sem, Fs["xt"].at(b))
                    v_.tensor_scalar(f_q, f_xn, f_am[:, 3:4], ROUND, ALU.mult, ALU.add).then_inc(Fs["am"].sem, 1)
                    dve.wait_ge(Fs["am"].sem, Fs["am"].at(6 * b + 5))
                    v_.tensor_scalar(f_q, f_q, -ROUND, 127.0, ALU.add, ALU.min).then_inc(Fs["am"].sem, 1)
                    dve.wait_ge(Fs["am"].sem, Fs["am"].at(6 * b + 6))
                    v_.tensor_scalar(f_q, f_q, -128.0, None, ALU.max).then_inc(Fs["qz"].sem, 1)
                if on(b + 1):
                    ln_apply(Fs, b + 1, f_xn, 2, (Fs["qz"], b + 1)).then_inc(Fs["xn"].sem, 1)
                if on(b - 1):
                    dve.wait_ge(Fs["mm"].sem, Fs["mm"].at(b))
                    dve.wait_ge(Fs["xb"].sem, Fs["xb"].at(b))
                    v_.scalar_tensor_tensor(xb_(b - 1), pb[2 + (1 - u)][0:S, 0:D], f_sc[:, 1 - u:2 - u], xb_(b - 1), ALU.mult,
                                            ALU.add).then_inc(Fs["xu"].sem, 1)

            dve.wait_ge(Es["xu"].sem, Es["xu"].at(B))
            batches(dve, phase_f, 1)


def kernel(**inputs):
    import numpy as _np
    import concourse.bacc as _bacc
    from concourse import mybir as _mybir
    from concourse.bass_utils import run_bass_kernel_spmd as _run

    def a(name):
        return _np.asarray(inputs[name])

    def cols(v):
        return v.reshape(-1, P).T

    def row(v):
        return v.reshape(-1)

    f = "L0_ffn_"
    arrays = {
        "x": a("x"), "ctx": a("ctx_1024"), "ctxT": a("ctx_1024").transpose(0, 2, 1),
        "mask": a("mask_Bx1x1xS2_ik0").reshape(B, SC), "consts": constants(),
        "Wq": a("L0_attn_Wq"), "Wk": a("L0_attn_Wk"), "Wv": a("L0_attn_Wv"), "Wo": a("L0_attn_Wo"),
        "bq": cols(a("L0_attn_bq")), "bk": cols(a("L0_attn_bk")), "bv": row(a("L0_attn_bv")), "bo": row(a("L0_attn_bo")),
        "W_out": a("L0_xattn_W_out").T,
        "n12": _np.concatenate([cols(a(f + "n1_w")), cols(a(f + "n2_w"))], 1),
        "qn": a(f + "qn_w").reshape(HD, 1), "kn": a(f + "kn_w").reshape(HD, 1),
        "wq": a(f + "wq").T, "wk": a(f + "wk").T, "wv": a(f + "wv").T, "wo": a(f + "wo").T[:, FREE:],
        "gate": a(f + "gate_w").T,
        "e0_up": a(f + "e0_up").T, "e0_down": a(f + "e0_down").T[:, FREE:],
        "w1": a(f + "e1_w1").T, "w2": a(f + "e1_w2").T, "e1_down": a(f + "e1_down").T[:, FREE:],
        "l1": a(f + "e2_l1").T, "l2": a(f + "e2_l2").T, "l3": a(f + "e2_l3").T, "l4": a(f + "e2_l4").T[:, FREE:],
        "e3_down": a(f + "e3_down").T, "e3_up": a(f + "e3_up").T, "e3_out": a(f + "e3_out").T[:, FREE:],
        "W_dq": a("L1_attn_W_dq"), "W_uq": a("L1_attn_W_uq"), "W_dkv": a("L1_attn_W_dkv"),
        "W_uk": a("L1_attn_W_uk"), "W_uv": a("L1_attn_W_uv"), "W_o": a("L1_attn_W_o"),
        "packed": a("L1_ffn_packed_weight").reshape(64, D).T, "wscale": row(a("L1_ffn_weight_scale")),
        "bias": row(a("L1_ffn_bias")),
    }
    for n in "qkvo":
        arrays[f"{n}_w"] = a(f"L1_xattn_{n}_w").T
        arrays[f"{n}_b"] = row(a(f"L1_xattn_{n}_b"))
    arrays = {n: _np.ascontiguousarray(v) for n, v in arrays.items()}
    nc = _bacc.Bacc("TRN2", target_bir_lowering=False, num_devices=1)
    tensors = {n: nc.dram_tensor(f"in_{n}", v.shape, _mybir.dt.from_np(v.dtype), kind="ExternalInput").ap()
               for n, v in arrays.items()}
    out = nc.dram_tensor("out_0", (B, S, D), _mybir.dt.float32, kind="ExternalOutput").ap()
    decoder_kernel(nc, tensors, out)
    r = _run(nc, [{f"in_{n}": v for n, v in arrays.items()}], core_ids=[0])
    return r.results[0]["out_0"]
```

```python
from contextlib import ExitStack

import numpy as np
import concourse.bass as bass
from concourse import mybir

F32 = mybir.dt.float32
BF16 = mybir.dt.bfloat16
I32 = mybir.dt.int32
F32R = mybir.dt.float32r
ALU = mybir.AluOpType
ACT = mybir.ActivationFunctionType
AX_X = mybir.AxisListType.X

P = 128
B, S, D = 16, 112, 256
H, HD = 16, 16
SC = 375
SCP = SC + SC % 2
KC, NKC = 125, 3
LD = 64
LW = H * LD
KT = D // P
HID = 512
FT = HID // P
FREE = 64
DO = D - FREE
WINDOW = 64
QUAD = 4
QN = QUAD * S
BIG = 1e30
HIGH = -4096
B_WORK = 3600
STACK = 4 * HD + 1
AREA = 15696
B_OWN = 8864
RMS_EPS = 1.1920929e-07
FLT_MAX = 3.4028234663852886e38
ROUND = 1.5 * 2.0 ** 23
UPS = 30

C_ID = 0
C_TRI = C_ID + P
C_CAUSAL = C_TRI + S
C_BAND = C_CAUSAL + S
C_BM = C_BAND + S
C_COS = C_BM + 8
C_SIN = C_COS + HD
C_LT = C_SIN + HD
C_END = C_LT + 16


def constants():
    c = np.zeros((P, C_END), np.float32)
    c[:, C_ID:C_ID + P] = np.eye(P, dtype=np.float32)
    r = np.arange(S)
    c[:S, C_TRI:C_TRI + S] = r[:, None] <= r[None, :]
    c[:S, C_CAUSAL:C_CAUSAL + S] = np.where(r[None, :] <= r[:, None], 0, -BIG)
    c[:S, C_BAND:C_BAND + S] = np.where((r[None, :] <= r[:, None]) & (r[None, :] >= r[:, None] - WINDOW), 0, -BIG)
    p = np.arange(P)
    c[:, C_BM:C_BM + 8] = p[:, None] // HD == np.arange(8)[None, :]
    half = HD // 2
    freqs = (1.0 / 10000.0 ** (np.arange(half, dtype=np.float32) / half)).astype(np.float32)
    ang = r.astype(np.float32)[:, None] * freqs[None, :]
    c[:S, C_COS:C_COS + HD] = np.tile(np.cos(ang), (1, 2))
    c[:S, C_SIN:C_SIN + HD] = np.concatenate([-np.sin(ang), np.sin(ang)], 1)
    e = np.arange(4)
    c[:, C_LT:C_LT + 16] = (e[None, :] < e[:, None]).reshape(1, 16)
    return c


def on(b):
    return not isinstance(b, int) or 0 <= b < B


class Counter:

    def __init__(self, sem, base):
        self.sem, self.base = sem, base

    def at(self, value):
        return value + self.base if not isinstance(value, int) else max(value, 0) and value + self.base


def least(a, b):
    return min(a, b) if isinstance(a, int) else a


def batches(eng, body, ahead, behind=1, first=1):
    n = 6 if ahead == 1 else 5
    for b in range(-ahead, 2 * first + 1):
        body(b, b % 2, b // 2)
    with eng.Fori(first, n + 1) as i:
        body(2 * i + 1, 1, i)
        body(2 * i + 2, 0, i + 1)
    for b in range(2 * n + 3, B + behind):
        body(b, b % 2, b // 2)


def decoder_kernel(nc, T, out):
    ctx = ExitStack()
    with ctx:
        def sb(name, shape, dt=F32):
            return ctx.enter_context(nc.sbuf_tensor(name, shape, dt))

        def sems(prefix, names):
            return {n: Counter(ctx.enter_context(nc.semaphore(f"{prefix}_{n}")), 0) for n in names.split()}

        banks = ctx.enter_context(nc.psum_tensor("banks", [P, 8, 512], F32))
        pb = [banks[:, i, :] for i in range(8)]

        cst = sb("cst", [P, C_END])
        ident = cst[:, C_ID:C_ID + P]
        X = sb("X", [S, B * D])
        Y_room = sb("Y_room", [P, B * D])
        Y = Y_room[0:S, :]
        kcol = sb("kcol", [S, 5, 32])
        stats = sb("stats", [S, 6])
        mv = sb("mv", [S, 2])
        rstd = sb("rstd", [S, 8])
        stats_f, mv_f, rstd_f = sb("stats_f", [S, 6]), sb("mv_f", [S, 2]), sb("rstd_f", [S, 4])
        f_am = sb("f_am", [S, B])
        minus_round = sb("minus_round", [P, 1])
        rms = sb("rms", [S, 2 * B])
        minus_one = sb("minus_one", [P, 1])
        ident_b = sb("ident_b", [S, S], BF16)
        masks_b = sb("masks_b", [S, 2, 4 * S], BF16)

        def xb_(b, lo=0, hi=D):
            return X[:, bass.ds(b * D + lo, hi - lo)]

        def yb_(b, lo=0, hi=D):
            return Y[:, bass.ds(b * D + lo, hi - lo)]

        def overlay(*parts):
            with ExitStack() as lent:
                return [lent.enter_context(nc.sbuf_tensor(*p)) for p in parts]

        _, b_cp1 = overlay(("room_fp32", [P, 8 * SC], F32), ("b_cp1", [STACK, H * SCP], F32R))
        room = sb("room", [P, 4 * 2048 + 1024 + D])
        wq0, wk0, wv0 = (room[:, i * 2048:(i + 1) * 2048].rearrange("p (k n) -> p k n", k=KT) for i in range(3))
        wo0 = room[:, 3 * 2048:4 * 2048].rearrange("p (k n) -> p k n", k=LW // P)
        bv0 = room[0:S, 8192:8192 + LW]
        bo0 = room[0:S, 8192 + LW:8192 + LW + D]
        bqk0 = sb("bqk0", [P, 16])
        wx0 = sb("wx0", [P, KT, D])
        wqk1, wv1, wo1 = sb("wqk1", [P, KT, 2 * D]), sb("wv1", [P, KT, D]), sb("wo1", [P, KT, DO])
        n12 = sb("n12", [P, 4])
        qkn = sb("qkn", [P, 2])
        gate = sb("gate", [P, KT, 4])
        up0, dn0 = sb("up0", [P, KT, HID]), sb("dn0", [P, FT, DO])
        g1, u1, dn1 = sb("g1", [P, KT, HID]), sb("u1", [P, KT, HID]), sb("dn1", [P, FT, DO])
        l1, l2, l3, dn2 = sb("l1", [P, KT, HID]), sb("l2", [P, FT, HID]), sb("l3", [P, FT, HID]), sb("dn2", [P, FT, DO])
        d3, up3, dn3 = sb("d3", [P, KT, D]), sb("up3", [P, KT, HID]), sb("dn3", [P, FT, DO])
        wdd = sb("wdd", [P, KT, P])
        wuqk, wuv = sb("wuqk", [P, 2, D]), sb("wuv", [P, D])
        wo4, wq5, wk5, wv5, wo5 = (Y_room[:, i * 512:(i + 1) * 512].rearrange("p (k n) -> p k n", k=KT) for i in range(5))
        b5 = Y_room[0:S, 2560:3584].rearrange("p (i n) -> p i n", i=4)
        packed = sb("packed", [P, KT, 64], I32)
        enc = sb("enc", [P, KT, 64], I32)
        tern = sb("tern", [P, KT, D], BF16)
        wscale = sb("wscale", [S, 1])
        b6 = sb("b6", [S, D])
        mask_i = sb("mask_i", [B, SC], I32)
        mask_f = sb("mask_f", [B, SC])

        _, b_qs0, b_qs1, _, b_cp0 = overlay(("area_fp32", [P, B_WORK], F32), ("b_qs0", [STACK, H * S], F32R),
                                            ("b_qs1", [STACK, H * S], F32R),
                                            ("area_gap", [P, B_OWN - B_WORK - 2 * H * S], F32),
                                            ("b_cp0", [STACK, H * SCP], F32R))
        area = sb("area", [P, AREA])
        top = [0]

        def take(parts, n, pattern=None, **dims):
            a = area[0:parts, top[0]:top[0] + n]
            top[0] += n
            assert top[0] <= AREA
            return a.rearrange(pattern, **dims) if pattern else a

        parts_scratch = nc.dram_tensor("parts_scratch", (2, B, D, SC), F32, kind="Internal").ap()
        mask_scratch = nc.dram_tensor("mask_scratch", (B, SC), F32, kind="Internal").ap()

        ld = sems("ld", "x0 x cst bias a0 a1 a2 a3 bo wx mask c1 c2 gate e0 e1 e2 e3 d4 e5 b5 f6 pk")
        pre = sems("pre", "masks bias1 pad scale m1 av rowbias scratch tern enc kn bx b6 cv raw0 raw1 hi lo parts")

        A = sems("A", "mv pc xn xb xt xte pg pj ex ph sg sm nd chain den nm ot oe wd xu")
        Bs = sems("B", "qh ql xq qs ue ut sg nb ex tp ted tea pv den nm ot oe cp0 cp1 cv0 cv1")
        for n in "mv xn chain wd xu".split():
            Bs[n] = Counter(A[n].sem, B)
        Bs["pc"] = Counter(A["pc"].sem, 2 * B)
        core1 = "mv xn xt xte v ve t7 qe pv ue ut chain den nm ot oe wd xu"
        core4 = "sg nb ex tp"
        Cs = sems("C", "y pc qk sq ss rc r qkn kb ted tea " + core1 + " " + core4)
        Ds = sems("D", "pc c ce")
        Es = sems("E", "xb z rope k0 k1")
        for s, n in ((Ds, 1), (Es, 2)):
            for names, per in ((core1, 1), (core4, 4), ("kb ted tea", 2)):
                for name in names.split():
                    s[name] = Counter(Cs[name].sem, n * per * B)
        for name in ("qk", "qkn"):
            Es[name] = Counter(Cs[name].sem, B)
        Es["pc"] = Counter(Ds["pc"].sem, 2 * B)
        G = sems("G", "sq pc xf xt xte lt ls lg le xy chain wt")
        M = sems("M", "up ev h1 t dn acc")
        Fs = sems("F", "am sm sh cl sf mm st")
        for n in "mv xn xu".split():
            Fs[n] = Counter(A[n].sem, 2 * B)
        for n in ("xb", "xt", "xte"):
            Fs[n] = Counter(A[n].sem, B)
        Fs["pc"] = Counter(A["pc"].sem, 4 * B)

        block = ctx.enter_context(nc.Block())

        def ln_stats(s, b):
            nc.vector.wait_ge(s["xn"].sem, s["xn"].at(b))
            nc.vector.bn_stats(stats[:, :], xb_(b)).then_inc(s["chain"].sem, 1)

        def ln_rstd(s, b, n_pc):
            nc.gpsimd.wait_ge(s["mv"].sem, s["mv"].at(b + 1))
            nc.gpsimd.tensor_tensor(rstd[:, 0:1], mv[:, 1:2], kcol[:, 1, 0:1], ALU.add).then_inc(s["pc"].sem, 1)
            nc.gpsimd.wait_ge(s["pc"].sem, s["pc"].at(b * n_pc + 1))
            nc.gpsimd.tensor_tensor(rstd[:, 1:2], rstd[:, 0:1], kcol[:, 0, 0:1], ALU.pow).then_inc(s["pc"].sem, 1)

        def ln_apply(s, b, dst, n_pc, src_free):
            nc.vector.wait_ge(s["pc"].sem, s["pc"].at(b * n_pc + 2))
            if src_free is not None:
                nc.vector.wait_ge(src_free[0].sem, src_free[0].at(src_free[1]))
            return nc.vector.tensor_scalar(dst, xb_(b), mv[:, 0:1], rstd[:, 1:2], ALU.subtract, ALU.mult)

        def twice(a):
            return a.rearrange("s (h e) -> s h e", h=H).unsqueeze(2).to_broadcast([S, H, 2, HD])

        def parts_of(a, c):
            return a[:, :, c * HD:(c + 2) * HD].rearrange("s h (c e) -> s h c e", c=2)

        def transposes(src, parts, n, dst):
            for k in range(n):
                last = nc.tensor.transpose(dst[:, k * parts:(k + 1) * parts], src[:, k * P:(k + 1) * P],
                                           ident[0:parts, 0:parts])
            return last

        def products(dst, lhs, rhs):
            for k, (a, w) in enumerate(zip(lhs, rhs)):
                last = nc.tensor.matmul(dst, a, w, start=(k == 0), stop=(k == len(lhs) - 1))
            return last

        top[0] = 0
        a_xn = take(S, D)
        a_xnT = take(P, KT * S, "p (k s) -> p k s", k=KT)
        a_q, a_k = take(P, 8 * S), take(P, 8 * S)
        a_z, a_e = take(P, 2 * 4 * S, "p (g n) -> p g n", g=2), take(P, 2 * 4 * S, "p (g n) -> p g n", g=2)
        a_v = take(S, H * (LD + 1), "p (h e) -> p h e", h=H)
        a_at = take(S, H * S)
        a_o = take(S, LW)
        a_oT = take(P, 8 * S)
        a_den = take(S, 32)
        assert top[0] <= B_OWN
        NUM = [(0, 6), (6, 12), (12, 16)]

        top[0] = 0
        b_x = take(S, D)
        b_xs = take(S, H * STACK, "p (h c) -> p h c", h=H)
        b_qs = [b_qs0[:, :], b_qs1[:, :]]
        b_pT = take(KC, 4 * NKC * S, "p (g n) -> p g n", g=4)
        b_nb = take(S, H)
        b_rc = take(S, H)
        b_u = take(P, 4 * S)
        b_o = take(S, D)
        b_oT = take(P, KT * S)
        assert top[0] <= B_WORK
        top[0] = B_OWN + H * SCP
        b_cp = [t[:, :].rearrange("p (h s) -> p h s", h=H) for t in (b_cp0, b_cp1)]
        b_p = room[0:S, 0:4 * 2 * SC].rearrange("p (g h s) -> p g h s", g=4, h=2)
        b_cv = [take(KC, NKC * H * 17, "p (c h e) -> p c h e", c=NKC, h=H),
                Y_room[0:KC, 4 * 2 * SC:4 * 2 * SC + NKC * H * 17].rearrange("p (c h e) -> p c h e", c=NKC, h=H)]
        s_raw = [Y_room[:, i * 2 * SC:(i + 1) * 2 * SC].rearrange("p (k s) -> p k s", k=KT) for i in range(2)]
        s_high, s_low = (Y_room[:, i * 2 * SC:(i + 1) * 2 * SC].rearrange("p (k s) -> p k s", k=KT) for i in (2, 3))

        top[0] = 0
        c_h = take(S, D)
        c_xnT = [take(P, KT * S, "p (k s) -> p k s", k=KT) for _ in range(2)]
        c_sq = take(S, 2 * D)
        c_t2, c_z = take(S, 2 * D), take(S, 2 * D)
        c_qk = take(S, 2 * D)
        c_ss, c_r = take(S, 32), take(S, 32)
        c_qT = [take(P, KT * S, "p (k s) -> p k s", k=KT) for _ in range(2)]
        c_kT = take(P, KT * S, "p (k s) -> p k s", k=KT)
        c_kbd = [take(P, KT * 8 * S, "p (k j s) -> p k j s", k=KT, j=8) for _ in range(2)]
        c_v = [take(S, H * 17, "p (h e) -> p h e", h=H) for _ in range(2)]
        c_p, c_pT = (take(S, H * S) for _ in range(2))
        c_nb, c_rc = take(S, H), take(S, H)
        c_u = take(P, 4 * S)
        c_o = take(S, D)
        c_oT = take(P, KT * S, "p (k s) -> p k s", k=KT)
        c_cT = [take(P, S) for _ in range(2)]
        c_junk = take(S, D)
        knbm, qn4 = take(P, 8), take(P, 1)
        e_ctx = [c_h_ for c_h_ in (room[:, i * KT * S:(i + 1) * KT * S].rearrange("p (k s) -> p k s", k=KT) for i in range(2))]

        top[0] = 0
        m_xfT = take(P, KT * B * S, "p (k n) -> p k n", k=KT)
        g_xf = [take(S, D) for _ in range(2)]
        g_lt = take(4, B * S)
        g_lg = take(S, B * 4)
        g_a, g_b2, g_w = take(S, B * 4), take(S, B * 4), take(S, B * 4)
        g_red, g_red2 = take(S, B), take(S, B)
        g_cmp, g_cmp2 = take(S, B * 16), take(S, B * 16)
        m_g, m_s, m_u, m_t = (take(P, 2 * QN, "p (g n) -> p g n", g=2) for _ in range(4))
        m_h0, m_h1, m_ha, m_hb = (room[:, i * FT * QN:(i + 1) * FT * QN].rearrange("p (k n) -> p k n", k=FT) for i in range(4))
        m_hc = room[:, 4 * FT * QN:4 * FT * QN + KT * QN].rearrange("p (k n) -> p k n", k=KT)
        m_hd = take(P, FT * QN, "p (k n) -> p k n", k=FT)

        top[0] = 0
        f_xn = room[0:S, 1024:1024 + B * D]
        f_q = [take(S, D) for _ in range(2)]
        f_s, f_sc = take(S, 2 * B), take(S, B)
        f_xT = [take(P, S).bitcast(BF16).rearrange("p (k s) -> p k s", k=KT) for _ in range(2)]

        def wload(eng, dst, name, sem):
            src = T[name].rearrange("(k p) n -> p k n", p=P)
            eng.dma_start(dst, src).then_inc(sem.sem, 16)

        def bcast(eng, dst, name, sem, parts=S):
            eng.dma_start(dst, T[name].partition_broadcast(parts)).then_inc(sem.sem, 16)

        @block.sync
        def _(sp):
            x_rows, x_out = T["x"].rearrange("b s d -> s b d"), X[:, :].rearrange("s (b d) -> s b d", b=B)
            sp.dma_start(x_out[:, 0:2], x_rows[:, 0:2]).then_inc(ld["x0"].sem, 16)
            sp.dma_start(cst[:, :], T["consts"]).then_inc(ld["cst"].sem, 16)
            wload(sp, wq0, "Wq", ld["a0"])
            sp.dma_start(bqk0[:, 0:8], T["bq"]).then_inc(ld["bias"].sem, 16)
            sp.dma_start(bqk0[:, 8:16], T["bk"]).then_inc(ld["bias"].sem, 16)
            wload(sp, wk0, "Wk", ld["a1"])
            bcast(sp, bv0, "bv", ld["a2"])
            wload(sp, wv0, "Wv", ld["a2"])
            sp.dma_start(x_out[:, 2:B], x_rows[:, 2:B]).then_inc(ld["x"].sem, 16)
            wload(sp, wo0, "Wo", ld["a3"])
            bcast(sp, bo0, "bo", ld["bo"])
            sp.dma_start(mask_i[:, :], T["mask"]).then_inc(ld["mask"].sem, 16)
            wload(sp, wx0[:, :, :], "W_out", ld["wx"])
            sp.dma_start(s_raw[0], T["ctxT"][0].rearrange("(k p) s -> p k s", p=P)).then_inc(pre["raw0"].sem, 16)
            sp.wait_ge(pre["rowbias"].sem, 1)
            sp.dma_start(mask_scratch, mask_f[:, :]).then_inc(pre["scratch"].sem, 16)
            wload(sp, wqk1[:, :, 0:D], "wq", ld["c1"])
            wload(sp, wqk1[:, :, D:2 * D], "wk", ld["c1"])
            wload(sp, wv1[:, :, :], "wv", ld["c1"])
            wload(sp, wo1[:, :, :], "wo", ld["c1"])
            sp.dma_start(n12[:, :], T["n12"]).then_inc(ld["c2"].sem, 16)
            for i, n in enumerate(("qn", "kn")):
                for r in range(8):
                    sp.dma_start(qkn[HD * r:HD * r + HD, i:i + 1], T[n]).then_inc(ld["c2"].sem, 16)
            wload(sp, gate[:, :, :], "gate", ld["gate"])
            sp.wait_ge(pre["scratch"].sem, 16)

            def part_stores(b, u, half):
                if on(b + 1) and not (isinstance(b, int) and b < 0):
                    n = b + 1
                    sp.wait_ge(pre["lo"].sem, b)
                    src = T["ctxT"][bass.ds(n, 1)].rearrange("o (k p) s -> (o p) k s", p=P)
                    sp.dma_start(s_raw[1 - u], src).then_inc(pre[f"raw{1 - u}"].sem, 16)
                if on(b):
                    sp.wait_ge(pre["lo"].sem, b + 1)
                    for i, src in enumerate((s_high, s_low)):
                        dst = parts_scratch[i, bass.ds(b, 1)].rearrange("o (k p) s -> (o p) k s", p=P)
                        sp.dma_start(dst, src).then_inc(pre["parts"].sem, 16)

            batches(sp, part_stores, 1)

            def ctx_loads(b, u, half):
                if not on(b):
                    return
                cv = Bs[f"cv{u}"]
                if isinstance(b, int) and b == 1:
                    sp.wait_ge(pre["parts"].sem, 32 * B)
                sp.wait_ge(pre["pad"].sem, 2)
                sp.wait_ge(Bs["pv"].sem, Bs["pv"].at(8 * (b - 1)))
                for c in range(NKC):
                    src = T["ctx"][bass.ds(b, 1), c * KC:(c + 1) * KC].rearrange("o p (h e) -> (o p) h e", h=H)
                    sp.dma_start(b_cv[u][:, c, :, 0:HD], src).then_inc(cv.sem, 16)

            batches(sp, ctx_loads, 1)
            for name, dst, sem in (("e0_up", up0, "e0"), ("e0_down", dn0, "e0"), ("l1", l1, "e2"),
                                   ("w1", g1, "e1"), ("w2", u1, "e1"), ("l2", l2, "e2"), ("e1_down", dn1, "e1"),
                                   ("e3_down", d3, "e3"), ("l3", l3, "e2"), ("e3_up", up3, "e3"),
                                   ("l4", dn2, "e2"), ("e3_out", dn3, "e3")):
                wload(sp, dst[:, :, :], name, ld[sem])
            sp.wait_ge(pre["pad"].sem, 3)
            wload(sp, wdd[:, :, 0:64], "W_dq", ld["d4"])
            wload(sp, wdd[:, :, 64:128], "W_dkv", ld["d4"])
            sp.dma_start(wuqk[0:64, 0, :], T["W_uq"]).then_inc(ld["d4"].sem, 16)
            sp.dma_start(wuqk[64:128, 1, :], T["W_uk"]).then_inc(ld["d4"].sem, 16)
            sp.dma_start(wuv[64:128, :], T["W_uv"]).then_inc(ld["d4"].sem, 16)
            sp.wait_ge(G["xy"].sem, G["xy"].at(B))
            sp.wait_ge(G["xf"].sem, G["xf"].at(B))
            wload(sp, wo4, "W_o", ld["d4"])
            for name, dst in (("q_w", wq5), ("k_w", wk5), ("v_w", wv5), ("o_w", wo5)):
                wload(sp, dst, name, ld["e5"])
            for i, name in enumerate(("q_b", "k_b", "v_b", "o_b")):
                bcast(sp, b5[:, i, :], name, ld["b5"])
            sp.dma_start(packed[:, :, :], T["packed"].rearrange("(k p) o -> p k o", p=P)).then_inc(ld["pk"].sem, 16)
            bcast(sp, wscale[:, :], "wscale", ld["f6"])
            bcast(sp, b6[:, :], "bias", ld["f6"])

            def window_loads(b, u, half):
                if not on(b):
                    return
                sp.wait_ge(M["acc"].sem, M["acc"].at(64))
                sp.wait_ge(Es["v"].sem, Es["v"].at(b - 1))
                src = T["ctxT"][bass.ds(b, 1), :, 0:S].rearrange("o (k p) s -> (o p) k s", p=P)
                sp.dma_start(e_ctx[u], src).then_inc(Es[f"k{u}"].sem, 16)

            batches(sp, window_loads, 1)

            def stores(b, u, half):
                if not on(b):
                    return
                sp.wait_ge(Fs["xu"].sem, Fs["xu"].at(b + 1))
                sp.dma_start(out[bass.ds(b, 1)].rearrange("o s d -> (o s) d"), xb_(b)).then_inc(Fs["st"].sem, 16)

            batches(sp, stores, 1)
            sp.wait_ge(Fs["st"].sem, Fs["st"].at(16 * B))

        @block.tensor
        def _(pe):
            T3 = nc.tensor

            def phase_a(b, u, half):
                if on(b):
                    pe.wait_ge(A["xte"].sem, A["xte"].at(b + 1))
                    for g in range(4):
                        pe.wait_ge(A["pj"].sem, A["pj"].at(6 * b + g - 1))
                        if isinstance(b, int) and b == 0:
                            pe.wait_ge(ld["a0" if g < 2 else "a1"].sem, 16)
                        w = wq0 if g < 2 else wk0
                        for t in range(4):
                            m = 4 * (g % 2) + t
                            last = products(pb[g % 2][:, t * S:(t + 1) * S],
                                            [w[:, k, m * P:(m + 1) * P] for k in range(KT)],
                                            [a_xnT[:, k, :] for k in range(KT)])
                        last.then_inc(A["pg"].sem, 1)
                if on(b - 1):
                    pe.wait_ge(A["nm"].sem, A["nm"].at(3 * b))
                    for g in range(2):
                        transposes(a_o[:, g * 512:(g + 1) * 512], S, 4, pb[2 + g]).then_inc(A["ot"].sem, 1)
                if on(b):
                    for g in range(2):
                        pe.wait_ge(A["pj"].sem, A["pj"].at(6 * b + 3 + g))
                        if isinstance(b, int) and b == 0:
                            pe.wait_ge(ld["a2"].sem, 32)
                        products(pb[g][0:S, :], [a_xnT[:, k, :] for k in range(KT)],
                                 [wv0[:, k, g * 512:(g + 1) * 512] for k in range(KT)]).then_inc(A["pg"].sem, 1)

                def scores(x):
                    pe.wait_ge(A["ph"].sem, A["ph"].at(4 * b + 3 + x))
                    pe.wait_ge(A["oe"].sem, A["oe"].at(2 * b))
                    pe.wait_ge(A["sm"].sem, A["sm"].at(4 * b + 2 * x))
                    for j in range(4):
                        m = 4 * x + j
                        for e in range(2):
                            r = LD * e
                            last = T3.matmul(pb[2 + e][0:S, j * S:(j + 1) * S], a_k[r:r + LD, m * S:(m + 1) * S],
                                             a_q[r:r + LD, m * S:(m + 1) * S], start=True, stop=True)
                            if j == 3:
                                last.then_inc(A["sg"].sem, 1)

                if on(b):
                    scores(0)
                if on(b - 1):
                    pe.wait_ge(A["oe"].sem, A["oe"].at(2 * b))
                    pe.wait_ge(A["xte"].sem, A["xte"].at(least(b + 1, B)))
                    if isinstance(b, int) and b == 1:
                        pe.wait_ge(ld["a3"].sem, 16)
                    products(pb[7][0:S, 0:D], [a_oT[:, m * S:(m + 1) * S] for m in range(8)],
                             [wo0[:, m, :] for m in range(8)]).then_inc(A["wd"].sem, 1)
                if on(b):
                    scores(1)
                if on(b + 1):
                    pe.wait_ge(A["xn"].sem, A["xn"].at(b + 2))
                    pe.wait_ge(A["xu"].sem, A["xu"].at(b))
                    transposes(a_xn, S, KT, pb[7]).then_inc(A["xt"].sem, 1)
                if on(b):
                    pe.wait_ge(A["nm"].sem, A["nm"].at(3 * b))
                    pe.wait_ge(A["pj"].sem, A["pj"].at(6 * b + 6))
                    for h in range(H):
                        if h % 8 == 0:
                            pe.wait_ge(A["sm"].sem, A["sm"].at(4 * b + h // 4 + 2))
                        n = h // 6
                        o = (h - NUM[n][0]) * (LD + 1)
                        last = T3.matmul(pb[4 + n][0:S, o:o + LD + 1], a_at[:, h * S:(h + 1) * S], a_v[:, h, :],
                                         start=True, stop=True)
                        if h + 1 == NUM[n][1]:
                            last.then_inc(A["nd"].sem, 1)

            pe.wait_ge(ld["cst"].sem, 16)
            batches(pe, phase_a, 1)

            def phase_b(b, u, half):
                for p in range(8):
                    if on(b):
                        if p == 0:
                            pe.wait_ge(Bs[f"cp{u}"].sem, Bs[f"cp{u}"].at(16 * 5 * (half + 1)))
                        if p % 2 == 0:
                            pe.wait_ge(Bs["qs"].sem, Bs["qs"].at(4 * b + p // 2 + 1))
                        pe.wait_ge(Bs["ex"].sem, Bs["ex"].at(16 * b + 2 * p - 2))
                        for e in range(2):
                            h = 2 * p + e
                            last = T3.matmul(pb[2 * (p % 2) + e][0:S, 0:SCP],
                                             b_qs[u][:, h * S:(h + 1) * S], b_cp[u][:, h, :], start=True, stop=True)
                        last.then_inc(Bs["sg"].sem, 1)
                    bt, pt = (b, p - 2) if p > 1 else (b - 1, 6 + p)
                    if on(bt):
                        for e in range(2):
                            h = 2 * pt + e
                            pe.wait_ge(Bs["ex"].sem, Bs["ex"].at(16 * bt + h + 1))
                            pe.wait_ge(Bs["tea" if e else "ted"].sem, Bs["tea" if e else "ted"].at(8 * bt + pt))
                            for c in range(NKC):
                                last = T3.transpose(pb[4 + e][0:KC, c * S:(c + 1) * S],
                                                    b_p[:, pt % 4, e, c * KC:(c + 1) * KC], ident[0:S, 0:S])
                            last.then_inc(Bs["tp"].sem, 1)
                    bv, pv = (b, p - 3) if p > 2 else (b - 1, 5 + p)
                    if on(bv):
                        if pv == 0:
                            pe.wait_ge(Bs["ue"].sem, Bs["ue"].at(bv))
                            pe.wait_ge(Bs[f"cv{u}"].sem, Bs[f"cv{u}"].at(16 * 3 * (half + 1)))
                            if isinstance(b, int) and b == 0:
                                pe.wait_ge(pre["b6"].sem, 1)
                        uv = u if p > 2 else 1 - u
                        pe.wait_ge(Bs["ted"].sem, Bs["ted"].at(8 * bv + pv + 1))
                        pe.wait_ge(Bs["tea"].sem, Bs["tea"].at(8 * bv + pv + 1))
                        for c in range(NKC):
                            for e in range(2):
                                h = 2 * pv + e
                                r = 32 * (h % 4)
                                last = T3.matmul(pb[6][r:r + 17, (h // 4) * S:(h // 4 + 1) * S], b_cv[uv][:, c, h, :],
                                                 b_pT[:, h % 4, c * S:(c + 1) * S], start=(c == 0), stop=(c == NKC - 1),
                                                 tile_position=(0, r))
                        last.then_inc(Bs["pv"].sem, 1)
                    if p == 3 and on(b - 1):
                        pe.wait_ge(Bs["ue"].sem, Bs["ue"].at(b))
                        pe.wait_ge(Bs["qs"].sem, Bs["qs"].at(4 * least(b + 1, B)))
                        for t in range(4):
                            last = T3.transpose(pb[7][0:S, t * P:(t + 1) * P], b_u[:, t * S:(t + 1) * S], ident)
                        last.then_inc(Bs["ut"].sem, 1)
                    if p == 4 and on(b - 1):
                        pe.wait_ge(Bs["nm"].sem, Bs["nm"].at(b))
                        transposes(b_o, S, KT, pb[7]).then_inc(Bs["ot"].sem, 1)
                    if p == 5 and on(b - 1):
                        pe.wait_ge(Bs["oe"].sem, Bs["oe"].at(b))
                        if isinstance(b, int) and b == 1:
                            pe.wait_ge(ld["wx"].sem, 16)
                        products(pb[7][0:S, 0:D], [b_oT[:, k * S:(k + 1) * S] for k in range(KT)],
                                 [wx0[:, k, :] for k in range(KT)]).then_inc(Bs["wd"].sem, 1)
                    if p < 2 and on(b):
                        stack(b, p + 2)
                    if p > 5 and on(b + 1):
                        if p == 6:
                            pe.wait_ge(Bs["ql"].sem, Bs["ql"].at(b + 2))
                            pe.wait_ge(Bs["xu"].sem, Bs["xu"].at(b))
                        stack(b + 1, p - 6)

            def stack(b, g):
                pe.wait_ge(Bs["qs"].sem, Bs["qs"].at(4 * b + g))
                for j in range(4):
                    last = T3.transpose(pb[7][0:STACK, j * S:(j + 1) * S], b_xs[:, 4 * g + j, :], ident[0:S, 0:S])
                last.then_inc(Bs["xq"].sem, 1)

            pe.wait_ge(A["xu"].sem, A["xu"].at(B))
            batches(pe, phase_b, 1)

            def attention(s, mask, project_qk, project_v, qk_read, to_columns, w_out, dst_out, col_g=2):
                def body(b, u, half):
                    for g in range(5):
                        if g < 4 and on(b):
                            if g == 0:
                                pe.wait_ge(s["kb"].sem, s["kb"].at(2 * b + 1))
                            if g == 2:
                                pe.wait_ge(s["kb"].sem, s["kb"].at(2 * b + 2))
                            pe.wait_ge(s["ex"].sem, s["ex"].at(4 * b + g - 1))
                            k, j = g // 2, 4 * (g % 2)
                            T3.matmul(pb[2 + g % 2][0:S, 0:4 * S], c_qT[u][:, k, :],
                                      c_kbd[u][:, k, j:j + 4, :].rearrange("p j s -> p (j s)"),
                                      start=True, stop=False)
                            T3.matmul(pb[2 + g % 2][0:S, 0:4 * S], ident_b[:, :], mask,
                                      start=False, stop=True).then_inc(s["sg"].sem, 1)
                        if g < 4 and on(b - 1):
                            pe.wait_ge(s["ex"].sem, s["ex"].at(4 * b + g - 3))
                            if g % 2:
                                pe.wait_ge(s["tea"].sem, s["tea"].at(2 * b - 2 + g // 2))
                            else:
                                pe.wait_ge(s["ted"].sem, s["ted"].at(2 * b - 2 + g // 2))
                            for j in range(4):
                                h = 4 * g + j
                                last = T3.transpose(pb[4 + g % 2][0:S, j * S:(j + 1) * S],
                                                    c_p[:, h * S:(h + 1) * S], ident[0:S, 0:S])
                            last.then_inc(s["tp"].sem, 1)
                        if g > 0 and on(b - 1):
                            v = g - 1
                            if v == 0:
                                pe.wait_ge(s["ue"].sem, s["ue"].at(b - 1))
                            if v % 2:
                                pe.wait_ge(s["tea"].sem, s["tea"].at(2 * b - 1 + v // 2))
                            else:
                                pe.wait_ge(s["ted"].sem, s["ted"].at(2 * b - 1 + v // 2))
                            for j in range(4):
                                h = 4 * v + j
                                last = T3.matmul(pb[6][32 * j:32 * j + 17, v * S:(v + 1) * S], c_v[1 - u][:, h, :],
                                                 c_pT[:, h * S:(h + 1) * S], start=True, stop=True, tile_position=(0, 32 * j))
                            if v == 3:
                                last.then_inc(s["pv"].sem, 1)
                        if g == 0 and on(b - 2):
                            pe.wait_ge(s["ue"].sem, s["ue"].at(b - 1))
                            pe.wait_ge(s["qe"].sem, s["qe"].at(least(b + 1, B)))
                            pe.wait_ge(s["xu"].sem, s["xu"].at(b - 2))
                            for t in range(4):
                                last = T3.transpose(pb[7][0:S, t * P:(t + 1) * P], c_u[:, t * S:(t + 1) * S], ident)
                            last.then_inc(s["ut"].sem, 1)
                        if g == 1 and on(b + 2):
                            pe.wait_ge(s["xn"].sem, s["xn"].at(b + 3))
                            pe.wait_ge(s["ve"].sem, s["ve"].at(b + 1))
                            transposes(c_h, S, KT, pb[1]).then_inc(s["xt"].sem, 1)
                        if g == 1 and on(b - 2):
                            pe.wait_ge(s["nm"].sem, s["nm"].at(b - 1))
                            transposes(c_o, S, KT, pb[7]).then_inc(s["ot"].sem, 1)
                        if g == col_g and on(b + 1):
                            pe.wait_ge(s["oe"].sem, s["oe"].at(b - 1))
                            pe.wait_ge(s["xu"].sem, s["xu"].at(b - 2))
                            to_columns(b + 1, 1 - u)
                        if g == 3 and on(b + 2):
                            pe.wait_ge(qk_read.sem, qk_read.at(b + 2))
                            pe.wait_ge(s["xte"].sem, s["xte"].at(b + 3))
                            project_qk(b + 2, u, half + 1)
                        if g == 3 and on(b + 1):
                            pe.wait_ge(s["ve"].sem, s["ve"].at(b + 1))
                            pe.wait_ge(s["xte"].sem, s["xte"].at(least(b + 3, B)))
                            project_v(b + 1, 1 - u)
                    if on(b - 2):
                        pe.wait_ge(s["oe"].sem, s["oe"].at(b - 1))
                        pe.wait_ge(s["qe"].sem, s["qe"].at(least(b + 2, B)))
                        products(pb[7][0:S, dst_out], [c_oT[:, m, :] for m in range(KT)],
                                 [w_out[:, m, :] for m in range(KT)]).then_inc(s["wd"].sem, 1)
                batches(pe, body, 3, 2)

            def c_qk_(b, u, half):
                products(pb[0][0:S, :], [c_xnT[u][:, k, :] for k in range(KT)],
                         [wqk1[:, k, :] for k in range(KT)]).then_inc(Cs["qk"].sem, 1)

            def c_v_(b, u):
                products(pb[1][0:S, 0:D], [c_xnT[u][:, k, :] for k in range(KT)],
                         [wv1[:, k, :] for k in range(KT)]).then_inc(Cs["v"].sem, 1)

            def columns_of(s):
                def f(b, u):
                    pe.wait_ge(s["qkn"].sem, s["qkn"].at(b + 1))
                    pe.wait_ge(s["qe"].sem, s["qe"].at(b))
                    transposes(c_qk, S, 4, pb[7]).then_inc(s["t7"].sem, 1)
                return f

            pe.wait_ge(Bs["xu"].sem, Bs["xu"].at(B))
            pe.wait_ge(ld["c1"].sem, 64)
            pe.wait_ge(pre["masks"].sem, 1)
            attention(Cs, masks_b[:, 0, :], c_qk_, c_v_, Cs["qkn"], columns_of(Cs), wo1, slice(0, DO), 3)

            def phase_g(b, u, half):
                pe.wait_ge(G["xf"].sem, G["xf"].at(b + 1))
                pe.wait_ge(G["xte"].sem, G["xte"].at(b - 1))
                transposes(g_xf[u], S, KT, pb[u]).then_inc(G["xt"].sem, 1)

            pe.wait_ge(Cs["xu"].sem, Cs["xu"].at(B))
            pe.wait_ge(ld["gate"].sem, 16)
            batches(pe, phase_g, 0, 0)
            for i in range(B // QUAD):
                pe.wait_ge(G["xte"].sem, G["xte"].at(QUAD * (i + 1)))
                if i > 1:
                    pe.wait_ge(G["ls"].sem, G["ls"].at(i - 1))
                products(pb[2 + i % 2][0:4, 0:QN], [gate[:, k, :] for k in range(KT)],
                         [m_xfT[:, k, i * QN:(i + 1) * QN] for k in range(KT)]).then_inc(G["lt"].sem, 1)
            pe.wait_ge(G["ls"].sem, G["ls"].at(B // QUAD))
            for b in range(B):
                last = T3.transpose(pb[4][0:S, 4 * b:4 * b + 4], g_lt[:, b * S:(b + 1) * S], ident[0:4, 0:4])
            last.then_inc(G["lg"].sem, 1)

            def phase_m(i, first):
                use = [0]

                def up(w, m, src, kn, ready):
                    n = use[0]
                    use[0] += 1
                    for sem, v in ready:
                        pe.wait_ge(sem.sem, sem.at(v))
                    if not first or n >= 4:
                        pe.wait_ge(M["ev"].sem, M["ev"].at(UPS * i + (n - 3 if n >= 4 else (-1, 0, -3, -2)[n])))
                    products(pb[n % 4][:, 0:QN], [w[:, k, m * P:(m + 1) * P] for k in range(kn)],
                             [src(k) for k in range(kn)]).then_inc(M["up"].sem, 1)

                def xf(k):
                    return m_xfT[:, k, bass.ds(i * QN, QN)]

                def down(w, hsrc, e, ready):
                    for sem, v in ready:
                        pe.wait_ge(sem.sem, sem.at(v))
                    for j in range(QUAD):
                        n = e * QUAD + j
                        if not first or n >= 4:
                            pe.wait_ge(M["acc"].sem, M["acc"].at(16 * i + n - 3))
                        products(pb[4 + j][0:S, 0:DO], [hsrc[:, k, j * S:(j + 1) * S] for k in range(FT)],
                                 [w[:, k, :] for k in range(FT)]).then_inc(M["dn"].sem, 1)

                for m in range(FT):
                    up(up0, m, xf, KT, [])
                for m in range(FT):
                    up(l1, m, xf, KT, [])
                for m in range(FT):
                    up(g1, m, xf, KT, [])
                    up(u1, m, xf, KT, [])
                for m in range(FT):
                    up(l2, m, lambda k: m_ha[:, k, :], FT, [(M["ev"], UPS * i + 8)])
                down(dn0, m_h0, 0, [(M["ev"], UPS * i + 4)])
                for m in range(KT):
                    up(d3, m, xf, KT, [])
                for m in range(FT):
                    up(l3, m, lambda k: m_hb[:, k, :], FT, [(M["ev"], UPS * i + 20)])
                for m in range(FT):
                    up(up3, m, lambda k: m_hc[:, k, :], KT, [(M["ev"], UPS * i + 22)])
                down(dn1, m_h1, 1, [(M["h1"], 4 * i + 4)])
                down(dn2, m_ha, 2, [(M["ev"], UPS * i + 26)])
                down(dn3, m_hd, 3, [(M["ev"], UPS * i + 30)])

            for sem, n in (("e0", 2), ("e1", 3), ("e2", 4), ("e3", 3)):
                pe.wait_ge(ld[sem].sem, ld[sem].at(16 * n))
            pe.wait_ge(G["le"].sem, G["le"].at(1))
            phase_m(0, True)
            with pe.Fori(1, B // QUAD) as i:
                phase_m(i, False)

            def d_qk_(b, u, half):
                products(pb[0][:, 0:S], [wdd[:, k, :] for k in range(KT)],
                         [c_xnT[u][:, k, :] for k in range(KT)]).then_inc(Ds["c"].sem, 1)

            def d_v_(b, u):
                products(pb[1][0:S, 0:D], [c_cT[u]], [wuv[:, :]]).then_inc(Ds["v"].sem, 1)

            def d_columns(b, u):
                pe.wait_ge(Ds["ce"].sem, Ds["ce"].at(b + 1))
                pe.wait_ge(Ds["qe"].sem, Ds["qe"].at(b))
                for n in range(4):
                    last = T3.matmul(pb[7][:, n * S:(n + 1) * S], wuqk[:, n // 2, (n % 2) * P:(n % 2 + 1) * P],
                                     c_cT[u],
                                     start=True, stop=True)
                last.then_inc(Ds["t7"].sem, 1)

            pe.wait_ge(M["acc"].sem, M["acc"].at(64))
            pe.wait_ge(ld["d4"].sem, 96)
            attention(Ds, masks_b[:, 0, :], d_qk_, d_v_, Ds["ce"], d_columns, wo4, slice(0, D))

            def e_qk_(b, u, half):
                pe.wait_ge(Es[f"k{u}"].sem, Es[f"k{u}"].at(16 * (half + 1)))
                products(pb[0][0:S, 0:D], [c_xnT[u][:, k, :] for k in range(KT)], [wq5[:, k, :] for k in range(KT)])
                products(pb[0][0:S, D:2 * D], [e_ctx[u][:, k, :] for k in range(KT)],
                         [wk5[:, k, :] for k in range(KT)]).then_inc(Es["qk"].sem, 1)

            def e_v_(b, u):
                products(pb[1][0:S, 0:D], [e_ctx[u][:, k, :] for k in range(KT)],
                         [wv5[:, k, :] for k in range(KT)]).then_inc(Es["v"].sem, 1)

            pe.wait_ge(Ds["xu"].sem, Ds["xu"].at(B))
            pe.wait_ge(ld["e5"].sem, 64)
            attention(Es, masks_b[:, 1, :], e_qk_, e_v_, Es["z"], columns_of(Es), wo5, slice(0, D))

            def phase_f(b, u, half):
                if on(b):
                    pe.wait_ge(Fs["cl"].sem, Fs["cl"].at(b + 1))
                    pe.wait_ge(Fs["xte"].sem, Fs["xte"].at(b - 1))
                    transposes(f_q[u], S, KT, pb[u]).then_inc(Fs["xt"].sem, 1)
                if on(b - 1):
                    pe.wait_ge(Fs["xte"].sem, Fs["xte"].at(b))
                    pe.wait_ge(Fs["xu"].sem, Fs["xu"].at(b - 2))
                    products(pb[2 + (1 - u)][0:S, 0:D], [f_xT[1 - u][:, k, :] for k in range(KT)],
                             [tern[:, k, :] for k in range(KT)]).then_inc(Fs["mm"].sem, 1)

            pe.wait_ge(Es["xu"].sem, Es["xu"].at(B))
            pe.wait_ge(pre["tern"].sem, 4)
            batches(pe, phase_f, 1)

        @block.gpsimd
        def _(pool):
            g_ = nc.gpsimd
            for i, v in enumerate((-0.5, 1e-5, RMS_EPS, 1.0 / HD, 1.0 / D)):
                g_.memset(kcol[:, i, :], v).then_inc(pre["scale"].sem, 1)
            for u in range(2):
                last = g_.memset(b_cv[u][:, :, :, HD:HD + 1], 1.0)
            last.then_inc(pre["pad"].sem, 1)
            pool.wait_ge(pre["scale"].sem, 5)

            def even_out(u):
                return g_.tensor_copy(b_cp[u][:, :, SC:SCP], kcol[0:STACK, 0, 0:H].unsqueeze(2))

            even_out(0).then_inc(pre["pad"].sem, 1)
            g_.memset(wuqk[:, :, :], 0.0).then_inc(pre["pad"].sem, 1)
            pool.wait_ge(pre["pad"].sem, 3)
            g_.memset(wuv[:, :], 0.0).then_inc(pre["pad"].sem, 1)

            def stacked_context(b, u):
                for c in range(4):
                    src = parts_scratch[c % 2, bass.ds(b, 1)].rearrange("o (h r) s -> (o r) h s", r=HD)
                    g_.dma_start(b_cp[u][HD * c:HD * c + HD, :, 0:SC], src).then_inc(Bs[f"cp{u}"].sem, 16)
                src = mask_scratch[bass.ds(b, 1)].unsqueeze(1).to_broadcast([1, H, SC])
                g_.dma_start(b_cp[u][4 * HD:STACK, :, 0:SC], src).then_inc(Bs[f"cp{u}"].sem, 16)

            def phase_a(b, u, half):
                if on(b + 1):
                    ln_rstd(A, b + 1, 2)
                    pool.wait_ge(A["xn"].sem, A["xn"].at(b + 2))
                    pool.wait_ge(ld["bo"].sem, 16)
                    g_.tensor_tensor(xb_(b + 1), xb_(b + 1), bo0, ALU.add).then_inc(A["xb"].sem, 1)
                if isinstance(b, int) and b == 2:
                    pool.wait_ge(pre["parts"].sem, 32)
                    stacked_context(0, 0)
                if on(b - 1):
                    pool.wait_ge(pre["hi"].sem, b)
                    g_.tensor_tensor(s_low, s_raw[1 - u], s_high, ALU.subtract).then_inc(pre["lo"].sem, 1)

            batches(pool, phase_a, 1)

            def phase_b(b, u, half):
                if on(b + 1) and not (isinstance(b, int) and b < 0):
                    if isinstance(b, int) and b == 0:
                        pool.wait_ge(A["wd"].sem, B)
                        even_out(1)
                    pool.wait_ge(pre["parts"].sem, 32 * (b + 2))
                    pool.wait_ge(Bs["sg"].sem, Bs["sg"].at(8 * b))
                    stacked_context(b + 1, 1 - u)
                if on(b + 1):
                    ln_rstd(Bs, b + 1, 2)
                    pool.wait_ge(Bs["qh"].sem, Bs["qh"].at(b + 2))
                    g_.tensor_tensor(parts_of(b_xs, 2), twice(b_x), parts_of(b_xs, 0), ALU.subtract).then_inc(Bs["ql"].sem, 1)

            pool.wait_ge(A["nm"].sem, 3 * B)
            g_.memset(b_xs[:, :, 4 * HD:STACK], 1.0).then_inc(pre["bx"].sem, 1)
            batches(pool, phase_b, 1)

            def keys(s, b, v, kbm):
                pool.wait_ge(s["qe"].sem, s["qe"].at(b + 1))
                for k in range(KT):
                    g_.tensor_tensor(c_kbd[v][:, k, :, :], c_kT[:, k, :].unsqueeze(1).to_broadcast([P, 8, S]),
                                     kbm.unsqueeze(2).to_broadcast([P, 8, S]), ALU.mult).then_inc(s["kb"].sem, 1)

            def phase_c(b, u, half):
                if on(b + 3):
                    n = b + 3
                    ln_rstd(Cs, n, 6)
                    pool.wait_ge(Cs["pc"].sem, Cs["pc"].at(6 * n + 2))
                    g_.tensor_tensor(rstd[:, 2:3], rstd[:, 1:2], rstd[:, 1:2], ALU.mult).then_inc(Cs["pc"].sem, 1)
                    pool.wait_ge(Cs["pc"].sem, Cs["pc"].at(6 * n + 3))
                    g_.tensor_tensor(rstd[:, 3:4], rstd[:, 2:3], mv[:, 1:2], ALU.mult).then_inc(Cs["pc"].sem, 1)
                    pool.wait_ge(Cs["pc"].sem, Cs["pc"].at(6 * n + 4))
                    g_.tensor_tensor(rstd[:, 4:5], rstd[:, 3:4], kcol[:, 2, 0:1], ALU.add).then_inc(Cs["pc"].sem, 1)
                    pool.wait_ge(Cs["pc"].sem, Cs["pc"].at(6 * n + 5))
                    g_.tensor_tensor(rstd[:, 5:6], rstd[:, 4:5], kcol[:, 0, 0:1], ALU.pow).then_inc(Cs["pc"].sem, 1)
                if on(b + 1):
                    keys(Cs, b + 1, 1 - u, knbm)
                if on(b + 2):
                    n = b + 2
                    pool.wait_ge(Cs["ss"].sem, Cs["ss"].at(n + 1))
                    pool.wait_ge(Cs["qkn"].sem, Cs["qkn"].at(n))
                    g_.tensor_tensor(c_r, c_ss, kcol[:, 2, :], ALU.add).then_inc(Cs["rc"].sem, 1)
                    pool.wait_ge(Cs["rc"].sem, Cs["rc"].at(n + 1))
                    g_.tensor_tensor(c_r, c_r, kcol[:, 0, :], ALU.pow).then_inc(Cs["r"].sem, 1)

            pool.wait_ge(Bs["xu"].sem, Bs["xu"].at(B))
            g_.memset(c_v[0][:, :, HD:HD + 1], 1.0)
            g_.memset(c_v[1][:, :, HD:HD + 1], 1.0).then_inc(pre["cv"].sem, 1)
            pool.wait_ge(pre["cv"].sem, 1)
            pool.wait_ge(pre["kn"].sem, 1)
            batches(pool, phase_c, 3)

            pool.wait_ge(G["sq"].sem, G["sq"].at(B))
            sums, factors = rms[:, 0:B], rms[:, B:2 * B]
            g_.tensor_tensor(sums, sums, kcol[:, 4, 0:B], ALU.mult).then_inc(G["pc"].sem, 1)
            pool.wait_ge(G["pc"].sem, G["pc"].at(1))
            g_.tensor_tensor(sums, sums, kcol[:, 2, 0:B], ALU.add).then_inc(G["pc"].sem, 1)
            pool.wait_ge(G["pc"].sem, G["pc"].at(2))
            g_.tensor_tensor(factors, sums, kcol[:, 0, 0:B], ALU.pow).then_inc(G["pc"].sem, 1)

            def phase_g(b, u, half):
                g_.tensor_tensor(xb_(b), xb_(b), yb_(b), ALU.add).then_inc(G["xy"].sem, 1)

            pool.wait_ge(Cs["xu"].sem, Cs["xu"].at(B))
            batches(pool, phase_g, 0, 0)

            def normalise(s, bias):
                def body(b, u, half):
                    if bias is not None and on(b - 4):
                        n = b - 4
                        pool.wait_ge(Fs["mv"].sem, Fs["mv"].at(n + 1))
                        g_.tensor_tensor(rstd_f[:, 0:1], mv_f[:, 1:2], kcol[:, 1, 0:1], ALU.add).then_inc(Fs["pc"].sem, 1)
                        pool.wait_ge(Fs["pc"].sem, Fs["pc"].at(2 * n + 1))
                        g_.tensor_tensor(rstd_f[:, 1:2], rstd_f[:, 0:1], kcol[:, 0, 0:1], ALU.pow).then_inc(Fs["pc"].sem, 1)
                    if bias is not None and on(b - 5):
                        pool.wait_ge(Fs["xn"].sem, Fs["xn"].at(b - 4))
                        pool.wait_ge(ld["f6"].sem, 32)
                        g_.tensor_tensor(xb_(b - 5), xb_(b - 5), b6[:, :], ALU.add).then_inc(Fs["xb"].sem, 1)
                    if on(b + 3):
                        n = b + 3
                        ln_rstd(s, n, 2)
                        if bias is not None:
                            pool.wait_ge(s["xn"].sem, s["xn"].at(n + 1))
                            pool.wait_ge(ld["b5"].sem, 64)
                            g_.tensor_tensor(xb_(n), xb_(n), bias, ALU.add).then_inc(s["xb"].sem, 1)
                    if on(b + 1):
                        keys(s, b + 1, 1 - u, cst[:, C_BM:C_BM + 8])
                    if bias is not None and on(b + 2):
                        n = b + 2
                        pool.wait_ge(s["rope"].sem, s["rope"].at(n + 1))
                        pool.wait_ge(s["t7"].sem, s["t7"].at(n))
                        g_.tensor_tensor(c_qk, c_sq, c_t2, ALU.add).then_inc(s["qkn"].sem, 1)
                return body

            pool.wait_ge(M["acc"].sem, M["acc"].at(64))
            g_.memset(c_v[0][:, :, HD:HD + 1], 1.0)
            g_.memset(c_v[1][:, :, HD:HD + 1], 1.0).then_inc(pre["cv"].sem, 1)
            pool.wait_ge(pre["cv"].sem, 2)
            batches(pool, normalise(Ds, None), 3)
            pool.wait_ge(Ds["xu"].sem, Ds["xu"].at(B))
            pool.wait_ge(ld["b5"].sem, 64)
            batches(pool, normalise(Es, b5[:, 3, :]), 3, 5, 2)

        @block.scalar
        def _(act):
            a_ = nc.scalar

            def phase_a(b, u, half):
                if on(b):
                    for g in range(4):
                        act.wait_ge(A["pj"].sem, A["pj"].at(6 * b + g + 1))
                        act.wait_ge(A["ph"].sem, A["ph"].at(4 * b + g - 1))
                        a_.activation(a_e[:, g % 2, :], a_z[:, g % 2, :], ACT.Exp, bias=minus_one[:, :]).then_inc(A["ex"].sem, 1)
                if on(b - 1):
                    for g in range(2):
                        act.wait_ge(A["ot"].sem, A["ot"].at(2 * (b - 1) + g + 1))
                        a_.activation(a_oT[:, g * 4 * S:(g + 1) * 4 * S], pb[2 + g][:, 0:4 * S], ACT.Copy).then_inc(A["oe"].sem, 1)
                if on(b + 1):
                    act.wait_ge(A["xt"].sem, A["xt"].at(b + 2))
                    a_.activation(a_xnT.rearrange("p k s -> p (k s)"), pb[7][:, 0:KT * S], ACT.Copy).then_inc(A["xte"].sem, 1)

            act.wait_ge(pre["m1"].sem, 2)
            batches(act, phase_a, 1)

            def phase_b(b, u, half):
                for p in range(8):
                    bt, pt = (b, p - 2) if p > 1 else (b - 1, 6 + p)
                    if on(bt):
                        h = 2 * pt + 1
                        act.wait_ge(Bs["tp"].sem, Bs["tp"].at(16 * bt + h + 1))
                        a_.activation(b_pT[:, h % 4, :], pb[5][0:KC, 0:NKC * S], ACT.Copy).then_inc(Bs["tea"].sem, 1)
                    if on(b):
                        for e in range(2):
                            h = 2 * p + e
                            act.wait_ge(Bs["nb"].sem, Bs["nb"].at(8 * b + p + 1))
                            act.wait_ge(Bs["tp"].sem, Bs["tp"].at(16 * b + 2 * p - 6))
                            a_.activation(b_p[:, p % 4, e, :], pb[2 * (p % 2) + e][0:S, 0:SC], ACT.Exp,
                                          bias=b_nb[:, h:h + 1]).then_inc(Bs["ex"].sem, 1)
                    if p < 2 and on(b):
                        stack(b, p + 2, u)
                    if p > 5 and on(b + 1):
                        stack(b + 1, p - 6, 1 - u)
                    if p == 2 and on(b - 1):
                        act.wait_ge(Bs["pv"].sem, Bs["pv"].at(8 * b))
                        a_.activation(b_u, pb[6][:, 0:4 * S], ACT.Copy).then_inc(Bs["ue"].sem, 1)
                    if p == 4 and on(b - 1):
                        act.wait_ge(Bs["ot"].sem, Bs["ot"].at(b))
                        a_.activation(b_oT, pb[7][:, 0:KT * S], ACT.Copy).then_inc(Bs["oe"].sem, 1)

            def stack(b, g, u):
                act.wait_ge(Bs["xq"].sem, Bs["xq"].at(4 * b + g + 1))
                a_.activation(b_qs[u][:, g * 4 * S:(g + 1) * 4 * S], pb[7][0:STACK, 0:4 * S], ACT.Copy,
                              scale=D ** -0.5).then_inc(Bs["qs"].sem, 1)

            act.wait_ge(A["xu"].sem, A["xu"].at(B))
            batches(act, phase_b, 1)

            def attention(s, head, columns, xt_scale, tail=None, col_g=2):
                def body(b, u, half):
                    for g in range(4):
                        if g % 2 and on(b - 1):
                            act.wait_ge(s["tp"].sem, s["tp"].at(4 * b + g - 3))
                            a_.activation(c_pT[:, g * 4 * S:(g + 1) * 4 * S], pb[5][0:S, 0:4 * S],
                                          ACT.Copy).then_inc(s["tea"].sem, 1)
                        if on(b):
                            act.wait_ge(s["nb"].sem, s["nb"].at(4 * b + g + 1))
                            act.wait_ge(s["tp"].sem, s["tp"].at(4 * b + g - 3))
                            for j in range(4):
                                h = 4 * g + j
                                last = a_.activation(c_p[:, h * S:(h + 1) * S], pb[2 + g % 2][0:S, j * S:(j + 1) * S], ACT.Exp,
                                                     bias=c_nb[:, h:h + 1])
                            last.then_inc(s["ex"].sem, 1)
                        if g == 1 and on(b + 2):
                            act.wait_ge(s["xt"].sem, s["xt"].at(b + 3))
                            act.wait_ge(s["v"].sem, s["v"].at(b + 1))
                            for k in range(KT):
                                f = xt_scale[:, k:k + 1] if xt_scale is not None else 1.0
                                last = a_.activation(c_xnT[u][:, k, :], pb[1][:, k * S:(k + 1) * S], ACT.Copy, scale=f)
                            last.then_inc(s["xte"].sem, 1)
                        if g == 1 and on(b - 2):
                            act.wait_ge(s["ot"].sem, s["ot"].at(b - 1))
                            act.wait_ge(s["wd"].sem, s["wd"].at(b - 2))
                            a_.activation(c_oT.rearrange("p k s -> p (k s)"), pb[7][:, 0:KT * S],
                                          ACT.Copy).then_inc(s["oe"].sem, 1)
                        if g == col_g and on(b + 1):
                            act.wait_ge(s["t7"].sem, s["t7"].at(b + 2))
                            act.wait_ge(s["kb"].sem, s["kb"].at(2 * b + 2))
                            a_.activation(c_qT[1 - u].rearrange("p k s -> p (k s)"), pb[7][:, 0:KT * S], ACT.Copy,
                                          scale=columns)
                            a_.activation(c_kT.rearrange("p k s -> p (k s)"), pb[7][:, KT * S:2 * KT * S],
                                          ACT.Copy).then_inc(s["qe"].sem, 1)
                    if on(b + 2) and head is not None:
                        head(b + 2, u)
                    if on(b - 1):
                        act.wait_ge(s["pv"].sem, s["pv"].at(b))
                        act.wait_ge(s["ut"].sem, s["ut"].at(b - 1))
                        a_.activation(c_u, pb[6][:, 0:4 * S], ACT.Copy).then_inc(s["ue"].sem, 1)
                    if tail is not None and on(b - 3):
                        tail(b - 3)
                batches(act, body, 3, 3)

            def c_square(b, u):
                act.wait_ge(Cs["qk"].sem, Cs["qk"].at(b + 1))
                act.wait_ge(Cs["ss"].sem, Cs["ss"].at(b))
                a_.activation(c_sq, pb[0][0:S, :], ACT.Square, scale=HD ** -0.5).then_inc(Cs["sq"].sem, 1)

            act.wait_ge(Bs["xu"].sem, Bs["xu"].at(B))
            act.wait_ge(ld["c2"].sem, ld["c2"].at(16 * 17))
            act.wait_ge(pre["kn"].sem, 1)
            
            def c_rms(b):
                act.wait_ge(Cs["xu"].sem, Cs["xu"].at(b + 1))
                act.wait_ge(G["sq"].sem, G["sq"].at(b))
                a_.activation(c_junk, yb_(b), ACT.Square, accum_out=rms[:, bass.ds(b, 1)]).then_inc(G["sq"].sem, 1)

            attention(Cs, c_square, qn4, n12[:, 0:2], c_rms, 3)

            def phase_g(b, u, half):
                act.wait_ge(G["xt"].sem, G["xt"].at(b + 1))
                for k in range(KT):
                    last = a_.activation(m_xfT[:, k, bass.ds(b * S, S)], pb[u][:, k * S:(k + 1) * S], ACT.Copy,
                                         scale=n12[:, 2 + k:3 + k])
                last.then_inc(G["xte"].sem, 1)

            act.wait_ge(Cs["xu"].sem, Cs["xu"].at(B))
            batches(act, phase_g, 0, 0)
            for i in range(B // QUAD):
                act.wait_ge(G["lt"].sem, G["lt"].at(i + 1))
                a_.activation(g_lt[:, i * QN:(i + 1) * QN], pb[2 + i % 2][0:4, 0:QN], ACT.Copy).then_inc(G["ls"].sem, 1)
            act.wait_ge(G["lg"].sem, G["lg"].at(1))
            a_.activation(g_lg, pb[4][0:S, 0:4 * B], ACT.Copy).then_inc(G["le"].sem, 1)
            act.wait_ge(G["wt"].sem, G["wt"].at(1))
            a_.activation(g_b2, g_a, ACT.Exp).then_inc(G["wt"].sem, 1)

            def phase_m(i):
                plan = ([("gelu", m_h0, m) for m in range(4)] + [("gelu", m_ha, m) for m in range(4)]
                        + [x for m in range(4) for x in (("gate", None, m), ("up", None, m))]
                        + [("gelu", m_hb, m) for m in range(4)] + [("gelu", m_hc, m) for m in range(2)]
                        + [("gelu", m_ha, m) for m in range(4)] + [("gelu", m_hd, m) for m in range(4)])
                for n, (what, dst, m) in enumerate(plan):
                    src = pb[n % 4][:, 0:QN]
                    act.wait_ge(M["up"].sem, M["up"].at(UPS * i + n + 1))
                    if what == "gelu":
                        a_.activation(dst[:, m, :], src, ACT.Gelu).then_inc(M["ev"].sem, 1)
                    elif what == "gate":
                        act.wait_ge(M["h1"].sem, M["h1"].at(4 * i + m - 1))
                        a_.activation(m_s[:, m % 2, :], src, ACT.Tanh, scale=0.5)
                        a_.activation(m_g[:, m % 2, :], src, ACT.Copy).then_inc(M["ev"].sem, 1)
                    else:
                        a_.activation(m_u[:, m % 2, :], src, ACT.Copy).then_inc(M["ev"].sem, 1)

            phase_m(0)
            with act.Fori(1, B // QUAD) as i:
                phase_m(i)

            def d_latent(b, u):
                act.wait_ge(Ds["c"].sem, Ds["c"].at(b + 1))
                act.wait_ge(Ds["v"].sem, Ds["v"].at(b - 1))
                a_.activation(c_cT[u], pb[0][:, 0:S], ACT.Copy).then_inc(Ds["ce"].sem, 1)

            act.wait_ge(M["acc"].sem, M["acc"].at(64))
            attention(Ds, d_latent, HD ** -0.5, None)
            act.wait_ge(Ds["xu"].sem, Ds["xu"].at(B))
            attention(Es, None, HD ** -0.5, None)

            def phase_f(b, u, half):
                act.wait_ge(Fs["xt"].sem, Fs["xt"].at(b + 1))
                act.wait_ge(Fs["mm"].sem, Fs["mm"].at(b - 1))
                a_.activation(f_xT[u].rearrange("p k s -> p (k s)"), pb[u][:, 0:KT * S], ACT.Identity,
                              bias=minus_round[:, :]).then_inc(Fs["xte"].sem, 1)

            act.wait_ge(Es["xu"].sem, Es["xu"].at(B))
            batches(act, phase_f, 0, 0)

        @block.vector
        def _(dve):
            v_ = nc.vector

            v_.memset(minus_one[:, :], -1.0).then_inc(pre["m1"].sem, 1)
            v_.memset(minus_round[:, :], -ROUND).then_inc(pre["m1"].sem, 1)
            v_.memset(a_v[:, :, LD:LD + 1], 1.0).then_inc(pre["av"].sem, 1)
            dve.wait_ge(ld["x0"].sem, 16)

            def stats_of(s, b, per, at):
                ln_stats(s, b)
                dve.wait_ge(s["chain"].sem, s["chain"].at(per * b + at + 1))
                v_.memset(rstd[:, 7:8], 0.0)
                v_.bn_aggr(mv[:, :], stats[:, :]).then_inc(s["mv"].sem, 1)

            def phase_a(b, u, half):
                def masked(g):
                    tri = cst[0:S, C_TRI:C_TRI + S].unsqueeze(1).to_broadcast([S, 4, S])
                    dve.wait_ge(A["sg"].sem, A["sg"].at(4 * b + g + 1))
                    v_.tensor_tensor(a_at.rearrange("k (x j e s) -> k x e j s", x=2, j=4, e=2)[:, g // 2, g % 2],
                                     pb[2 + g % 2][0:S, 0:4 * S].rearrange("p (j s) -> p j s", j=4), tri,
                                     ALU.mult).then_inc(A["sm"].sem, 1)

                if isinstance(b, int) and b == 1:
                    dve.wait_ge(ld["x"].sem, 16)
                if on(b + 1):
                    stats_of(A, b + 1, 1, 0)
                if isinstance(b, int) and b == -1:
                    ln_apply(A, 0, a_xn, 2, None).then_inc(A["xn"].sem, 1)
                    dve.wait_ge(ld["bias"].sem, 32)
                    v_.tensor_scalar(bqk0[:, :], bqk0[:, :], 1.0, None, ALU.add).then_inc(pre["bias1"].sem, 1)
                    dve.wait_ge(pre["bias1"].sem, 1)
                    dve.wait_ge(pre["av"].sem, 1)
                    dve.wait_ge(ld["a2"].sem, 32)
                if on(b):
                    def z_of(g):
                        dve.wait_ge(A["pg"].sem, A["pg"].at(6 * b + g + 1))
                        dve.wait_ge(A["ph"].sem, A["ph"].at(4 * b + g - 1))
                        bias = bqk0[:, 4 * g:4 * g + 4].unsqueeze(2).to_broadcast([P, 4, S])
                        v_.tensor_tensor(a_z[:, g % 2, :].rearrange("p (m s) -> p m s", m=4),
                                         pb[g % 2][:, 0:4 * S].rearrange("p (m s) -> p m s", m=4), bias,
                                         ALU.add).then_inc(A["pj"].sem, 1)

                    def phi_of(g):
                        dve.wait_ge(A["ex"].sem, A["ex"].at(4 * b + g + 1))
                        dst = (a_q if g < 2 else a_k)[:, (g % 2) * 4 * S:(g % 2 + 1) * 4 * S]
                        v_.scalar_tensor_tensor(dst, a_e[:, g % 2, :], 1.0, a_z[:, g % 2, :], ALU.min,
                                                ALU.max).then_inc(A["ph"].sem, 1)

                    def v_of(g):
                        dve.wait_ge(A["pg"].sem, A["pg"].at(6 * b + 5 + g))
                        v_.tensor_tensor(a_v[:, 8 * g:8 * g + 8, 0:LD],
                                         pb[g][0:S, :].rearrange("s (h e) -> s h e", h=8),
                                         bv0[:, g * 512:(g + 1) * 512].rearrange("s (h e) -> s h e", h=8),
                                         ALU.add).then_inc(A["pj"].sem, 1)

                    if isinstance(b, int) and b == 0:
                        dve.wait_ge(ld["cst"].sem, 16)
                    for g in range(4):
                        z_of(g)
                        if g:
                            phi_of(g - 1)
                    v_of(0)
                    phi_of(3)
                    v_of(1)
                    if on(b + 1):
                        ln_apply(A, b + 1, a_xn, 2, (A["xt"], b + 1)).then_inc(A["xn"].sem, 1)
                    masked(0)
                    masked(1)
                if isinstance(b, int) and b == 0:
                    v_.tensor_copy(ident_b[:, :], cst[0:S, C_ID:C_ID + S])
                    for i, c in enumerate((C_CAUSAL, C_BAND)):
                        last = v_.tensor_copy(masks_b[:, i, :].rearrange("q (j s) -> q j s", j=4),
                                              cst[0:S, c:c + S].unsqueeze(1).to_broadcast([S, 4, S]))
                    last.then_inc(pre["masks"].sem, 1)
                if isinstance(b, int) and b == 0:
                    dve.wait_ge(ld["mask"].sem, 16)
                    v_.tensor_scalar(mask_f[:, :], mask_i[:, :], 0, -1e20, ALU.is_equal, ALU.mult).then_inc(pre["rowbias"].sem, 1)
                if isinstance(b, int) and b == B:
                    stats_of(Bs, 0, 1, 0)
                if on(b - 1):
                    dve.wait_ge(A["wd"].sem, A["wd"].at(b))
                    dve.wait_ge(A["xb"].sem, A["xb"].at(b))
                    v_.tensor_tensor(xb_(b - 1), xb_(b - 1), pb[7][0:S, 0:D], ALU.add).then_inc(A["xu"].sem, 1)
                if on(b):
                    masked(2)
                    masked(3)
                if on(b - 1):
                    v = 1 - u
                    dve.wait_ge(pre[f"raw{v}"].sem, 16 * half if v else 16 * (half + 1))
                    dve.wait_ge(pre["parts"].sem, max(32 * (b - 1), 0) if isinstance(b, int) else 32 * (b - 1))
                    v_.tensor_scalar(s_high.bitcast(I32), s_raw[v].bitcast(I32), HIGH, None,
                                     ALU.bitwise_and).then_inc(pre["hi"].sem, 1)
                if on(b):
                    dve.wait_ge(A["nd"].sem, A["nd"].at(3 * b + 3))
                    for n, (lo, hi) in enumerate(NUM):
                        num = pb[4 + n][0:S, 0:(hi - lo) * (LD + 1)].rearrange("s (h e) -> s h e", e=LD + 1)
                        last = v_.tensor_scalar(a_den[:, lo:hi].unsqueeze(2), num[:, :, LD:LD + 1], 1e-6, None, ALU.add)
                    last.then_inc(A["den"].sem, 1)
                    dve.wait_ge(A["den"].sem, A["den"].at(2 * b + 1))
                    v_.reciprocal(a_den[:, 16:32], a_den[:, 0:16]).then_inc(A["den"].sem, 1)
                    dve.wait_ge(A["den"].sem, A["den"].at(2 * b + 2))
                    for n, (lo, hi) in enumerate(NUM):
                        num = pb[4 + n][0:S, 0:(hi - lo) * (LD + 1)].rearrange("s (h e) -> s h e", e=LD + 1)
                        v_.tensor_tensor(a_o[:, lo * LD:hi * LD].rearrange("s (h e) -> s h e", e=LD), num[:, :, 0:LD],
                                         a_den[:, 16 + lo:16 + hi].unsqueeze(2).to_broadcast([S, hi - lo, LD]),
                                         ALU.mult).then_inc(A["nm"].sem, 1)

            batches(dve, phase_a, 1)

            def phase_b(b, u, half):
                for p in range(8):
                    if p == 0 and on(b + 1) and not (isinstance(b, int) and b < 0):
                        stats_of(Bs, b + 1, 1, 0)
                    if on(b):
                        dve.wait_ge(Bs["sg"].sem, Bs["sg"].at(8 * b + p + 1))
                        pair = banks[0:S, 2 * (p % 2):2 * (p % 2) + 2, 0:SC]
                        v_.tensor_reduce(b_nb[:, 2 * p:2 * p + 2], pair, AX_X, ALU.max, negate=True).then_inc(Bs["nb"].sem, 1)
                    bt, pt = (b, p - 2) if p > 1 else (b - 1, 6 + p)
                    if on(bt):
                        h = 2 * pt
                        dve.wait_ge(Bs["tp"].sem, Bs["tp"].at(16 * bt + h + 1))
                        v_.tensor_copy(b_pT[:, h % 4, :], pb[4][0:KC, 0:NKC * S]).then_inc(Bs["ted"].sem, 1)
                    if p == 3 and on(b - 1):
                        dve.wait_ge(Bs["ut"].sem, Bs["ut"].at(b))
                        normalise(Bs, b - 1, pb[7][0:S, :].rearrange("s (h e) -> s h e", e=32), b_rc, b_o)
                    if on(b + 1) and p == 2:
                        dve.wait_ge(pre["bx"].sem, 1)
                        ln_heads(b + 1)
                    if p == 5 and on(b - 1):
                        dve.wait_ge(Bs["wd"].sem, Bs["wd"].at(b))
                        v_.tensor_tensor(xb_(b - 1), xb_(b - 1), pb[7][0:S, 0:D], ALU.add).then_inc(Bs["xu"].sem, 1)

            def ln_heads(b):
                dve.wait_ge(Bs["pc"].sem, Bs["pc"].at(b * 2 + 2))
                dve.wait_ge(Bs["ql"].sem, Bs["ql"].at(b))
                v_.tensor_scalar(b_x, xb_(b), mv[:, 0:1], rstd[:, 1:2], ALU.subtract, ALU.mult).then_inc(Bs["xn"].sem, 1)
                dve.wait_ge(Bs["xn"].sem, Bs["xn"].at(b + 1))
                dve.wait_ge(Bs["xq"].sem, Bs["xq"].at(4 * b))
                v_.tensor_scalar(parts_of(b_xs.bitcast(I32), 0), twice(b_x.bitcast(I32)), HIGH, None,
                                 ALU.bitwise_and).then_inc(Bs["qh"].sem, 1)

            def normalise(s, b, acc, rc, o):
                v_.reciprocal(rc.unsqueeze(2), acc[:, :, HD:HD + 1]).then_inc(s["den"].sem, 1)
                dve.wait_ge(s["den"].sem, s["den"].at(b + 1))
                v_.tensor_tensor(o.rearrange("s (h e) -> s h e", e=HD), acc[:, :, 0:HD],
                                 rc.unsqueeze(2).to_broadcast([S, H, HD]), ALU.mult).then_inc(s["nm"].sem, 1)

            dve.wait_ge(A["xu"].sem, A["xu"].at(B))
            v_.memset(pb[6][:, 0:4 * S], 0.0).then_inc(pre["b6"].sem, 1)
            batches(dve, phase_b, 1)

            def c_ln(b):
                ln_apply(Cs, b, yb_(b), 6, None).then_inc(Cs["y"].sem, 1)
                dve.wait_ge(Cs["y"].sem, Cs["y"].at(b + 1))
                dve.wait_ge(Cs["pc"].sem, Cs["pc"].at(6 * b + 6))
                dve.wait_ge(Cs["xt"].sem, Cs["xt"].at(b))
                v_.tensor_scalar(c_h, yb_(b), rstd[:, 5:6], None, ALU.mult).then_inc(Cs["xn"].sem, 1)

            def x_ln(s):
                def f(b):
                    ln_apply(s, b, c_h, 2, (s["xt"], b)).then_inc(s["xn"].sem, 1)
                return f

            def attention(s, ln_of, v_in, before, between, residual, first=1, follow=None, col_g=2):
                def body(b, u, half):
                    for g in range(4):
                        if on(b):
                            dve.wait_ge(s["sg"].sem, s["sg"].at(4 * b + g + 1))
                            v_.tensor_reduce(c_nb[:, 4 * g:4 * g + 4],
                                             pb[2 + g % 2][0:S, 0:4 * S].rearrange("q (j s) -> q j s", j=4),
                                             AX_X, ALU.max, negate=True).then_inc(s["nb"].sem, 1)
                        if g == col_g and on(b + 1):
                            between(b + 1)
                        if g % 2 == 0 and on(b - 1):
                            dve.wait_ge(s["tp"].sem, s["tp"].at(4 * b + g - 3))
                            v_.tensor_copy(c_pT[:, g * 4 * S:(g + 1) * 4 * S], pb[4][0:S, 0:4 * S]).then_inc(s["ted"].sem, 1)
                        if g == 0 and on(b - 2):
                            dve.wait_ge(s["ut"].sem, s["ut"].at(b - 1))
                            normalise(s, b - 2, pb[7][0:S, :].rearrange("s (h e) -> s h e", e=32), c_rc, c_o)
                        if g == 1 and on(b + 3):
                            stats_of(s, b + 3, 1, 0)
                        if g == 3 and on(b + 3):
                            ln_of(b + 3)
                        if g == 1 and follow is not None:
                            follow(b - 3)
                    if on(b + 1):
                        dve.wait_ge(s["pv"].sem, s["pv"].at(b))
                        v_in(b + 1, 1 - u)
                    if on(b - 2):
                        dve.wait_ge(s["wd"].sem, s["wd"].at(b - 1))
                        residual(b - 2)
                    if on(b + 2):
                        before(b + 2)
                batches(dve, body, 3, 2, first)

            def plain_v(s):
                def f(b, u):
                    dve.wait_ge(s["v"].sem, s["v"].at(b + 1))
                    v_.tensor_copy(c_v[u][:, :, 0:HD], pb[1][0:S, 0:D].rearrange("s (h e) -> s h e", h=H)).then_inc(s["ve"].sem, 1)
                return f

            def nothing(b):
                pass

            def c_sums(b):
                dve.wait_ge(Cs["sq"].sem, Cs["sq"].at(b + 1))
                dve.wait_ge(Cs["r"].sem, Cs["r"].at(b))
                v_.tensor_reduce(c_ss, c_sq.rearrange("s (h e) -> s h e", e=HD), AX_X, ALU.add).then_inc(Cs["ss"].sem, 1)

            def c_scaled(b):
                dve.wait_ge(Cs["r"].sem, Cs["r"].at(b + 1))
                v_.tensor_tensor(c_qk.rearrange("s (h e) -> s h e", e=HD), pb[0][0:S, :].rearrange("s (h e) -> s h e", e=HD),
                                 c_r.unsqueeze(2).to_broadcast([S, 32, HD]), ALU.mult).then_inc(Cs["qkn"].sem, 1)

            def c_residual(b):
                v_.tensor_tensor(yb_(b, FREE), yb_(b, FREE), pb[7][0:S, 0:DO], ALU.add).then_inc(Cs["xu"].sem, 1)

            def x_residual(s):
                def f(b):
                    v_.tensor_tensor(xb_(b), xb_(b), pb[7][0:S, 0:D], ALU.add).then_inc(s["xu"].sem, 1)
                return f

            dve.wait_ge(Bs["xu"].sem, Bs["xu"].at(B))
            dve.wait_ge(ld["c2"].sem, ld["c2"].at(16 * 17))
            v_.tensor_scalar(qn4, qkn[:, 0:1], HD ** -0.5, None, ALU.mult)
            v_.tensor_scalar(knbm, cst[:, C_BM:C_BM + 8], qkn[:, 1:2], None, ALU.mult).then_inc(pre["kn"].sem, 1)
            attention(Cs, c_ln, plain_v(Cs), c_sums, c_scaled, c_residual, col_g=3)

            def phase_g(b, u, half):
                dve.wait_ge(G["xt"].sem, G["xt"].at(b - 1))
                v_.tensor_scalar(g_xf[u], yb_(b), rms[:, bass.ds(B + b, 1)], None, ALU.mult).then_inc(G["xf"].sem, 1)

            dve.wait_ge(G["pc"].sem, G["pc"].at(3))
            batches(dve, phase_g, 0, 0)
            dve.wait_ge(G["le"].sem, G["le"].at(1))
            steps = [0]

            def step(ins):
                steps[0] += 1
                ins.then_inc(G["chain"].sem, 1)
                dve.wait_ge(G["chain"].sem, G["chain"].at(steps[0]))

            lg3, a3, p3, w3 = (t.rearrange("s (b e) -> s b e", e=4) for t in (g_lg, g_a, g_b2, g_w))
            step(v_.tensor_scalar(g_lg, g_lg, -FLT_MAX, FLT_MAX, ALU.max, ALU.min))
            step(v_.tensor_reduce(g_red, lg3, AX_X, ALU.max))
            v_.tensor_tensor(a3, lg3, g_red.unsqueeze(2).to_broadcast([S, B, 4]), ALU.subtract).then_inc(G["wt"].sem, 1)
            dve.wait_ge(G["wt"].sem, G["wt"].at(2))
            step(v_.tensor_reduce(g_red, p3, AX_X, ALU.add))
            step(v_.reciprocal(g_red2, g_red))
            step(v_.tensor_tensor(a3, p3, g_red2.unsqueeze(2).to_broadcast([S, B, 4]), ALU.mult))
            c4, d4 = (t.rearrange("s (b e f) -> s b e f", e=4, f=4) for t in (g_cmp, g_cmp2))
            other = a3.unsqueeze(2).to_broadcast([S, B, 4, 4])
            own = a3.unsqueeze(3).to_broadcast([S, B, 4, 4])
            lt = cst[0:S, C_LT:C_LT + 16].rearrange("s (e f) -> s e f", e=4).unsqueeze(1).to_broadcast([S, B, 4, 4])
            step(v_.tensor_tensor(c4, other, own, ALU.is_equal))
            step(v_.tensor_tensor(c4, c4, lt, ALU.mult))
            step(v_.tensor_tensor(d4, other, own, ALU.is_gt))
            step(v_.tensor_tensor(g_cmp, g_cmp, g_cmp2, ALU.add))
            step(v_.tensor_reduce(g_b2, g_cmp.rearrange("s (n f) -> s n f", f=4), AX_X, ALU.add))
            step(v_.tensor_scalar(g_b2, g_b2, 2.0, None, ALU.is_lt))
            step(v_.tensor_tensor(g_w, g_b2, g_a, ALU.mult))
            step(v_.tensor_reduce(g_red, w3, AX_X, ALU.add))
            step(v_.tensor_scalar(g_red, g_red, 1e-8, None, ALU.add))
            step(v_.reciprocal(g_red2, g_red))
            step(v_.tensor_tensor(w3, w3, g_red2.unsqueeze(2).to_broadcast([S, B, 4]), ALU.mult))
            dve.wait_ge(G["xy"].sem, G["xy"].at(B))

            def phase_m(i, first):
                for m in range(FT):
                    dve.wait_ge(M["ev"].sem, M["ev"].at(UPS * i + 10 + 2 * m))
                    v_.scalar_tensor_tensor(m_t[:, m % 2, :], m_s[:, m % 2, :], 1.0, m_g[:, m % 2, :], ALU.add,
                                            ALU.mult).then_inc(M["t"].sem, 1)
                    dve.wait_ge(M["t"].sem, M["t"].at(4 * i + m + 1))
                    v_.scalar_tensor_tensor(m_h1[:, m, :], m_t[:, m % 2, :], 0.5, m_u[:, m % 2, :], ALU.mult,
                                            ALU.mult).then_inc(M["h1"].sem, 1)
                for e in range(4):
                    for j in range(QUAD):
                        n = e * QUAD + j
                        b = i * QUAD + j
                        dve.wait_ge(M["dn"].sem, M["dn"].at(16 * i + n + 1))
                        if n >= QUAD:
                            dve.wait_ge(M["acc"].sem, M["acc"].at(16 * i + n - 3))
                        v_.scalar_tensor_tensor(xb_(b, FREE), pb[4 + j][0:S, 0:DO], g_w[:, bass.ds(b * 4 + e, 1)],
                                                xb_(b, FREE), ALU.mult, ALU.add).then_inc(M["acc"].sem, 1)

            phase_m(0, True)
            with dve.Fori(1, B // QUAD) as i:
                phase_m(i, False)

            dve.wait_ge(M["acc"].sem, M["acc"].at(64))
            attention(Ds, x_ln(Ds), plain_v(Ds), nothing, nothing, x_residual(Ds))

            dve.wait_ge(ld["pk"].sem, 16)
            dve.wait_ge(ld["f6"].sem, 32)
            for q in range(4):
                dve.wait_ge(pre["tern"].sem, pre["tern"].at(q))
                v_.tensor_scalar(enc[:, :, :], packed[:, :, :], 2 * q, 3, ALU.logical_shift_right,
                                 ALU.bitwise_and).then_inc(pre["enc"].sem, 1)
                dve.wait_ge(pre["enc"].sem, pre["enc"].at(q + 1))
                v_.tensor_scalar(tern[:, :, 64 * q:64 * q + 64], enc[:, :, :], -1.0, None, ALU.add).then_inc(pre["tern"].sem, 1)

            def e_v(b, u):
                dve.wait_ge(Es["v"].sem, Es["v"].at(b + 1))
                v_.tensor_tensor(c_v[u][:, :, 0:HD], pb[1][0:S, 0:D].rearrange("s (h e) -> s h e", h=H),
                                 b5[:, 2, :].rearrange("s (h e) -> s h e", h=H), ALU.add).then_inc(Es["ve"].sem, 1)

            def e_rotary(b):
                dve.wait_ge(Es["qk"].sem, Es["qk"].at(b + 1))
                dve.wait_ge(Es["rope"].sem, Es["rope"].at(b))
                z = c_z
                v_.tensor_tensor(z, pb[0][0:S, :], b5[:, 0:2, :].rearrange("s i n -> s (i n)"), ALU.add).then_inc(Es["z"].sem, 1)
                dve.wait_ge(Es["z"].sem, Es["z"].at(b + 1))
                dve.wait_ge(Es["qkn"].sem, Es["qkn"].at(b))
                z3, c3, t3 = (t.rearrange("s (h e) -> s h e", e=HD) for t in (z, c_sq, c_t2))
                cos = cst[0:S, C_COS:C_COS + HD].unsqueeze(1).to_broadcast([S, 32, HD])
                v_.tensor_tensor(c3, z3, cos, ALU.mult)
                for lo, hi in ((0, 8), (8, 0)):
                    sin = cst[0:S, C_SIN + lo:C_SIN + lo + 8].unsqueeze(1).to_broadcast([S, 32, 8])
                    last = v_.tensor_tensor(t3[:, :, lo:lo + 8], z3[:, :, hi:hi + 8], sin, ALU.mult)
                last.then_inc(Es["rope"].sem, 1)

            dve.wait_ge(Ds["xu"].sem, Ds["xu"].at(B))
            dve.wait_ge(ld["b5"].sem, 64)

            def e_res(b):
                dve.wait_ge(Es["xb"].sem, Es["xb"].at(b + 1))
                x_residual(Es)(b)

            def f_step(b):
                if on(b):
                    f_rows(b + 1)
                    f_stats(b)

            def f_rows(b):
                if on(b - 2):
                    dve.wait_ge(Fs["pc"].sem, Fs["pc"].at(2 * (b - 1)))
                    v_.tensor_scalar(f_xn[:, bass.ds((b - 2) * D, D)], xb_(b - 2), mv_f[:, 0:1], rstd_f[:, 1:2],
                                     ALU.subtract, ALU.mult).then_inc(Fs["xn"].sem, 1)
                if on(b - 3):
                    dve.wait_ge(Fs["xn"].sem, Fs["xn"].at(b - 2))
                    v_.tensor_reduce(f_am[:, bass.ds(b - 3, 1)], f_xn[:, bass.ds((b - 3) * D, D)], AX_X, ALU.max,
                                     apply_absolute_value=True).then_inc(Fs["am"].sem, 1)

            def f_stats(b):
                dve.wait_ge(Es["xu"].sem, Es["xu"].at(b + 1))
                dve.wait_ge(Fs["xn"].sem, Fs["xn"].at(b))
                v_.memset(rstd_f[:, 2:3], 0.0)
                v_.bn_stats(stats_f[:, :], xb_(b)).then_inc(Fs["sf"].sem, 1)
                dve.wait_ge(Fs["sf"].sem, Fs["sf"].at(b + 1))
                v_.memset(rstd_f[:, 3:4], 0.0)
                v_.bn_aggr(mv_f[:, :], stats_f[:, :]).then_inc(Fs["mv"].sem, 1)

            attention(Es, x_ln(Es), e_v, e_rotary, nothing, e_res, 2, f_step)

            f_step(B - 1)
            f_rows(B + 1)
            f_rows(B + 2)
            dve.wait_ge(Fs["am"].sem, Fs["am"].at(B))
            v_.tensor_scalar(f_am[:, :], f_am[:, :], 1e-5, None, ALU.max).then_inc(Fs["sm"].sem, 1)
            dve.wait_ge(Fs["sm"].sem, Fs["sm"].at(1))
            v_.reciprocal(f_s[:, 0:B], f_am[:, :]).then_inc(Fs["sm"].sem, 1)
            v_.tensor_scalar(f_sc, f_am[:, :], wscale[:, 0:1], 1.0 / 127, ALU.mult, ALU.mult)
            dve.wait_ge(Fs["sm"].sem, Fs["sm"].at(2))
            v_.tensor_scalar(f_s[:, B:2 * B], f_s[:, 0:B], 127.0, None, ALU.mult).then_inc(Fs["sm"].sem, 1)
            dve.wait_ge(Fs["sm"].sem, Fs["sm"].at(3))

            def phase_f(b, u, half):
                if on(b + 1):
                    dve.wait_ge(Fs["xt"].sem, Fs["xt"].at(b))
                    v_.tensor_scalar(f_q[1 - u], f_xn[:, bass.ds((b + 1) * D, D)], f_s[:, bass.ds(B + b + 1, 1)], ROUND,
                                     ALU.mult, ALU.add).then_inc(Fs["sh"].sem, 1)
                if on(b):
                    dve.wait_ge(Fs["sh"].sem, Fs["sh"].at(b + 1))
                    v_.tensor_scalar(f_q[u], f_q[u], ROUND + 127.0, ROUND - 128.0, ALU.min, ALU.max).then_inc(Fs["cl"].sem, 1)
                if on(b - 2):
                    dve.wait_ge(Fs["mm"].sem, Fs["mm"].at(b - 1))
                    dve.wait_ge(Fs["xb"].sem, Fs["xb"].at(b - 1))
                    v_.scalar_tensor_tensor(xb_(b - 2), pb[2 + u][0:S, 0:D], f_sc[:, bass.ds(b - 2, 1)], xb_(b - 2),
                                            ALU.mult, ALU.add).then_inc(Fs["xu"].sem, 1)

            batches(dve, phase_f, 1, 2)


def kernel(**inputs):
    import numpy as _np
    import concourse.bacc as _bacc
    from concourse import mybir as _mybir
    from concourse.bass_utils import run_bass_kernel_spmd as _run

    def a(name):
        return _np.asarray(inputs[name])

    def cols(v):
        return v.reshape(-1, P).T

    def row(v):
        return v.reshape(-1)

    f = "L0_ffn_"
    arrays = {
        "x": a("x"), "ctx": a("ctx_1024"), "ctxT": a("ctx_1024").transpose(0, 2, 1),
        "mask": a("mask_Bx1x1xS2_ik0").reshape(B, SC), "consts": constants(),
        "Wq": a("L0_attn_Wq"), "Wk": a("L0_attn_Wk"), "Wv": a("L0_attn_Wv"), "Wo": a("L0_attn_Wo"),
        "bq": cols(a("L0_attn_bq")), "bk": cols(a("L0_attn_bk")), "bv": row(a("L0_attn_bv")), "bo": row(a("L0_attn_bo")),
        "W_out": a("L0_xattn_W_out").T,
        "n12": _np.concatenate([cols(a(f + "n1_w")), cols(a(f + "n2_w"))], 1),
        "qn": a(f + "qn_w").reshape(HD, 1), "kn": a(f + "kn_w").reshape(HD, 1),
        "wq": a(f + "wq").T, "wk": a(f + "wk").T, "wv": a(f + "wv").T, "wo": a(f + "wo").T[:, FREE:],
        "gate": a(f + "gate_w").T,
        "e0_up": a(f + "e0_up").T, "e0_down": a(f + "e0_down").T[:, FREE:],
        "w1": a(f + "e1_w1").T, "w2": a(f + "e1_w2").T, "e1_down": a(f + "e1_down").T[:, FREE:],
        "l1": a(f + "e2_l1").T, "l2": a(f + "e2_l2").T, "l3": a(f + "e2_l3").T, "l4": a(f + "e2_l4").T[:, FREE:],
        "e3_down": a(f + "e3_down").T, "e3_up": a(f + "e3_up").T, "e3_out": a(f + "e3_out").T[:, FREE:],
        "W_dq": a("L1_attn_W_dq"), "W_uq": a("L1_attn_W_uq"), "W_dkv": a("L1_attn_W_dkv"),
        "W_uk": a("L1_attn_W_uk"), "W_uv": a("L1_attn_W_uv"), "W_o": a("L1_attn_W_o"),
        "packed": a("L1_ffn_packed_weight").reshape(64, D).T, "wscale": row(a("L1_ffn_weight_scale")),
        "bias": row(a("L1_ffn_bias")),
    }
    for n in "qkvo":
        arrays[f"{n}_w"] = a(f"L1_xattn_{n}_w").T
        arrays[f"{n}_b"] = row(a(f"L1_xattn_{n}_b"))
    arrays = {n: _np.ascontiguousarray(v) for n, v in arrays.items()}
    nc = _bacc.Bacc("TRN2", target_bir_lowering=False, num_devices=1)
    tensors = {n: nc.dram_tensor(f"in_{n}", v.shape, _mybir.dt.from_np(v.dtype), kind="ExternalInput").ap()
               for n, v in arrays.items()}
    out = nc.dram_tensor("out_0", (B, S, D), _mybir.dt.float32, kind="ExternalOutput").ap()
    decoder_kernel(nc, tensors, out)
    r = _run(nc, [{f"in_{n}": v for n, v in arrays.items()}], core_ids=[0])
    return r.results[0]["out_0"]
```
